# Optimizing a Trainium2 kernel written in Bass

```python
import numpy as np
import jax
import jax.numpy as jnp

def _softmax(x, axis=-1):
    return jax.nn.softmax(x, axis=axis)

def _gelu(x):
    return jax.nn.gelu(x, approximate=True)

def _silu(x):
    return jax.nn.silu(x)

def _sigmoid(x):
    return jax.nn.sigmoid(x)

def _layernorm(x, axis=-1, eps=1e-05):
    m = jnp.mean(x, axis=axis, keepdims=True)
    v = jnp.var(x, axis=axis, keepdims=True)
    return (x - m) / jnp.sqrt(v + eps)

def _scatter_add(tgt, idx, src, axis=0):
    return tgt.at[idx].add(src)

def _segment_sum(src, seg, n):
    return jax.ops.segment_sum(src, seg, n)
kernel_name = 'mk_gnn_preln_d4_gnn_r32_a5435f'

def setup_inputs(seed: int=0):
    np.random.seed(seed)
    _w = jnp.asarray

    def _rec_inputs():
        import jax
        import jax.numpy as jnp
        _gk = jax.random.key(seed)
        x = -0.000202 + 1 * jax.random.normal(jax.random.fold_in(_gk, 1), (3125, 128), jnp.float32)
        src = jax.random.randint(jax.random.fold_in(_gk, 2), (50000,), 0, 3125, jnp.int32)
        dst = jax.random.randint(jax.random.fold_in(_gk, 3), (50000,), 0, 3125, jnp.int32)
        _o = jnp.argsort(dst, stable=True)
        src = src[_o]
        dst = dst[_o]
        edge_attr_32 = 0.000298249 + 1.00014 * jax.random.normal(jax.random.fold_in(_gk, 13), (50000, 32), jnp.float32)
        edge_type_40 = jax.random.randint(jax.random.fold_in(_gk, 15), (50000,), 0, 40, jnp.int32)
        edge_weight = jax.random.uniform(jax.random.fold_in(_gk, 16), (50000,), jnp.float32, 0.0, 1)
        return (x, src, dst, edge_attr_32, edge_type_40, edge_weight)
    x, src, dst, edge_attr_32, edge_type_40, edge_weight = _rec_inputs()

    def _L0_gnn_setup():
        import jax, jax.numpy as jnp
        import numpy as np
        N = 50000
        E = 625000
        D = 128
        H = 8
        C = D // H
        DE = 32
        NEG_SLOPE = 0.2
        LN_EPS = 1e-05

        def _ln(x, g, b):
            mu = x.mean(-1, keepdims=True)
            var = ((x - mu) ** 2).mean(-1, keepdims=True)
            return (x - mu) * jax.lax.rsqrt(var + LN_EPS) * g + b

        def _gatv2(x, edge_index, edge_attr, W_l, W_r, W_e, att, bias):
            n = x.shape[0]
            loop = jnp.arange(n, dtype=edge_index.dtype)
            src = jnp.concatenate([edge_index[0], loop])
            dst = jnp.concatenate([edge_index[1], loop])
            ea = jnp.concatenate([edge_attr, jnp.broadcast_to(edge_attr.mean(0), (n, edge_attr.shape[1]))], 0)
            x_l = (x @ W_l).reshape(n, H, C)
            x_r = (x @ W_r).reshape(n, H, C)
            e = (ea @ W_e).reshape(-1, H, C)
            m = jax.nn.leaky_relu(x_l[src] + x_r[dst] + e, NEG_SLOPE)
            alpha = jnp.einsum('ehc,hc->eh', m, att)
            amax = jax.ops.segment_max(alpha, dst, num_segments=n)
            expa = jnp.exp(alpha - amax[dst])
            denom = jax.ops.segment_sum(expa, dst, num_segments=n)
            a = expa / (denom[dst] + 1e-16)
            out = jax.ops.segment_sum(x_l[src] * a[:, :, None], dst, num_segments=n)
            return out.reshape(n, D) + bias
        key = jax.random.key(seed)
        k = jax.random.split(key, 9)

        def gw(i, shape, fan_in):
            return jax.random.normal(k[i], shape, jnp.float32) / np.sqrt(fan_in).astype(np.float32)
        return {'x': jax.random.normal(k[0], (N, D), jnp.float32), 'edge_index': jax.random.randint(k[1], (2, E), 0, N, jnp.int32), 'edge_attr': jax.random.normal(k[2], (E, DE), jnp.float32), 'W_l': gw(3, (D, D), D), 'W_r': gw(4, (D, D), D), 'W_e': gw(5, (DE, D), DE), 'att': gw(6, (H, C), C), 'bias': jnp.zeros((D,), jnp.float32), 'ln1_g': jnp.ones((D,), jnp.float32), 'ln1_b': jnp.zeros((D,), jnp.float32), 'ln2_g': jnp.ones((D,), jnp.float32), 'ln2_b': jnp.zeros((D,), jnp.float32), 'W1': gw(7, (D, 2 * D), D), 'b1': jnp.zeros((2 * D,), jnp.float32), 'W2': gw(8, (2 * D, D), 2 * D), 'b2': jnp.zeros((D,), jnp.float32)}
    _L0_gnn_all = _L0_gnn_setup()
    _L0_gnn_in = {k: v for k, v in _L0_gnn_all.items() if k in ('W_l', 'W_r', 'W_e', 'att', 'bias', 'ln1_g', 'ln1_b', 'ln2_g', 'ln2_b', 'W1', 'b1', 'W2', 'b2')}
    del _L0_gnn_all

    def _L1_gnn_setup():
        import jax, jax.numpy as jnp
        import numpy as np
        N, E, D, R = (50000, 50000, 128, 40)
        DIFFUSION_STEPS = 1
        key = jax.random.key(seed)
        ks = jax.random.split(key, 8)
        return {'h': jax.random.normal(ks[0], (N, D), dtype=jnp.float32), 'rFeatures': jax.random.normal(ks[1], (R, D), dtype=jnp.float32), 'relation_weights': jax.random.normal(ks[2], (R, D, D), dtype=jnp.float32) * (1.0 / np.sqrt(D)), 'loop_weight': jax.random.normal(ks[3], (D, D), dtype=jnp.float32) * (1.0 / np.sqrt(D)), 'norm': jax.random.uniform(ks[4], (N, 1), dtype=jnp.float32), 'edge_src': jax.random.randint(ks[5], (E,), 0, N, dtype=jnp.int32), 'edge_dst': jax.random.randint(ks[6], (E,), 0, N, dtype=jnp.int32), 'edge_type': jax.random.randint(ks[7], (E,), 0, R, dtype=jnp.int32)}
    _L1_gnn_all = _L1_gnn_setup()
    _L1_gnn_in = {k: v for k, v in _L1_gnn_all.items() if k in ('rFeatures', 'relation_weights', 'loop_weight')}
    del _L1_gnn_all

    def _L2_gnn_setup():
        import jax, jax.numpy as jnp
        import numpy as np
        N = 3125
        E = 50000
        D = 128
        key = jax.random.key(seed)
        ks = jax.random.split(key, 8)
        x = jax.random.normal(ks[0], (N, D), dtype=jnp.float32)
        rows = jnp.concatenate([jnp.arange(N, dtype=jnp.int64), jax.random.randint(ks[1], (E - N,), 0, N, dtype=jnp.int64)])
        cols = jax.random.randint(ks[2], (E,), 0, N, dtype=jnp.int64)
        vals = jnp.ones((E,), dtype=jnp.float32)
        W1 = jax.random.normal(ks[3], (D, D), dtype=jnp.float32) * (1.0 / np.sqrt(D))
        b1 = jax.random.normal(ks[4], (D,), dtype=jnp.float32) * 0.01
        W2 = jax.random.normal(ks[5], (D, D), dtype=jnp.float32) * (1.0 / np.sqrt(D))
        b2 = jax.random.normal(ks[6], (D,), dtype=jnp.float32) * 0.01
        return {'x': x, 'rows': rows, 'cols': cols, 'vals': vals, 'W1': W1, 'b1': b1, 'W2': W2, 'b2': b2}
    _L2_gnn_all = _L2_gnn_setup()
    _L2_gnn_in = {k: v for k, v in _L2_gnn_all.items() if k in ('W1', 'b1', 'W2', 'b2')}
    del _L2_gnn_all

    def _L3_gnn_setup():
        import jax, jax.numpy as jnp
        import numpy as np
        N_NODES = 3125

        def _deg_inv_sqrt(idx, n):
            deg = jax.ops.segment_sum(jnp.ones(idx.shape, jnp.float32), idx, num_segments=n)
            deg = jnp.clip(deg, 1.0)
            return jax.lax.rsqrt(deg)

        def _graph_conv(h, W, b, src, dst, out_norm, in_norm, n):
            h = h * out_norm[:, None]
            h = h @ W
            msg = jnp.take(h, src, axis=0)
            agg = jax.ops.segment_sum(msg, dst, num_segments=n)
            return jax.nn.relu(agg * in_norm[:, None] + b)
        key = jax.random.key(seed)
        ks = jax.random.split(key, 5)
        E = 50000
        return {'features': jax.random.normal(ks[0], (N_NODES, 128), jnp.float32), 'src': jax.random.randint(ks[1], (E,), 0, N_NODES, jnp.int32), 'dst': jax.random.randint(ks[2], (E,), 0, N_NODES, jnp.int32), 'W1': jax.random.normal(ks[3], (128, 128), jnp.float32) * (1.0 / np.sqrt(128)), 'b1': jnp.zeros((128,), jnp.float32), 'W2': jax.random.normal(ks[4], (128, 128), jnp.float32) * (1.0 / np.sqrt(128)), 'b2': jnp.zeros((128,), jnp.float32)}
    _L3_gnn_all = _L3_gnn_setup()
    _L3_gnn_in = {k: v for k, v in _L3_gnn_all.items() if k in ('W1', 'b1', 'W2', 'b2')}
    del _L3_gnn_all
    return {'x': x, 'src': src, 'dst': dst, 'edge_attr_32': edge_attr_32, 'edge_type_40': edge_type_40, 'edge_weight': edge_weight, 'L0_gnn_W_l': _L0_gnn_in['W_l'], 'L0_gnn_W_r': _L0_gnn_in['W_r'], 'L0_gnn_W_e': _L0_gnn_in['W_e'], 'L0_gnn_att': _L0_gnn_in['att'], 'L0_gnn_bias': _L0_gnn_in['bias'], 'L0_gnn_ln1_g': _L0_gnn_in['ln1_g'], 'L0_gnn_ln1_b': _L0_gnn_in['ln1_b'], 'L0_gnn_ln2_g': _L0_gnn_in['ln2_g'], 'L0_gnn_ln2_b': _L0_gnn_in['ln2_b'], 'L0_gnn_W1': _L0_gnn_in['W1'], 'L0_gnn_b1': _L0_gnn_in['b1'], 'L0_gnn_W2': _L0_gnn_in['W2'], 'L0_gnn_b2': _L0_gnn_in['b2'], 'L1_gnn_rFeatures': _L1_gnn_in['rFeatures'], 'L1_gnn_relation_weights': _L1_gnn_in['relation_weights'], 'L1_gnn_loop_weight': _L1_gnn_in['loop_weight'], 'L2_gnn_W1': _L2_gnn_in['W1'], 'L2_gnn_b1': _L2_gnn_in['b1'], 'L2_gnn_W2': _L2_gnn_in['W2'], 'L2_gnn_b2': _L2_gnn_in['b2'], 'L3_gnn_W1': _L3_gnn_in['W1'], 'L3_gnn_b1': _L3_gnn_in['b1'], 'L3_gnn_W2': _L3_gnn_in['W2'], 'L3_gnn_b2': _L3_gnn_in['b2']}

def reference(x, src, dst, edge_attr_32, edge_type_40, edge_weight, L0_gnn_W_l, L0_gnn_W_r, L0_gnn_W_e, L0_gnn_att, L0_gnn_bias, L0_gnn_ln1_g, L0_gnn_ln1_b, L0_gnn_ln2_g, L0_gnn_ln2_b, L0_gnn_W1, L0_gnn_b1, L0_gnn_W2, L0_gnn_b2, L1_gnn_rFeatures, L1_gnn_relation_weights, L1_gnn_loop_weight, L2_gnn_W1, L2_gnn_b1, L2_gnn_W2, L2_gnn_b2, L3_gnn_W1, L3_gnn_b1, L3_gnn_W2, L3_gnn_b2):
    import jax
    import jax.numpy as jnp

    def _L0_gnn_ref(x, edge_index, edge_attr, W_l, W_r, W_e, att, bias, ln1_g, ln1_b, ln2_g, ln2_b, W1, b1, W2, b2):
        import jax, jax.numpy as jnp
        import numpy as np
        N = 50000
        E = 625000
        D = 128
        H = 8
        C = D // H
        DE = 32
        NEG_SLOPE = 0.2
        LN_EPS = 1e-05

        def _ln(x, g, b):
            mu = x.mean(-1, keepdims=True)
            var = ((x - mu) ** 2).mean(-1, keepdims=True)
            return (x - mu) * jax.lax.rsqrt(var + LN_EPS) * g + b

        def _gatv2(x, edge_index, edge_attr, W_l, W_r, W_e, att, bias):
            n = x.shape[0]
            loop = jnp.arange(n, dtype=edge_index.dtype)
            src = jnp.concatenate([edge_index[0], loop])
            dst = jnp.concatenate([edge_index[1], loop])
            ea = jnp.concatenate([edge_attr, jnp.broadcast_to(edge_attr.mean(0), (n, edge_attr.shape[1]))], 0)
            x_l = (x @ W_l).reshape(n, H, C)
            x_r = (x @ W_r).reshape(n, H, C)
            e = (ea @ W_e).reshape(-1, H, C)
            m = jax.nn.leaky_relu(x_l[src] + x_r[dst] + e, NEG_SLOPE)
            alpha = jnp.einsum('ehc,hc->eh', m, att)
            amax = jax.ops.segment_max(alpha, dst, num_segments=n)
            expa = jnp.exp(alpha - amax[dst])
            denom = jax.ops.segment_sum(expa, dst, num_segments=n)
            a = expa / (denom[dst] + 1e-16)
            out = jax.ops.segment_sum(x_l[src] * a[:, :, None], dst, num_segments=n)
            return out.reshape(n, D) + bias
        h = x + _gatv2(_ln(x, ln1_g, ln1_b), edge_index, edge_attr, W_l, W_r, W_e, att, bias)
        ff = jax.nn.gelu(_ln(h, ln2_g, ln2_b) @ W1 + b1, approximate=False) @ W2 + b2
        return h + ff

    def _L1_gnn_ref(h, rFeatures, relation_weights, loop_weight, norm, edge_src, edge_dst, edge_type):
        import jax, jax.numpy as jnp
        import numpy as np
        N, E, D, R = (50000, 50000, 128, 40)
        DIFFUSION_STEPS = 1
        n, d = h.shape
        r = relation_weights.shape[0]
        seg = edge_dst.astype(jnp.int32) * r + edge_type.astype(jnp.int32)
        for _ in range(DIFFUSION_STEPS):
            S = jax.ops.segment_sum(h[edge_src], seg, num_segments=n * r).reshape(n, r, d)
            cnt = jax.ops.segment_sum(jnp.ones(edge_src.shape, h.dtype), seg, num_segments=n * r).reshape(n, r)
            agg = jnp.einsum('nrd,rdf->nf', S, relation_weights) + cnt @ rFeatures
            h = agg * norm
        h = jax.nn.relu(h + h @ loop_weight)
        return h

    def _L2_gnn_ref(x, rows, cols, vals, W1, b1, W2, b2):
        import jax, jax.numpy as jnp
        import numpy as np
        N = 3125
        E = 50000
        D = 128
        n = x.shape[0]
        x_node = x @ W1.T + b1
        m = jax.ops.segment_sum(vals[:, None] * x[cols], rows, num_segments=n)
        m = m @ W2.T + b2
        deg = jax.ops.segment_sum(vals, rows, num_segments=n)
        return x_node + m / deg[:, None]

    def _L3_gnn_ref(features, src, dst, W1, b1, W2, b2):
        import jax, jax.numpy as jnp
        import numpy as np
        N_NODES = 3125

        def _deg_inv_sqrt(idx, n):
            deg = jax.ops.segment_sum(jnp.ones(idx.shape, jnp.float32), idx, num_segments=n)
            deg = jnp.clip(deg, 1.0)
            return jax.lax.rsqrt(deg)

        def _graph_conv(h, W, b, src, dst, out_norm, in_norm, n):
            h = h * out_norm[:, None]
            h = h @ W
            msg = jnp.take(h, src, axis=0)
            agg = jax.ops.segment_sum(msg, dst, num_segments=n)
            return jax.nn.relu(agg * in_norm[:, None] + b)
        n = features.shape[0]
        out_norm = _deg_inv_sqrt(src, n)
        in_norm = _deg_inv_sqrt(dst, n)
        h = _graph_conv(features, W1, b1, src, dst, out_norm, in_norm, n)
        h = _graph_conv(h, W2, b2, src, dst, out_norm, in_norm, n)
        return h
    edge_index = jnp.stack([src, dst])
    deg = jnp.maximum(jax.ops.segment_sum(jnp.ones(dst.shape, jnp.float32), dst, num_segments=3125), 1.0)
    deg_isqrt = deg ** (-0.5)
    h = jnp.maximum(_layernorm(x, axis=-1), 0.0)
    x = x + _L0_gnn_ref(h, edge_index, edge_attr_32, L0_gnn_W_l, L0_gnn_W_r, L0_gnn_W_e, L0_gnn_att, L0_gnn_bias, L0_gnn_ln1_g, L0_gnn_ln1_b, L0_gnn_ln2_g, L0_gnn_ln2_b, L0_gnn_W1, L0_gnn_b1, L0_gnn_W2, L0_gnn_b2)
    h = jnp.maximum(_layernorm(x, axis=-1), 0.0)
    x = x + _L1_gnn_ref(h, L1_gnn_rFeatures, L1_gnn_relation_weights, L1_gnn_loop_weight, deg_isqrt[:, None], src, dst, edge_type_40)
    h = jnp.maximum(_layernorm(x, axis=-1), 0.0)
    x = x + _L2_gnn_ref(h, src, dst, edge_weight, L2_gnn_W1, L2_gnn_b1, L2_gnn_W2, L2_gnn_b2)
    h = jnp.maximum(_layernorm(x, axis=-1), 0.0)
    x = x + _L3_gnn_ref(h, src, dst, L3_gnn_W1, L3_gnn_b1, L3_gnn_W2, L3_gnn_b2)
    return x

_drawn_inputs = setup_inputs


def setup_inputs(seed=0):
    import zlib

    import numpy as np

    out = dict(_drawn_inputs(seed))
    spreads = {'L0_gnn_bias': (0.0, 0.1),
     'L0_gnn_ln1_g': (1.0, 0.2),
     'L0_gnn_ln1_b': (0.0, 0.1),
     'L0_gnn_ln2_g': (1.0, 0.2),
     'L0_gnn_ln2_b': (0.0, 0.269),
     'L0_gnn_b1': (0.0, 0.1),
     'L0_gnn_b2': (0.0, 0.1),
     'L3_gnn_b1': (0.0, 0.471),
     'L3_gnn_b2': (0.0, 0.348)}
    factors = {'L2_gnn_b1': 8.0, 'L2_gnn_b2': 64.0}
    for name, (base, spread) in spreads.items():
        noise = np.random.default_rng([zlib.crc32(name.encode()), seed]).standard_normal(out[name].shape)
        drawn = base * np.exp(spread * noise) if base else spread * noise
        out[name] = jnp.asarray(drawn.astype(out[name].dtype))
    for name, factor in factors.items():
        out[name] = (out[name] * factor).astype(out[name].dtype)
    return out
```

```python
from contextlib import ExitStack

import concourse.bass as bass
from concourse import mybir

F32 = mybir.dt.float32
BF16 = mybir.dt.bfloat16
I32 = mybir.dt.int32
ALU = mybir.AluOpType
ACT = mybir.ActivationFunctionType
AX = mybir.AxisListType

P = 128
D = 128
N = 3125
NT = -(-N // P)
NP = NT * P
E = 50000
ET = -(-E // P)
EP = ET * P
T = ET + NT
TE = T * P
LN1_G, LN1_B, LN2_G, LN2_B, ATT, BIAS, L0_B2, L2_B1, L2_B2, L3_B1, L3_B2 = range(11)
PARS = 11
H, C = 8, 16
DE = 32
R = 40
EPS = 1e-5
RW = DE + 5
RW2 = 3
SELF, WEIGHT, SRC, TYPE, DST = range(5)
FAR = 1e30
G = 4
U = 8
NB = 5
CH = P // H
CT = T // CH
CL = CT * P
assert T == CH * CT and T % (2 * G) == 0 and T % (2 * U) == 0 and NT % NB == 0


class Space:

    def __init__(self, nc, name):
        self.nc, self.name, self.ctx, self.sems = nc, name, ExitStack(), []
        self.blocks = ExitStack()

    def __enter__(self):
        return self

    def __exit__(self, *a):
        self.blocks.close()
        if self.sems:
            self.nc.clear_and_free_semaphores(self.sems)
            self.nc.all_engine_barrier()
        self.ctx.close()

    def sb(self, name, shape, dt=F32):
        return self.ctx.enter_context(self.nc.sbuf_tensor(f"{self.name}_{name}", shape, dt))

    def ps(self, name, shape, dt=F32):
        return self.ctx.enter_context(self.nc.psum_tensor(f"{self.name}_{name}", shape, dt))

    def sem(self, name):
        self.sems.append(self.nc.alloc_semaphore(f"{self.name}_{name}"))
        return self.sems[-1]

    def block(self):
        return self.blocks.enter_context(self.nc.Block())


def bc(ap, shape, axis):
    return ap.unsqueeze(axis).to_broadcast(shape)


def hold(eng):
    eng.nop(nofuse=True)


def count_phase(nc, d, k):
    B = 16
    with Space(nc, "count") as s:
        diff_i, part_i, flat_i = s.sb("diff_i", [P, P], I32), s.sb("part_i", [P, 1], I32), s.sb("flat_i", [P, T], I32)
        diff = s.sb("diff", [P, P])
        part = s.sb("part", [P, 1])
        flat = s.sb("flat", [P, T])
        raw = s.sb("raw", [P, 3, T], I32)
        lohi_i = s.sb("lohi_i", [P, 4, T], I32)
        upper, ones = s.sb("upper", [P, P]), s.sb("ones", [P, P])
        zeros = s.sb("zeros", [P, P], BF16)
        oh = s.sb("oh", [P, 2, 2, B, P], BF16)
        ohh = s.sb("ohh", [P, 2, 2, B, NT], BF16)
        hist_sb = s.sb("hist_sb", [P, 2, NT])
        tot_sb, run_sb = s.sb("tot_sb", [P, 2, NT]), s.sb("run_sb", [P, 2, NT])
        hist = [s.ps(f"hist{j}", [P, 512]) for j in range(2)]
        pre, tot = s.ps("pre", [P, 512]), s.ps("tot", [P, 512])
        loaded = s.sem("loaded")
        iotas = s.sem("iotas")
        made = s.sem("made")
        onehots = [s.sem(f"onehots{h}") for h in range(2)]
        counted = [s.sem(f"counted{h}") for h in range(2)]
        total = s.sem("total")
        hist_out = s.sem("hist_out")
        prefix = s.sem("prefix")
        based = s.sem("based")
        consts = s.sem("consts")
        block = s.block()
        MADE = 16

        @block.sync
        def _(sp):
            for j, name in enumerate(("src", "type", "dst")):
                sp.dma_start(raw[:, j, :], d[name].rearrange("(p t) -> p t", p=P)).then_inc(loaded, 16)
            sp.dma_start(k["meta"][:, WEIGHT, :], d["weight"].rearrange("(p t) -> p t", p=P)).then_inc(loaded, 16)
            sp.wait_ge(loaded, 64)

        @block.gpsimd
        def _(pool):
            pool.iota(diff_i[:, :], pattern=[[1, P]], base=0, channel_multiplier=-1).then_inc(iotas, 1)
            pool.iota(part_i[:, :], pattern=[[1, 1]], base=0, channel_multiplier=1).then_inc(iotas, 1)
            pool.iota(flat_i[:, :], pattern=[[1, T]], base=0, channel_multiplier=T).then_inc(iotas, 1)

        @block.vector
        def _(v):
            v.memset(zeros[:, :], 0.0).then_inc(consts, 1)
            v.memset(ones[:, :], 1.0).then_inc(consts, 1)
            v.wait_ge(iotas, 3)
            v.tensor_copy(diff[:, :], diff_i[:, :]).then_inc(made, 1)
            v.tensor_copy(part[:, :], part_i[:, :]).then_inc(made, 1)
            v.tensor_copy(flat[:, :], flat_i[:, :]).then_inc(made, 1)
            v.wait_ge(loaded, 64)
            for j, f in enumerate((SRC, TYPE, DST)):
                v.tensor_copy(k["meta"][:, f, :], raw[:, j, :]).then_inc(made, 1)
            for j, f in ((0, 2), (2, 0)):
                v.tensor_scalar(lohi_i[:, j, :], raw[:, f, :], P - 1, None, ALU.bitwise_and).then_inc(made, 1)
                v.tensor_scalar(lohi_i[:, j + 1, :], raw[:, f, :], 7, None,
                                ALU.arith_shift_right).then_inc(made, 1)
            v.wait_ge(made, 10)
            v.tensor_scalar(k["ident"][:, :], diff[:, :], 0.0, None, ALU.is_equal).then_inc(made, 1)
            v.tensor_scalar(k["identb"][:, :], diff[:, :], 0.0, None, ALU.is_equal).then_inc(made, 1)
            v.tensor_scalar(k["before"][:, :], diff[:, :], 0.0, None, ALU.is_lt).then_inc(made, 1)
            v.tensor_scalar(upper[:, :], diff[:, :], 0.0, None, ALU.is_gt).then_inc(made, 1)
            v.tensor_scalar(k["iota"][:, :], diff[:, :], part[:, 0:1], None, ALU.add).then_inc(made, 1)
            v.tensor_scalar(k["last"][:, :], part[:, :], float(P - 1), None, ALU.is_equal).then_inc(made, 1)
            v.tensor_scalar(k["meta"][:, SELF, :], flat[:, :], float(EP), None, ALU.is_ge)
            for j, to in enumerate((k["dlo"], k["dhi"], k["slo"], k["shi"])):
                w = v.tensor_copy(to[:, :], lohi_i[:, j, :])
            w.then_inc(made, 1)
            v.wait_ge(made, MADE + 1)
            with v.Fori(0, T // (2 * B)) as i:
                for h in range(2):
                    v.wait_ge(counted[h], i)
                    at = bass.ds(i * (2 * B) + h * B, B)
                    for j, (lo, hi) in enumerate(((k["dlo"], k["dhi"]), (k["slo"], k["shi"]))):
                        v.tensor_tensor(oh[:, h, j], bc(lo[:, at], [P, B, P], 2), bc(k["iota"][:, :], [P, B, P], 1),
                                        ALU.is_equal)
                        w = v.tensor_tensor(ohh[:, h, j], bc(hi[:, at], [P, B, NT], 2),
                                            bc(k["iota"][:, 0:NT], [P, B, NT], 1), ALU.is_equal)
                    w.then_inc(onehots[h], 1)
            v.wait_ge(total, 1)
            for j in range(2):
                v.tensor_copy(hist_sb[:, j, :], hist[j][:, 0:NT]).then_inc(hist_out, 1)
            v.wait_ge(prefix, 1)
            v.wait_ge(hist_out, 2)
            v.tensor_copy(tot_sb[:, :, :], tot[:, 0:2 * NT].rearrange("p (j t) -> p j t", j=2)).then_inc(based, 1)
            v.wait_ge(based, 1)
            for j in range(2):
                w = v.tensor_tensor_scan(run_sb[:, j, :], ones[:, 0:NT], tot_sb[:, j, :], 0.0, ALU.mult, ALU.add)
            w.then_inc(based, 1)
            v.wait_ge(based, 2)
            v.tensor_tensor(run_sb[:, :, :], run_sb[:, :, :], tot_sb[:, :, :], ALU.subtract).then_inc(based, 1)
            v.wait_ge(based, 3)
            v.tensor_tensor(k["base"][:, :, :], run_sb[:, :, :], pre[:, 0:2 * NT].rearrange("p (j t) -> p j t", j=2),
                            ALU.add).then_inc(based, 1)
            v.wait_ge(based, 4)
            v.scalar_tensor_tensor(k["lastpos"][:, :, :], k["base"][:, :, :], -1.0, hist_sb[:, :, :], ALU.add, ALU.add)
            v.tensor_scalar(k["deg_dst"][:, :], hist_sb[:, 0, :], -1.0, None, ALU.add)
            v.tensor_scalar(k["deg_src"][:, :], hist_sb[:, 1, :], -1.0, None, ALU.add).then_inc(based, 1)

        @block.tensor
        def _(pe):
            pe.wait_ge(consts, 2)
            for j in range(2):
                pe.matmul(hist[j][:, 0:NT], zeros[:, :], zeros[:, 0:NT], start=True, stop=False)
            with pe.Fori(0, T // (2 * B)) as i:
                for h in range(2):
                    pe.wait_ge(onehots[h], i + 1)
                    for j in range(2):
                        for u in range(B):
                            m = pe.matmul(hist[j][:, 0:NT], oh[:, h, j, u, :], ohh[:, h, j, u, :],
                                          start=False, stop=False, skip_group_check=True)
                    m.then_inc(counted[h], 1)
            for j in range(2):
                m = pe.matmul(hist[j][:, 0:NT], zeros[:, :], zeros[:, 0:NT], start=False, stop=True)
            m.then_inc(total, 1)
            pe.wait_ge(hist_out, 2)
            pe.wait_ge(made, MADE)
            pe.matmul(pre[:, 0:2 * NT], upper[:, :], hist_sb[:, :, :], start=True, stop=True)
            pe.matmul(tot[:, 0:2 * NT], ones[:, :], hist_sb[:, :, :], start=True, stop=True).then_inc(prefix, 1)


def sort_phase(nc, d, k, by):
    with Space(nc, f"sort{by}") as s:
        width, field, lo, hi = ((RW, DST, k["dlo"], k["dhi"]), (RW2, SRC, k["slo"], k["shi"]))[by]
        attr = s.sb("attr", [P, T, DE]) if by == 0 else None
        asum = s.sb("asum", [P, DE])
        ones = s.sb("ones", [P, 1])
        oh = s.sb("oh", [P, 2, G, P], BF16)
        ohh = s.sb("ohh", [P, 2, G, NT])
        ohhb = s.sb("ohhb", [P, 2, G, NT], BF16)
        oht = s.sb("oht", [P, 2, G, P])
        dcol = s.sb("dcol", [P, 2, G])
        base = s.sb("base", [P, 2, G, NT])
        junk = s.sb("junk", [P, G, P])
        junk2 = s.sb("junk2", [P, G, NT])
        inside, outside = s.sb("inside", [P, 2, G]), s.sb("outside", [P, 2, G])
        place = s.sb("place", [P, 2, G], I32)
        rec = s.sb("rec", [P, 2, G, width])
        rowb = [s.ps(f"rowb{h}", [P, G, P]) for h in range(2)]
        tr = s.ps("tr", [P, 2, G, P], BF16)
        step = s.ps("step", [P, 2, G, 32])
        got = s.ps("got", [P, 2, G, 32])
        mean = s.ps("mean", [DE, 512])
        loaded = s.sem("loaded")
        summed = s.sem("summed")
        onehots = s.sem("onehots")
        rows = s.sem("rows")
        turned = s.sem("turned")
        tr_out = s.sem("tr_out")
        based = s.sem("based")
        looked = s.sem("looked")
        placed = [s.sem(f"placed{h}") for h in range(2)]
        chain = s.sem("chain")
        recs = s.sem("recs")
        sent = [s.sem(f"sent{h}") for h in range(2)]
        meaned = s.sem("meaned")
        ready = s.sem("ready")
        block = s.block()
        n = T // (2 * G)

        @block.sync
        def _(sp):
            if by == 0:
                sp.dma_start(attr[:, :, :], d["attr"].rearrange("(p t) w -> p t w", p=P)).then_inc(loaded, 16)

        @block.vector
        def _(v):
            v.memset(ones[:, :], 1.0).then_inc(ready, 1)
            v.tensor_copy(base[:, 0, 0, :], k["base"][:, by, :]).then_inc(ready, 1)
            v.wait_ge(ready, 2)
            with v.Fori(0, n) as i:
                for h in range(2):
                    g = i * 2 + h
                    at = bass.ds(i * (2 * G) + h * G, G)
                    v.tensor_copy(dcol[:, h, :], k["meta"][:, field, at])
                    v.tensor_tensor(oh[:, h], bc(lo[:, at], [P, G, P], 2), bc(k["iota"][:, :], [P, G, P], 1),
                                    ALU.is_equal)
                    v.tensor_tensor(ohhb[:, h], bc(hi[:, at], [P, G, NT], 2),
                                    bc(k["iota"][:, 0:NT], [P, G, NT], 1), ALU.is_equal)
                    v.tensor_tensor(ohh[:, h], bc(hi[:, at], [P, G, NT], 2),
                                    bc(k["iota"][:, 0:NT], [P, G, NT], 1), ALU.is_equal).then_inc(onehots, 1)
                    v.wait_ge(onehots, g + 1)
                    v.wait_ge(rows, g + 1)
                    v.wait_ge(sent[h], i * (16 * G))
                    for u in range(G):
                        v.scalar_tensor_tensor(junk[:, u, :], rowb[h][:, u, :], dcol[:, h, u:u + 1], k["before"][:, :],
                                               ALU.is_equal, ALU.mult, accum_out=inside[:, h, u:u + 1]
                                               ).then_inc(chain, 1)
                    v.wait_ge(turned, g + 1)
                    for u in range(G):
                        nh, nu = (h, u + 1) if u < G - 1 else (1 - h, 0)
                        if u:
                            v.wait_ge(based, g * G + u)
                        v.tensor_tensor(base[:, nh, nu, :], base[:, h, u, :], step[:, h, u, 0:NT],
                                        ALU.add).then_inc(based, 1)
                    v.wait_ge(looked, g + 1)
                    v.wait_ge(chain, g * (2 * G) + G)
                    for u in range(G):
                        v.scalar_tensor_tensor(junk2[:, u, :], got[:, h, u, 0:NT], 1.0, ohh[:, h, u, :],
                                               ALU.mult, ALU.mult, accum_out=outside[:, h, u:u + 1]
                                               ).then_inc(chain, 1)
                    v.wait_ge(chain, (g + 1) * (2 * G))
                    v.wait_ge(based, (g + 1) * G)
                    v.tensor_tensor(place[:, h, :], inside[:, h, :], outside[:, h, :], ALU.add).then_inc(placed[h], 1)
            if by == 0:
                v.wait_ge(loaded, 16)
                v.tensor_reduce(asum[:, :], attr[:, :, :].rearrange("p t w -> p w t"), AX.X, ALU.add).then_inc(summed, 1)
                v.wait_ge(meaned, 1)
                v.tensor_scalar(k["mean"][:, :], mean[:, 0:1], 1.0 / E, None, ALU.mult).then_inc(summed, 1)

        @block.tensor
        def _(pe):
            pe.wait_ge(ready, 2)
            with pe.Fori(0, n) as i:
                for h in range(2):
                    g = i * 2 + h
                    pe.wait_ge(onehots, g + 1)
                    pe.wait_ge(placed[h], i)
                    for u in range(G):
                        m = pe.matmul(rowb[h][:, u, :], dcol[:, h, u:u + 1].to_broadcast([P, P]), k["ident"][:, :],
                                      start=True, stop=True)
                    m.then_inc(rows, 1)
                    for u in range(G):
                        pe.transpose(tr[:, h, u, :], oh[:, h, u, :], k["identb"][:, :])
                    for u in range(G):
                        m = pe.matmul(step[:, h, u, 0:NT], oh[:, h, u, :], ohhb[:, h, u, :], start=True, stop=True)
                    m.then_inc(turned, 1)
                    pe.wait_ge(tr_out, g + 1)
                    pe.wait_ge(based, (g + 1) * G - 1)
                    for u in range(G):
                        m = pe.matmul(got[:, h, u, 0:NT], oht[:, h, u, :], base[:, h, u, :], start=True, stop=True)
                    m.then_inc(looked, 1)
            if by == 0:
                pe.wait_ge(summed, 1)
                pe.matmul(mean[:, 0:1], asum[:, :], ones[:, :], start=True, stop=True).then_inc(meaned, 1)

        @block.scalar
        def _(act):
            if by == 0:
                act.wait_ge(loaded, 16)
            with act.Fori(0, n) as i:
                for h in range(2):
                    at = bass.ds(i * (2 * G) + h * G, G)
                    act.wait_ge(turned, i * 2 + h + 1)
                    act.copy(oht[:, h], tr[:, h]).then_inc(tr_out, 1)
                    act.wait_ge(sent[h], i * (16 * G))
                    if by == 0:
                        act.copy(rec[:, h, :, 0:DE], attr[:, at, :])
                        act.copy(rec[:, h, :, DE:RW], k["meta"][:, :, at].rearrange("p f t -> p t f")).then_inc(recs, 1)
                    else:
                        for c, f in enumerate((DST, WEIGHT, SRC)):
                            m = act.copy(rec[:, h, :, c], k["meta"][:, f, at])
                        m.then_inc(recs, 1)

        @block.gpsimd
        def _(pool):
            with pool.Fori(0, n) as i:
                for h in range(2):
                    pool.wait_ge(placed[h], i + 1)
                    pool.wait_ge(recs, i * 2 + h + 1)
                    hold(pool)
                    for u in range(G):
                        pool.indirect_dma_start(
                            out=d[("records", "records2")[by]][:, :], out_offset=bass.IndirectOffsetOnAxis(ap=place[:, h, u:u + 1], axis=0),
                            in_=rec[:, h, u, :], in_offset=None).then_inc(sent[h], 16)
            for h in range(2):
                pool.wait_ge(sent[h], n * 16 * G)


def norm_tensors(s, name):
    return dict(stats=s.sb(f"{name}_stats", [P, NB, 6]), mv=s.sb(f"{name}_mv", [P, NB, 2]), sd=s.sb(f"{name}_sd", [P, NB]),
                rs=s.sb(f"{name}_rs", [P, NB]), have_stats=s.sem(f"{name}_have_stats"), have_mv=s.sem(f"{name}_have_mv"),
                have_sd=s.sem(f"{name}_have_sd"), have_rs=s.sem(f"{name}_have_rs"), normed=s.sem(f"{name}_normed"))


def norm_vector(v, q, i, x, out):
    for u in range(NB):
        w = v.bn_stats(q["stats"][:, u, :], x[:, u, :])
    w.then_inc(q["have_stats"], 1)
    v.wait_ge(q["have_stats"], i + 1)
    hold(v)
    for u in range(NB):
        w = v.bn_aggr(q["mv"][:, u, :], q["stats"][:, u, :])
    w.then_inc(q["have_mv"], 1)
    v.wait_ge(q["have_sd"], i + 1)
    v.reciprocal(q["rs"][:, :], q["sd"][:, :]).then_inc(q["have_rs"], 1)
    v.wait_ge(q["have_rs"], i + 1)
    for u in range(NB):
        w = v.tensor_scalar(out[:, u, :], x[:, u, :], q["mv"][:, u, 0:1], q["rs"][:, u:u + 1], ALU.subtract, ALU.mult)
    w.then_inc(q["normed"], 1)


def norm_scalar(act, q, i, k):
    act.wait_ge(q["have_mv"], i + 1)
    act.activation(q["sd"][:, :], q["mv"][:, :, 1], ACT.Sqrt, bias=k["eps"][:, 0:1]).then_inc(q["have_sd"], 1)


def rows_of(table, i):
    return table.rearrange("(a l) w -> l a w", l=P)[:, bass.ds(i * NB, NB), :]


def enter_phase(nc, d, k):
    with Space(nc, "enter") as s:
        wlr = s.sb("wlr", [P, 2 * D])
        we = s.sb("we", [DE, D])
        aug = s.sb("aug", [DE, DE + 1])
        xs, h0, hn, ht = (s.sb(n, [P, NB, D]) for n in ("xs", "h0", "hn", "ht"))
        lr = s.sb("lr", [P, 2, NB, D])
        tp = s.ps("tp", [P, 8, D])
        mm = s.ps("mm", [P, 6, 2 * D])
        wa = s.ps("wa", [P, 512])
        q1, q2 = norm_tensors(s, "n1"), norm_tensors(s, "n2")
        loaded, epsed, tabled = s.sem("loaded"), s.sem("epsed"), s.sem("tabled")
        augged, edged, kept = s.sem("augged"), s.sem("edged"), s.sem("kept")
        taken, relued, scaled = s.sem("taken"), s.sem("relued"), s.sem("scaled")
        affine, turned, turned_out = s.sem("affine"), s.sem("turned"), s.sem("turned_out")
        product, product_out, stored = s.sem("product"), s.sem("product_out"), s.sem("stored")
        block = s.block()
        n = NT // NB
        par = k["par"]

        @block.sync
        def _(sp):
            sp.dma_start(k["x"][:, :, :], d["x"].rearrange("(a l) w -> l a w", l=P)).then_inc(loaded, 16)
            sp.dma_start(wlr[:, :], d["wlr"]).then_inc(loaded, 16)
            sp.dma_start(we[:, :], d["we"]).then_inc(loaded, 16)
            sp.dma_start(k["rec2"][:, :, :], d["records2"].rearrange("(t p) w -> p t w", p=P)).then_inc(tabled, 16)
            sp.dma_start(k["par"][:, :, :], d["par"].rearrange("(o a) w -> o a w", o=1).to_broadcast([P, PARS, D])
                         ).then_inc(loaded, 16)
            with sp.Fori(0, n) as i:
                sp.wait_ge(product_out, i + 1)
                sp.dma_start(rows_of(d["left"], i), lr[:, 0]).then_inc(stored, 16)
                sp.dma_start(rows_of(d["right"], i), lr[:, 1]).then_inc(stored, 16)
            sp.wait_ge(stored, 32 * n)
            sp.wait_ge(tabled, 16)

        @block.vector
        def _(v):
            v.memset(k["eps"][:, :], EPS).then_inc(epsed, 1)
            v.tensor_copy(aug[:, 0:DE], k["ident"][0:DE, 0:DE])
            v.tensor_copy(aug[:, DE:DE + 1], k["mean"][:, :]).then_inc(augged, 1)
            v.wait_ge(loaded, 64)
            with v.Fori(0, n) as i:
                v.tensor_copy(xs[:, :, :], k["x"][:, bass.ds(i * NB, NB), :]).then_inc(taken, 1)
                v.wait_ge(taken, i + 1)
                norm_vector(v, q1, i, xs, h0)
                v.wait_ge(relued, i + 1)
                norm_vector(v, q2, i, h0, hn)
                v.wait_ge(q2["normed"], i + 1)
                v.tensor_tensor(hn[:, :, :], hn[:, :, :], bc(par[:, LN1_G, :], [P, NB, D], 1), ALU.mult).then_inc(scaled, 1)
                v.wait_ge(scaled, i + 1)
                v.tensor_tensor(hn[:, :, :], hn[:, :, :], bc(par[:, LN1_B, :], [P, NB, D], 1), ALU.add).then_inc(affine, 1)
                v.wait_ge(product, i + 1)
                v.wait_ge(stored, i * 32)
                v.tensor_copy(lr[:, :, :, :].rearrange("p s a w -> p a s w"),
                              mm[:, 0:NB, :].rearrange("p a (s w) -> p a s w", s=2)).then_inc(product_out, 1)

        @block.scalar
        def _(act):
            act.wait_ge(epsed, 1)
            with act.Fori(0, n) as i:
                norm_scalar(act, q1, i, k)
                act.wait_ge(q1["normed"], i + 1)
                act.activation(h0[:, :, :], h0[:, :, :], ACT.Relu).then_inc(relued, 1)
                act.wait_ge(relued, i + 1)
                act.copy(k["h"][:, bass.ds(i * NB, NB), :], h0[:, :, :]).then_inc(kept, 1)
                norm_scalar(act, q2, i, k)
                act.wait_ge(turned, i + 1)
                act.copy(ht[:, :, :], tp[:, 0:NB, :]).then_inc(turned_out, 1)
            act.wait_ge(edged, 1)
            act.copy(k["wedge"][:, :], wa[0:DE + 1, 0:D])

        @block.tensor
        def _(pe):
            with pe.Fori(0, n) as i:
                pe.wait_ge(affine, i + 1)
                for u in range(NB):
                    m = pe.transpose(tp[:, u, :], hn[:, u, :], k["ident"][:, :])
                m.then_inc(turned, 1)
                pe.wait_ge(turned_out, i + 1)
                pe.wait_ge(loaded, 64)
                for u in range(NB):
                    m = pe.matmul(mm[:, u, :], ht[:, u, :], wlr[:, :], start=True, stop=True)
                m.then_inc(product, 1)
            pe.wait_ge(augged, 1)
            pe.wait_ge(loaded, 64)
            pe.matmul(wa[0:DE + 1, 0:D], aug[:, :], we[:, :], start=True, stop=True).then_inc(edged, 1)


def score_phase(nc, d, k):
    with Space(nc, "score") as s:
        rec = s.sb("rec", [P, 2, U, RW])
        ends = s.sb("ends", [P, 2, 2, U], I32)
        rows = s.sb("rows", [P, 2, 2, U, D])
        at_sb = s.sb("at_sb", [DE + 1, 2, G, P])
        part, lk = s.sb("part", [P, 2, G, D]), s.sb("lk", [P, 2, G, D])
        yf = s.sb("yf", [P, 2, U])
        tp = [s.ps(f"tp{b}", [P, G, P]) for b in range(2)]
        z = [s.ps(f"z{b}", [P, G, D]) for b in range(2)]
        loaded = [s.sem(f"loaded{h}") for h in range(2)]
        cols = [s.sem(f"cols{h}") for h in range(2)]
        yready = s.sem("yready")
        gathered = [s.sem(f"gathered{h}") for h in range(2)]
        turned, turned_out = s.sem("turned"), s.sem("turned_out")
        summed = s.sem("summed")
        fifth, leaky, weighed = s.sem("fifth"), s.sem("leaky"), s.sem("weighed")
        scored = [[s.sem(f"scored{h}{b}") for b in range(2)] for h in range(2)]
        block = s.block()
        n = T // (2 * U)

        def loop(eng, body):
            with eng.Fori(0, n - 1) as i:
                body(i, False)
            body(n - 1, True)

        @block.sync
        def _(sp):
            with sp.Fori(0, n) as i:
                for h in range(2):
                    sp.wait_ge(scored[h][1], i)
                    at = bass.ds(i * (2 * U) + h * U, U)
                    sp.dma_start(rec[:, h], d["records"].rearrange("(t p) w -> p t w", p=P)[:, at, :]
                                 ).then_inc(loaded[h], 16)

        @block.vector
        def _(v):
            def extract(i, h):
                at = bass.ds(i * (2 * U) + h * U, U)
                v.wait_ge(loaded[h], (i + 1) * 16)
                v.tensor_copy(ends[:, h, 0, :], rec[:, h, :, DE + SRC])
                v.tensor_copy(ends[:, h, 1, :], rec[:, h, :, DE + DST]).then_inc(cols[h], 1)
                v.scalar_tensor_tensor(yf[:, h, :], rec[:, h, :, DE + SRC], float(R), rec[:, h, :, DE + TYPE],
                                       ALU.mult, ALU.add).then_inc(yready, 1)
                v.tensor_copy(k["src"][:, at], rec[:, h, :, DE + SRC])
                v.tensor_copy(k["dst"][:, at], rec[:, h, :, DE + DST])
                v.tensor_scalar(k["real"][:, at], rec[:, h, :, DE + SELF], -1.0, 1.0, ALU.mult, ALU.add)
                v.wait_ge(yready, i * 2 + h + 1)
                v.tensor_copy(k["relsrc"][:, at], yf[:, h, :])

            def score(i, h):
                for b in range(2):
                    g = (i * 2 + h) * 2 + b
                    v.wait_ge(summed, g + 1)
                    v.wait_ge(fifth, g + 1)
                    v.tensor_tensor(lk[:, b], z[b][:, :, :], part[:, b], ALU.max).then_inc(leaky, 1)
                    v.wait_ge(leaky, g + 1)
                    v.tensor_tensor(lk[:, b], lk[:, b], bc(k["par"][:, ATT, :], [P, G, D], 1), ALU.mult).then_inc(weighed, 1)
                    v.wait_ge(weighed, g + 1)
                    v.tensor_reduce(k["alpha"][:, bass.ds((i * 2 + h) * U + b * G, G), :],
                                    lk[:, b].rearrange("p g (h c) -> p g h c", h=H), AX.X, ALU.add).then_inc(scored[h][b], 1)

            def body(i, last):
                extract(i, 1)
                score(i, 0)
                if not last:
                    extract(i + 1, 0)
                score(i, 1)

            extract(0, 0)
            loop(v, body)

        @block.gpsimd
        def _(pool):
            with pool.Fori(0, n) as i:
                for h in range(2):
                    pool.wait_ge(cols[h], i + 1)
                    pool.wait_ge(scored[h][1], i)
                    hold(pool)
                    for e, table in enumerate(("left", "right")):
                        for u in range(U):
                            pool.indirect_dma_start(
                                out=rows[:, h, e, u, :], out_offset=None, in_=d[table][:, :],
                                in_offset=bass.IndirectOffsetOnAxis(ap=ends[:, h, e, u:u + 1], axis=0)
                            ).then_inc(gathered[h], 16)

        @block.tensor
        def _(pe):
            with pe.Fori(0, n) as i:
                for h in range(2):
                    pe.wait_ge(loaded[h], (i + 1) * 16)
                    for b in range(2):
                        pe.wait_ge(scored[1 - h][b], i + h)
                        hold(pe)
                        for u in range(G):
                            m = pe.transpose(tp[b][0:DE + 1, u, :], rec[:, h, b * G + u, 0:DE + 1], k["ident"][:, :])
                        m.then_inc(turned, 1)
                    for b in range(2):
                        g = (i * 2 + h) * 2 + b
                        pe.wait_ge(gathered[h], (i + 1) * (2 * U * 16))
                        pe.matmul(z[b][:, :, :], k["ident"][:, :], rows[:, h, 0, b * G:b * G + G, :],
                                  start=True, stop=False)
                        pe.wait_ge(turned_out, g + 1)
                        for u in range(G):
                            pe.matmul(z[b][:, u, :], at_sb[:, b, u, :], k["wedge"][:, :], start=False,
                                      stop=False, skip_group_check=True)
                        pe.matmul(z[b][:, :, :], k["ident"][:, :], rows[:, h, 1, b * G:b * G + G, :],
                                  start=False, stop=True).then_inc(summed, 1)

        @block.scalar
        def _(act):
            with act.Fori(0, n) as i:
                for h in range(2):
                    for b in range(2):
                        g = (i * 2 + h) * 2 + b
                        act.wait_ge(turned, g + 1)
                        act.wait_ge(scored[1 - h][b], i + h)
                        act.copy(at_sb[:, b], tp[b][0:DE + 1]).then_inc(turned_out, 1)
                    for b in range(2):
                        act.wait_ge(summed, (i * 2 + h) * 2 + b + 1)
                        act.mul(part[:, b], z[b][:, :, :], 0.2).then_inc(fifth, 1)


def softmax_phase(nc, d, k):
    with Space(nc, "softmax") as s:
        val, dst, run, back = (s.sb(x, [P, CT, P]) for x in ("val", "dst", "run", "back"))
        shut = s.sb("shut", [P, CL + 1])
        pack = s.sb("pack", [P, 2, CT, P])
        packed = s.sem("packed")
        one = s.sb("one", [1, 1])
        edge = s.sb("edge", [P, 4])
        lv, lk, lr, lf, lb = (s.sb(x, [1, 2 * P + 1]) for x in ("lv", "lk", "lr", "lf", "lb"))
        full = s.sb("full", [P, 2])
        tp = [s.ps(f"tp{b}", [P, 4, P]) for b in range(4)]
        line = s.ps("line", [1, 4, P])
        fullp = s.ps("fullp", [P, 512])
        turned, out = s.sem("turned"), s.sem("out")
        step = s.sem("step")
        lined, fulled = s.sem("lined"), s.sem("fulled")
        expd = s.sem("expd")
        turned2, out2 = s.sem("turned2"), s.sem("out2")
        block = s.block()
        n4 = -(-CT // 4)
        vf, df, rf, bf = (x[:, :, :].rearrange("p t e -> p (t e)") for x in (val, dst, run, back))

        @block.tensor
        def _(pe):
            pe.wait_ge(packed, 2)
            for q in range(2 * n4):
                if q >= 4:
                    pe.wait_ge(out, q - 3)
                for j in range(4 * (q // 2), min(CT, 4 * (q // 2) + 4)):
                    m = pe.transpose(tp[q % 4][:, j % 4, :], pack[:, q % 2, j, :], k["ident"][:, :])
                m.then_inc(turned, 1)
            pe.wait_ge(step, 5)
            for c in range(4):
                m = pe.transpose(line[:, c, :], edge[:, c:c + 1], k["ident"][:, :])
            m.then_inc(lined, 1)
            pe.wait_ge(step, 11)
            for c in range(2):
                m = pe.transpose(fullp[:, c:c + 1], lf[:, c * P:(c + 1) * P], one[:, :])
            m.then_inc(fulled, 1)
            for q in range(n4):
                pe.wait_ge(expd, q + 1)
                if q >= 4:
                    pe.wait_ge(out2, q - 3)
                for j in range(4 * q, min(CT, 4 * q + 4)):
                    m = pe.transpose(tp[q % 4][:, j % 4, :], val[:, j, :], k["ident"][:, :])
                m.then_inc(turned2, 1)

        @block.scalar
        def _(act):
            for q in range(2 * n4):
                a, b = 4 * (q // 2), min(CT, 4 * (q // 2) + 4)
                act.wait_ge(turned, q + 1)
                act.copy((val, dst)[q % 2][:, a:b, :], tp[q % 4][:, 0:b - a, :]).then_inc(out, 1)
            act.wait_ge(step, 17)
            for q in range(n4):
                a, b = 4 * q, min(CT, 4 * q + 4)
                act.activation(val[:, a:b, :], val[:, a:b, :], ACT.Exp).then_inc(expd, 1)

        @block.vector
        def _(v):
            v.tensor_copy(pack[:, 0].rearrange("p j (c h) -> p j c h", h=H),
                          k["alpha"][:, :, :].rearrange("p (c j) h -> p j c h", c=CH)).then_inc(packed, 1)
            v.tensor_copy(pack[:, 1].rearrange("p j (c h) -> p j c h", h=H),
                          k["dst"][:, :].rearrange("p (c j) -> p j c", c=CH).unsqueeze(3).to_broadcast([P, CT, CH, H])
                          ).then_inc(packed, 1)
            v.memset(one[:, :], 1.0)
            v.memset(shut[:, 0:1], 0.0)
            v.memset(shut[:, CL:CL + 1], 0.0)
            v.memset(lr[:, 0:1], 0.0)
            v.memset(lr[:, 2 * P:2 * P + 1], 0.0)
            v.wait_ge(out, 2 * n4)
            v.tensor_tensor(rf[:, 1:CL], df[:, 1:CL], df[:, 0:CL - 1], ALU.not_equal).then_inc(step, 1)
            v.wait_ge(step, 1)
            v.tensor_scalar(shut[:, 1:CL], rf[:, 1:CL], -FAR, None, ALU.mult).then_inc(step, 1)
            v.wait_ge(step, 2)
            v.tensor_tensor_scan(rf[:, :], shut[:, 0:CL], vf[:, :], -FAR, ALU.add, ALU.max).then_inc(step, 1)
            v.wait_ge(step, 3)
            v.tensor_tensor_scan(bf[:, ::-1], shut[:, 1:CL + 1][:, ::-1], rf[:, ::-1], -FAR, ALU.add, ALU.max).then_inc(step, 1)
            v.wait_ge(step, 4)
            for c, x in enumerate((bf[:, 0:1], bf[:, CL - 1:CL], df[:, 0:1], df[:, CL - 1:CL])):
                w = v.tensor_copy(edge[:, c:c + 1], x)
            w.then_inc(step, 1)
            v.wait_ge(lined, 1)
            for to, c in ((lv, 0), (lk, 2)):
                for e in range(2):
                    w = v.tensor_copy(to[:, e:2 * P:2].rearrange("o (h c) -> o h c", h=H),
                                      line[:, c + e, :].rearrange("o (c h) -> o h c", h=H))
            w.then_inc(step, 1)
            v.wait_ge(step, 6)
            v.tensor_tensor(lf[:, 1:2 * P], lk[:, 1:2 * P], lk[:, 0:2 * P - 1], ALU.not_equal).then_inc(step, 1)
            v.wait_ge(step, 7)
            v.tensor_scalar(lr[:, 1:2 * P], lf[:, 1:2 * P], -FAR, None, ALU.mult).then_inc(step, 1)
            v.wait_ge(step, 8)
            v.tensor_tensor_scan(lf[:, 0:2 * P], lr[:, 0:2 * P], lv[:, 0:2 * P], -FAR, ALU.add, ALU.max).then_inc(step, 1)
            v.wait_ge(step, 9)
            v.tensor_tensor_scan(lb[:, 0:2 * P][:, ::-1], lr[:, 1:2 * P + 1][:, ::-1], lf[:, 0:2 * P][:, ::-1], -FAR,
                                 ALU.add, ALU.max).then_inc(step, 1)
            v.wait_ge(step, 10)
            for e in range(2):
                w = v.tensor_copy(lf[:, e * P:(e + 1) * P].rearrange("o (c h) -> o h c", h=H),
                                  lb[:, e:2 * P:2].rearrange("o (h c) -> o h c", h=H))
            w.then_inc(step, 1)
            v.wait_ge(fulled, 1)
            v.tensor_copy(full[:, :], fullp[:, 0:2]).then_inc(step, 1)
            for e in range(2):
                v.wait_ge(step, 12 + 2 * e)
                v.tensor_scalar(rf[:, :], df[:, :], edge[:, 2 + e:3 + e], -FAR, ALU.not_equal, ALU.mult).then_inc(step, 1)
                v.wait_ge(step, 13 + 2 * e)
                v.scalar_tensor_tensor(bf[:, :], rf[:, :], full[:, e:e + 1], bf[:, :], ALU.add, ALU.max).then_inc(step, 1)
            v.wait_ge(step, 16)
            v.tensor_tensor(vf[:, :], vf[:, :], bf[:, :], ALU.subtract).then_inc(step, 1)
            for q in range(n4):
                v.wait_ge(turned2, q + 1)
                for j in range(4 * q, min(CT, 4 * q + 4)):
                    w = v.tensor_copy(k["alpha"][:, j::CT, :], tp[q % 4][:, j % 4, :].rearrange("p (c h) -> p c h", h=H))
                w.then_inc(out2, 1)
            for c, f in enumerate(("idx2", "w2", "dst2")):
                w = v.tensor_copy(k[f][:, :], k["rec2"][:, :, c])
            w.then_inc(step, 1)
            v.wait_ge(step, 18)
            for key, dst_ in (("key", "dst"), ("key2", "dst2")):
                v.memset(k[key][:, 0:1], -1.0)
                w = v.tensor_scalar(k[key][:, 1:T], k[dst_][:, 0:T - 1], 1.0, k["last"][:, 0:1], ALU.add, ALU.mult)
            w.then_inc(step, 1)
            v.wait_ge(step, 19)
            for key in ("key", "key2"):
                v.tensor_scalar(k[key][:, 1:T], k[key][:, 1:T], -1.0, None, ALU.add)


def run_sum_phase(nc, d, k, name, table, index, width, weight=None, sums="sums", node="dst", keys="key"):
    gat = weight is None
    with Space(nc, name) as s:
        W = width
        idx = s.sb("idx", [P, 2, U], I32)
        dcol, key, wcol = s.sb("dcol", [P, 2, U]), s.sb("key", [P, 2, U]), s.sb("wcol", [P, 2, U])
        rows = s.sb("rows", [P, 2, U, D if gat else W])
        msg = s.sb("msg", [P, 2, G, W]) if gat else None
        same, open_ = s.sb("same", [P, 2, G, P]), s.sb("open", [P, 2, G, P])
        res = s.sb("res", [P, 2, U, W])
        rowb = [s.ps(f"rowb{b}", [P, G, P]) for b in range(2)]
        acc = [s.ps(f"acc{a}", [P, 512]) for a in range(4)]
        init = s.sem("init")
        cols = [s.sem(f"cols{h}") for h in range(2)]
        gathered = [s.sem(f"gathered{h}") for h in range(2)]
        spread = [s.sem(f"spread{b}") for b in range(2)]
        masks = [s.sem(f"masks{b}") for b in range(2)]
        scaled = [s.sem(f"scaled{b}") for b in range(2)]
        summed = [[s.sem(f"summed{h}{b}") for b in range(2)] for h in range(2)]
        out = s.sem("out")
        stored = [s.sem(f"stored{h}") for h in range(2)]
        block = s.block()
        n = T // (2 * U)

        @block.vector
        def _(v):
            def columns(i, h):
                at = bass.ds(i * (2 * U) + h * U, U)
                v.tensor_copy(idx[:, h, :], k[index][:, at])
                v.tensor_copy(dcol[:, h, :], k[node][:, at])
                if not gat:
                    v.tensor_copy(wcol[:, h, :], k[weight][:, at])
                v.tensor_copy(key[:, h, :], k[keys][:, at]).then_inc(cols[h], 1)

            def group(i, h, b):
                v.wait_ge(spread[b], i * 2 + h + 1)
                v.wait_ge(summed[1 - h][b], (i + h) * G)
                for u in range(G):
                    j = b * G + u
                    if gat:
                        v.tensor_scalar(same[:, b, u, :], rowb[b][:, u, :], dcol[:, h, j:j + 1], None, ALU.is_equal)
                    else:
                        v.tensor_scalar(same[:, b, u, :], rowb[b][:, u, :], dcol[:, h, j:j + 1], wcol[:, h, j:j + 1],
                                        ALU.is_equal, ALU.mult)
                    w = v.tensor_scalar(open_[:, b, u, :], rowb[b][:, u, :], key[:, h, j:j + 1], None, ALU.is_equal)
                w.then_inc(masks[b], 1)
                if gat:
                    if b == 0:
                        v.wait_ge(gathered[h], (i + 1) * (16 * U))
                    at = bass.ds((i * 2 + h) * U + b * G, G)
                    v.tensor_copy(msg[:, b, :, D:D + H], k["alpha"][:, at, :])
                    v.tensor_tensor(msg[:, b, :, 0:D].rearrange("p g (h c) -> p g h c", h=H),
                                    rows[:, h, b * G:b * G + G, :].rearrange("p g (h c) -> p g h c", h=H),
                                    k["alpha"][:, at, :].unsqueeze(3).to_broadcast([P, G, H, C]), ALU.mult
                                    ).then_inc(scaled[b], 1)

            def body(i, last):
                for h in range(2):
                    group(i, h, 0)
                    v.wait_ge(masks[1], i * 2 + h)
                    if h == 0:
                        columns(i, 1)
                    elif not last:
                        columns(i + 1, 0)
                    group(i, h, 1)

            if W > D and not gat:
                v.memset(rows[:, :, :, D:W], 1.0)
            v.memset(res[:, 1, U - 1, :], 0.0).then_inc(init, 1)
            columns(0, 0)
            with v.Fori(0, n - 1) as i:
                body(i, False)
            body(n - 1, True)

        @block.gpsimd
        def _(pool):
            with pool.Fori(0, n) as i:
                for h in range(2):
                    pool.wait_ge(cols[h], i + 1)
                    pool.wait_ge(summed[h][1], i * G)
                    hold(pool)
                    for u in range(U):
                        pool.indirect_dma_start(
                            out=rows[:, h, u, 0:D], out_offset=None, in_=d[table][:, :],
                            in_offset=bass.IndirectOffsetOnAxis(ap=idx[:, h, u:u + 1], axis=0)).then_inc(gathered[h], 16)

        @block.tensor
        def _(pe):
            pe.wait_ge(init, 1)
            with pe.Fori(0, n) as i:
                for h in range(2):
                    pe.wait_ge(cols[h], i + 1)
                    for b in range(2):
                        pe.wait_ge(masks[b], i * 2 + h)
                        for u in range(G):
                            m = pe.matmul(rowb[b][:, u, :], dcol[:, h, b * G + u:b * G + u + 1].to_broadcast([P, P]),
                                          k["ident"][:, :], start=True, stop=True)
                        m.then_inc(spread[b], 1)
                    for b in range(2):
                        pe.wait_ge(masks[b], i * 2 + h + 1)
                        if gat:
                            pe.wait_ge(scaled[b], i * 2 + h + 1)
                        elif b == 0:
                            pe.wait_ge(gathered[h], (i + 1) * (16 * U))
                        for u in range(G):
                            j = b * G + u
                            what = msg[:, b, u, :] if gat else rows[:, h, j, :]
                            before = res[:, h, j - 1, :] if j else res[:, 1 - h, U - 1, :]
                            pe.matmul(acc[u][:, 0:W], same[:, b, u, :], what, start=True, stop=False)
                            pe.wait_ge(out, (i * 2 + h) * U + j)
                            m = pe.matmul(acc[u][:, 0:W], open_[:, b, u, :], before, start=False, stop=True)
                            m.then_inc(summed[h][b], 1)

        @block.scalar
        def _(act):
            with act.Fori(0, n) as i:
                for h in range(2):
                    act.wait_ge(stored[h], i * 16)
                    for j in range(U):
                        act.wait_ge(summed[h][j // G], i * G + j % G + 1)
                        act.copy(res[:, h, j, :], acc[j % G][:, 0:W]).then_inc(out, 1)

        @block.sync
        def _(sp):
            with sp.Fori(0, n) as i:
                for h in range(2):
                    sp.wait_ge(out, (i * 2 + h + 1) * U)
                    sp.dma_start(d[sums].rearrange("(t p) w -> p t w", p=P)[:, bass.ds(i * (2 * U) + h * U, U), 0:W],
                                 res[:, h]).then_inc(stored[h], 16)
            for h in range(2):
                sp.wait_ge(stored[h], n * 16)


def node_phase(nc, d, k, layer, width, sums="sums", table=None):
    with Space(nc, f"nodes{layer}") as s:
        NN = NT // NB
        agg = s.sb("agg", [P, NT, width])
        a, at, y, xs = (s.sb(x, [P, NB, D]) for x in ("a", "at", "y", "xs"))
        hs, ht, tab = (s.sb(x, [P, NB, D]) for x in ("hs", "ht", "tab"))
        nrm = s.sb("nrm", [P, NB, H])
        tp = s.ps("tp", [P, 8, D])
        mm = s.ps("mm", [P, 8, D])
        tp2 = s.ps("tp2", [P, 8, D]) if layer == 2 else None
        mm2 = s.ps("mm2", [P, 8, D]) if layer == 2 else None
        cols = s.sb("cols", [P, 4, NT])
        w = s.sb("w", [P, 2 * D + 2 * D])
        b1 = s.sb("b1", [P, 2])
        ff = s.sb("ff", [P, 2, NB, D])
        fp = s.ps("fp", [P, 12, D]) if layer == 0 else None
        q1, q2 = norm_tensors(s, "n1"), norm_tensors(s, "n2")
        gathered = s.sem("gathered")
        loaded = s.sem("loaded")
        names = ("rooted", "degree", "taken", "den", "inv", "divided", "mixed", "ready", "turned", "turned_out", "product",
                 "y1", "y2", "y3", "got_x", "scaled", "affine", "ff1", "gelu", "kept", "kept_h", "relued", "tabled", "fresh")
        e = {x: s.sem(x) for x in names}
        stored = s.sem("stored")
        block = s.block()
        par = k["par"]
        normed_next = layer in (0, 1, 2)

        def row(j):
            return bc(par[:, j, :], [P, NB, D], 1)

        def col(c, i):
            return cols[:, c, bass.ds(i * NB, NB)].unsqueeze(2).to_broadcast([P, NB, D])

        DST_ROOT, SRC_ROOT = 0, 1

        @block.gpsimd
        def _(pool):
            for t in range(NT):
                pool.indirect_dma_start(out=agg[:, t, :], out_offset=None, in_=d[sums][:, :],
                                        in_offset=bass.IndirectOffsetOnAxis(ap=k["lastpos"][:, int(layer == 2), t:t + 1], axis=0)
                                        ).then_inc(gathered, 16)
            pool.wait_ge(gathered, 16 * NT)

        @block.sync
        def _(sp):
            if layer == 0:
                sp.dma_start(w[:, 0:2 * D], d["w1"]).then_inc(loaded, 16)
                sp.dma_start(w[:, 2 * D:4 * D].rearrange("p (f w) -> p f w", f=2),
                             d["w2"].rearrange("(f p) w -> p f w", p=P)).then_inc(loaded, 16)
                sp.dma_start(b1[:, :], d["b1"]).then_inc(loaded, 16)
            else:
                sp.dma_start(w[:, 0:D], d["square"][SQUARE[layer]]).then_inc(loaded, 16)
                if layer == 2:
                    sp.dma_start(w[:, D:2 * D], d["square"][SQUARE[layer] + 1]).then_inc(loaded, 16)
            if table or layer == 4:
                with sp.Fori(0, NN) as i:
                    sp.wait_ge(e["tabled"], i + 1)
                    sp.dma_start(rows_of(d[table] if table else d["out"], i), tab[:, :, :]).then_inc(stored, 16)
                sp.wait_ge(stored, 16 * NN)

        LOADS = 48 if layer == 0 else 32 if layer == 2 else 16

        @block.vector
        def _(v):
            for c, deg in enumerate(("deg_dst", "deg_src")):
                m = v.tensor_scalar(cols[:, 2 + c, :], k[deg][:, :], 1.0, None, ALU.max)
            m.then_inc(e["degree"], 1)
            v.wait_ge(e["rooted"], 1)
            v.reciprocal(cols[:, 0:2, :], cols[:, 2:4, :]).then_inc(e["degree"], 1)
            v.wait_ge(e["degree"], 2)
            v.wait_ge(gathered, 16 * NT)
            v.wait_ge(loaded, LOADS)
            with v.Fori(0, NN) as i:
                at_i = bass.ds(i * NB, NB)
                if layer == 4:
                    v.wait_ge(e["tabled"], i)
                v.tensor_copy(xs[:, :, :], k["x"][:, at_i, :])
                v.tensor_copy(hs[:, :, :], k["h"][:, at_i, :]).then_inc(e["taken"], 1)
                v.wait_ge(e["taken"], i + 1)
                if layer == 0:
                    v.tensor_scalar(nrm[:, :, :], agg[:, at_i, D:D + H], 1e-16, None, ALU.add).then_inc(e["den"], 1)
                    v.wait_ge(e["den"], i + 1)
                    v.reciprocal(nrm[:, :, :], nrm[:, :, :]).then_inc(e["inv"], 1)
                    v.wait_ge(e["inv"], i + 1)
                    v.tensor_tensor(a[:, :, :].rearrange("p a (h c) -> p a h c", h=H),
                                    agg[:, at_i, 0:D].rearrange("p a (h c) -> p a h c", h=H),
                                    nrm[:, :, :].unsqueeze(3).to_broadcast([P, NB, H, C]), ALU.mult).then_inc(e["divided"], 1)
                    v.wait_ge(e["divided"], i + 1)
                    v.tensor_tensor(a[:, :, :], a[:, :, :], row(BIAS), ALU.add).then_inc(e["mixed"], 1)
                    v.wait_ge(e["mixed"], i + 1)
                    v.tensor_tensor(hs[:, :, :], hs[:, :, :], a[:, :, :], ALU.add).then_inc(e["fresh"], 1)
                    v.wait_ge(e["fresh"], i + 1)
                    norm_vector(v, q1, i, hs, a)
                    v.wait_ge(q1["normed"], i + 1)
                    v.tensor_tensor(a[:, :, :], a[:, :, :], row(LN2_G), ALU.mult).then_inc(e["scaled"], 1)
                    v.wait_ge(e["scaled"], i + 1)
                    v.tensor_tensor(a[:, :, :], a[:, :, :], row(LN2_B), ALU.add).then_inc(e["ready"], 1)
                elif layer == 1:
                    v.tensor_tensor(a[:, :, :], agg[:, at_i, 0:D], col(DST_ROOT, i), ALU.mult).then_inc(e["ready"], 1)
                else:
                    v.tensor_copy(a[:, :, :], agg[:, at_i, 0:D]).then_inc(e["ready"], 1)
                if layer == 2:
                    v.reciprocal(nrm[:, :, 0:1], agg[:, at_i, D:D + 1]).then_inc(e["inv"], 1)
                v.wait_ge(e["product"], i + 1)
                if layer == 0:
                    v.tensor_tensor(y[:, :, :], mm[:, 0:NB, :], hs[:, :, :], ALU.add).then_inc(e["y1"], 1)
                    v.wait_ge(e["y1"], i + 1)
                    v.tensor_tensor(y[:, :, :], y[:, :, :], row(L0_B2), ALU.add).then_inc(e["y2"], 1)
                    v.wait_ge(e["y2"], i + 1)
                    v.tensor_tensor(xs[:, :, :], xs[:, :, :], y[:, :, :], ALU.add).then_inc(e["got_x"], 1)
                elif layer == 1:
                    v.tensor_tensor(y[:, :, :], mm[:, 0:NB, :], a[:, :, :], ALU.add).then_inc(e["y1"], 1)
                    v.wait_ge(e["y1"], i + 1)
                    v.scalar_tensor_tensor(xs[:, :, :], y[:, :, :], 0.0, xs[:, :, :], ALU.max, ALU.add).then_inc(e["got_x"], 1)
                elif layer == 2:
                    v.tensor_tensor(y[:, :, :], mm[:, 0:NB, :], row(L2_B2), ALU.add).then_inc(e["y1"], 1)
                    v.wait_ge(e["y1"], i + 1)
                    v.wait_ge(e["inv"], i + 1)
                    v.tensor_tensor(y[:, :, :], y[:, :, :], nrm[:, :, 0:1].to_broadcast([P, NB, D]), ALU.mult)
                    v.tensor_tensor(a[:, :, :], mm2[:, 0:NB, :], row(L2_B1), ALU.add).then_inc(e["y2"], 1)
                    v.wait_ge(e["y2"], i + 1)
                    v.tensor_tensor(y[:, :, :], y[:, :, :], a[:, :, :], ALU.add).then_inc(e["y3"], 1)
                    v.wait_ge(e["y3"], i + 1)
                    v.tensor_tensor(xs[:, :, :], xs[:, :, :], y[:, :, :], ALU.add).then_inc(e["got_x"], 1)
                else:
                    v.tensor_tensor(y[:, :, :], mm[:, 0:NB, :], col(DST_ROOT, i), ALU.mult).then_inc(e["y1"], 1)
                    v.wait_ge(e["y1"], i + 1)
                    v.tensor_tensor(y[:, :, :], y[:, :, :], row(L3_B1 if layer == 3 else L3_B2), ALU.add).then_inc(e["y2"], 1)
                    v.wait_ge(e["y2"], i + 1)
                    v.wait_ge(stored, i * 16)
                    if layer == 3:
                        v.tensor_scalar(y[:, :, :], y[:, :, :], 0.0, None, ALU.max).then_inc(e["y3"], 1)
                        v.wait_ge(e["y3"], i + 1)
                        v.tensor_tensor(tab[:, :, :], y[:, :, :], col(SRC_ROOT, i), ALU.mult).then_inc(e["tabled"], 1)
                    else:
                        v.scalar_tensor_tensor(tab[:, :, :], y[:, :, :], 0.0, xs[:, :, :], ALU.max, ALU.add
                                               ).then_inc(e["tabled"], 1)
                if normed_next:
                    v.wait_ge(e["got_x"], i + 1)
                    norm_vector(v, q2, i, xs, y)
                    v.wait_ge(e["kept"], i + 1)
                    v.wait_ge(e["relued"], i + 1)
                    if table:
                        v.wait_ge(stored, i * 16)
                        if layer == 2:
                            v.tensor_tensor(tab[:, :, :], y[:, :, :], col(SRC_ROOT, i), ALU.mult).then_inc(e["tabled"], 1)
                        else:
                            v.tensor_copy(tab[:, :, :], y[:, :, :]).then_inc(e["tabled"], 1)
                    v.wait_ge(e["kept_h"], i + 1)

        @block.scalar
        def _(act):
            act.wait_ge(e["degree"], 1)
            act.activation(cols[:, 2:4, :], cols[:, 2:4, :], ACT.Sqrt).then_inc(e["rooted"], 1)
            with act.Fori(0, NN) as i:
                at_i = bass.ds(i * NB, NB)
                if layer == 0:
                    norm_scalar(act, q1, i, k)
                act.wait_ge(e["turned"], i + 1)
                if layer == 2:
                    act.copy(ht[:, :, :], tp2[:, 0:NB, :])
                act.copy(at[:, :, :], tp[:, 0:NB, :]).then_inc(e["turned_out"], 1)
                if layer == 0:
                    act.wait_ge(e["ff1"], i + 1)
                    for f in range(2):
                        m = act.activation(ff[:, f, :, :], fp[:, f * 6:f * 6 + NB, :], ACT.Gelu, bias=b1[:, f:f + 1])
                    m.then_inc(e["gelu"], 1)
                if normed_next:
                    act.wait_ge(e["got_x"], i + 1)
                    act.copy(k["x"][:, at_i, :], xs[:, :, :]).then_inc(e["kept"], 1)
                    norm_scalar(act, q2, i, k)
                    act.wait_ge(q2["normed"], i + 1)
                    act.activation(y[:, :, :], y[:, :, :], ACT.Relu).then_inc(e["relued"], 1)
                    act.wait_ge(e["relued"], i + 1)
                    act.copy(k["h"][:, at_i, :], y[:, :, :]).then_inc(e["kept_h"], 1)

        @block.tensor
        def _(pe):
            pe.wait_ge(loaded, LOADS)
            with pe.Fori(0, NN) as i:
                pe.wait_ge(e["ready"], i + 1)
                if layer == 2:
                    for u in range(NB):
                        pe.transpose(tp2[:, u, :], hs[:, u, :], k["ident"][:, :])
                for u in range(NB):
                    m = pe.transpose(tp[:, u, :], a[:, u, :], k["ident"][:, :])
                m.then_inc(e["turned"], 1)
                pe.wait_ge(e["turned_out"], i + 1)
                if layer == 0:
                    for f in range(2):
                        for u in range(NB):
                            m = pe.matmul(fp[:, f * 6 + u, :], w[:, f * D:(f + 1) * D], at[:, u, :], start=True, stop=True)
                    m.then_inc(e["ff1"], 1)
                    pe.wait_ge(e["gelu"], i + 1)
                    for u in range(NB):
                        for f in range(2):
                            m = pe.matmul(mm[:, u, :], ff[:, f, u, :], w[:, (2 + f) * D:(3 + f) * D],
                                          start=(f == 0), stop=(f == 1))
                else:
                    if layer == 2:
                        for u in range(NB):
                            pe.matmul(mm2[:, u, :], ht[:, u, :], w[:, D:2 * D], start=True, stop=True)
                    for u in range(NB):
                        m = pe.matmul(mm[:, u, :], at[:, u, :], w[:, 0:D], start=True, stop=True)
                m.then_inc(e["product"], 1)


def relation_phase(nc, d, k):
    GR = 4
    HR = R // 2
    with Space(nc, "relation") as s:
        wr = s.sb("wr", [P, R, D])
        feat = s.sb("feat", [P, R, D])
        hs, ht = s.sb("hs", [P, D]), s.sb("ht", [P, D])
        out = s.sb("out", [P, 2, HR, D])
        tp = s.ps("tp", [P, 512])
        mm = [s.ps(f"mm{b}", [P, GR, D]) for b in range(HR // GR)]
        loaded = s.sem("loaded")
        taken, turned, turned_out = s.sem("taken"), s.sem("turned"), s.sem("turned_out")
        product = s.sem("product")
        made = [s.sem(f"made{b}") for b in range(HR // GR)]
        stored = [s.sem(f"stored{h}") for h in range(2)]
        block = s.block()
        K = R // GR
        HK = K // 2

        @block.sync
        def _(sp):
            sp.dma_start(wr[:, :, :], d["wr"].rearrange("r p w -> p r w")).then_inc(loaded, 16)
            sp.dma_start(feat[:, :, :], d["feat"].rearrange("(o a) w -> o a w", o=1).to_broadcast([P, R, D])
                         ).then_inc(loaded, 16)
            table = d["relation"].rearrange("(t l r) w -> l t (r w)", l=P, r=R)
            with sp.Fori(0, NT) as i:
                for h in range(2):
                    for b in range(HK):
                        sp.wait_ge(made[b], i * 2 + h + 1)
                    sp.dma_start(table[:, bass.ds(i, 1), h * HR * D:(h + 1) * HR * D],
                                 out[:, h:h + 1].rearrange("p o r w -> p o (r w)")).then_inc(stored[h], 16)
            for h in range(2):
                sp.wait_ge(stored[h], NT * 16)

        @block.scalar
        def _(act):
            with act.Fori(0, NT) as i:
                act.copy(hs[:, :].rearrange("p (o w) -> p o w", o=1), k["h"][:, bass.ds(i, 1), :]).then_inc(taken, 1)
                act.wait_ge(turned, i + 1)
                act.wait_ge(product, i * K)
                act.copy(ht[:, :], tp[:, 0:D]).then_inc(turned_out, 1)

        @block.tensor
        def _(pe):
            pe.wait_ge(loaded, 32)
            with pe.Fori(0, NT) as i:
                pe.wait_ge(taken, i + 1)
                pe.transpose(tp[:, 0:D], hs[:, :], k["ident"][:, :]).then_inc(turned, 1)
                pe.wait_ge(turned_out, i + 1)
                for g in range(K):
                    pe.wait_ge(made[g % HK], i * 2 + g // HK)
                    pe.matmul(mm[g % HK][:, :, :], ht[:, :], wr[:, g * GR:(g + 1) * GR, :], start=True, stop=True
                              ).then_inc(product, 1)

        @block.vector
        def _(v):
            v.wait_ge(loaded, 32)
            with v.Fori(0, NT) as i:
                for g in range(K):
                    h = g // HK
                    if g % HK == 0:
                        v.wait_ge(stored[h], i * 16)
                    v.wait_ge(product, i * K + g + 1)
                    v.tensor_tensor(out[:, h, (g % HK) * GR:(g % HK + 1) * GR, :], mm[g % HK][:, :, :],
                                    feat[:, g * GR:(g + 1) * GR, :], ALU.add).then_inc(made[g % HK], 1)


SQUARE = {1: 0, 2: 1, 3: 3, 4: 4}


def gnn_kernel(nc, d):
    with Space(nc, "kept") as s:
        k = {}
        for name in ("meta",):
            k[name] = s.sb(name, [P, 5, T])
        for name in ("ident", "before", "iota"):
            k[name] = s.sb(name, [P, P])
        k["identb"] = s.sb("identb", [P, P], BF16)
        for name in ("dlo", "dhi", "slo", "shi", "dst", "dst2", "w2", "real", "key", "key2"):
            k[name] = s.sb(name, [P, T])
        for name in ("src", "relsrc", "idx2"):
            k[name] = s.sb(name, [P, T], I32)
        k["rec2"] = s.sb("rec2", [P, T, RW2])
        for name in ("deg_dst", "deg_src"):
            k[name] = s.sb(name, [P, NT])
        k["base"], k["lastpos"] = s.sb("base", [P, 2, NT]), s.sb("lastpos", [P, 2, NT], I32)
        k["last"], k["eps"] = s.sb("last", [P, 1]), s.sb("eps", [P, 1])
        k["mean"] = s.sb("mean", [DE, 1])
        k["wedge"] = s.sb("wedge", [DE + 1, D])
        k["x"], k["h"] = s.sb("x", [P, NT, D]), s.sb("h", [P, NT, D])
        k["par"] = s.sb("par", [P, PARS, D])
        k["alpha"] = s.sb("alpha", [P, T, H])
        count_phase(nc, d, k)
        sort_phase(nc, d, k, 0)
        sort_phase(nc, d, k, 1)
        enter_phase(nc, d, k)
        score_phase(nc, d, k)
        softmax_phase(nc, d, k)
        run_sum_phase(nc, d, k, "gat", "left", "src", D + H, sums="sums_gat")
        node_phase(nc, d, k, 0, D + H, sums="sums_gat")
        relation_phase(nc, d, k)
        run_sum_phase(nc, d, k, "rel", "relation", "relsrc", D, "real")
        node_phase(nc, d, k, 1, D, table="table")
        run_sum_phase(nc, d, k, "avg", "table", "idx2", D + 1, "w2", sums="sums_avg", node="dst2", keys="key2")
        node_phase(nc, d, k, 2, D + 1, sums="sums_avg", table="table2")
        run_sum_phase(nc, d, k, "conv1", "table2", "src", D, "real", sums="sums1")
        node_phase(nc, d, k, 3, D, sums="sums1", table="table3")
        run_sum_phase(nc, d, k, "conv2", "table3", "src", D, "real", sums="sums2")
        node_phase(nc, d, k, 4, D, sums="sums2")


def kernel(**inputs):
    import numpy as np
    import concourse.bacc as bacc
    from concourse.bass_utils import run_bass_kernel_spmd

    z = {n: np.asarray(a) for n, a in inputs.items()}
    loops, pad = np.arange(NP, dtype=np.int32), EP - E
    rest = pad + NP
    l0 = lambda n: z["L0_gnn_" + n]
    arrays = {
        "x": np.concatenate([z["x"], np.zeros((NP - N, D), np.float32)]),
        "src": np.concatenate([z["src"], np.full(pad, N, np.int32), loops]),
        "dst": np.concatenate([z["dst"], np.full(pad, N, np.int32), loops]),
        "type": np.concatenate([z["edge_type_40"], np.zeros(rest, np.int32)]),
        "weight": np.concatenate([z["edge_weight"], np.ones(pad, np.float32), np.zeros(N, np.float32),
                                  np.ones(NP - N, np.float32)]),
        "attr": np.concatenate([z["edge_attr_32"], np.zeros((rest, DE), np.float32)]),
        "wlr": np.concatenate([l0("W_l"), l0("W_r")], axis=1),
        "we": l0("W_e"),
        "w1": l0("W1"),
        "w2": l0("W2"),
        "b1": np.ascontiguousarray(l0("b1").reshape(2, D).T),
        "par": np.stack([l0("ln1_g"), l0("ln1_b"), l0("ln2_g"), l0("ln2_b"), l0("att").reshape(D), l0("bias"), l0("b2"),
                         z["L2_gnn_b1"], z["L2_gnn_b2"], z["L3_gnn_b1"], z["L3_gnn_b2"]]),
        "wr": z["L1_gnn_relation_weights"],
        "feat": z["L1_gnn_rFeatures"],
        "square": np.stack([z["L1_gnn_loop_weight"], z["L2_gnn_W2"].T, z["L2_gnn_W1"].T, z["L3_gnn_W1"], z["L3_gnn_W2"]]),
    }
    arrays = {f"in_{n}": np.ascontiguousarray(a) for n, a in arrays.items()}
    nc = bacc.Bacc("TRN2", target_bir_lowering=False, num_devices=1)
    d = {n[3:]: nc.dram_tensor(n, a.shape, mybir.dt.from_np(a.dtype), kind="ExternalInput").ap() for n, a in arrays.items()}
    for name, rows, width in (("records", TE, RW), ("records2", TE, RW2), ("left", NP, D), ("right", NP, D), ("relation", NP * R, D),
                              ("table", NP, D), ("table2", NP, D), ("table3", NP, D), ("sums_gat", TE, D + H), ("sums", TE, D),
                              ("sums_avg", TE, D + 1), ("sums1", TE, D), ("sums2", TE, D)):
        d[name] = nc.dram_tensor(name, (rows, width), F32, kind="Internal").ap()
    d["out"] = nc.dram_tensor("out_x", (NP, D), F32, kind="ExternalOutput").ap()
    gnn_kernel(nc, d)
    r = run_bass_kernel_spmd(nc, [arrays], core_ids=[0])
    return r.results[0]["out_x"][:N]
```

```python
from contextlib import ExitStack

import concourse.bass as bass
from concourse import mybir

F32 = mybir.dt.float32
BF16 = mybir.dt.bfloat16
I32 = mybir.dt.int32
ALU = mybir.AluOpType
ACT = mybir.ActivationFunctionType
AX = mybir.AxisListType

P = 128
D = 128
N = 3125
NT = -(-N // P)
NP = NT * P
E = 50000
ET = -(-E // P)
EP = ET * P
T = ET + NT
TE = T * P
LN1_G, LN1_B, LN2_G, LN2_B, ATT, BIAS, L0_B2, L2_B1, L2_B2, L3_B1, L3_B2 = range(11)
PARS = 11
H, C = 8, 16
DE = 32
R = 40
EPS = 1e-5
SLOPE = 0.2
RW = DE + 5
RW2 = 3
SELF, WEIGHT, SRC, TYPE, DST = range(5)
FAR = 1e30
G = 4
U = 2 * G
SLOTS = 4
NB = 5
CH = P // H
CT = T // CH
CL = CT * P
assert T == CH * CT and T % (2 * G) == 0 and T % (SLOTS * U) == 0 and NT % NB == 0


class Space:

    def __init__(self, nc, name):
        self.nc, self.name, self.ctx, self.sems = nc, name, ExitStack(), []
        self.blocks = ExitStack()

    def __enter__(self):
        return self

    def __exit__(self, *a):
        self.blocks.close()
        if self.sems:
            self.nc.clear_and_free_semaphores(self.sems)
            self.nc.all_engine_barrier()
        self.ctx.close()

    def sb(self, name, shape, dt=F32):
        return self.ctx.enter_context(self.nc.sbuf_tensor(f"{self.name}_{name}", shape, dt))

    def ps(self, name, shape, dt=F32):
        return self.ctx.enter_context(self.nc.psum_tensor(f"{self.name}_{name}", shape, dt))

    def sem(self, name):
        self.sems.append(self.nc.alloc_semaphore(f"{self.name}_{name}"))
        return self.sems[-1]

    def block(self):
        return self.blocks.enter_context(self.nc.Block())


def bc(ap, shape, axis):
    return ap.unsqueeze(axis).to_broadcast(shape)


def hold(eng):
    eng.nop(nofuse=True)


def past(eng, sem, value):
    if not isinstance(value, int) or value > 0:
        eng.wait_ge(sem, value)


def each(eng, n, body):
    body(0)
    with eng.Fori(1, n) as i:
        body(i)


def each_ahead(eng, n, body):
    body(0, False)
    with eng.Fori(1, n - 1) as i:
        body(i, False)
    body(n - 1, True)


def number(i, h, b=0):
    return (i * SLOTS + h) * 2 + b


def reused(i, h):
    return number(i - 1, h) + 2


def ring(i, last):
    for h in range(SLOTS):
        for b in range(2):
            over = None if last else (i + 1, 0, 0)
            yield ((i, h, b), (i, h, 1) if b == 0 else (i, h + 1, 0) if h + 1 < SLOTS else over,
                   None if b == 1 else (i, h + 2) if h + 2 < SLOTS else None if last else (i + 1, h + 2 - SLOTS))


def count_phase(nc, d, k):
    B = 16
    with Space(nc, "count") as s:
        diff_i, part_i, flat_i = s.sb("diff_i", [P, P], I32), s.sb("part_i", [P, 1], I32), s.sb("flat_i", [P, T], I32)
        diff = s.sb("diff", [P, P])
        part = s.sb("part", [P, 1])
        flat = s.sb("flat", [P, T])
        raw = s.sb("raw", [P, 3, T], I32)
        lohi_i = s.sb("lohi_i", [P, 4, T], I32)
        upper, ones = s.sb("upper", [P, P]), s.sb("ones", [P, P])
        zeros = s.sb("zeros", [P, P], BF16)
        oh = s.sb("oh", [P, 2, 2, B, P], BF16)
        ohh = s.sb("ohh", [P, 2, 2, B, NT], BF16)
        ohw = s.sb("ohw", [P, 2, B, 3, NT], BF16)
        wpart, wrest = s.sb("wpart", [P, T, 3], BF16), s.sb("wrest", [P, T, 2])
        hist_sb, parts_sb = s.sb("hist_sb", [P, 2, NT]), s.sb("parts_sb", [P, 3 * NT])
        tot_sb, run_sb = s.sb("tot_sb", [P, 2, NT]), s.sb("run_sb", [P, 2, NT])
        hist = [s.ps(f"hist{j}", [P, 512]) for j in range(2)]
        pre, tot = s.ps("pre", [P, 512]), s.ps("tot", [P, 512])
        loaded = s.sem("loaded")
        iotas = s.sem("iotas")
        split = s.sem("split")
        made = s.sem("made")
        onehots = [s.sem(f"onehots{h}") for h in range(2)]
        counted = [s.sem(f"counted{h}") for h in range(2)]
        total = s.sem("total")
        hist_out = s.sem("hist_out")
        prefix = s.sem("prefix")
        based = s.sem("based")
        consts = s.sem("consts")
        block = s.block()
        MADE = 16

        @block.sync
        def _(sp):
            for j, name in enumerate(("src", "type", "dst")):
                sp.dma_start(raw[:, j, :], d[name].rearrange("(p t) -> p t", p=P)).then_inc(loaded, 16)
            sp.dma_start(k["meta"][:, WEIGHT, :], d["weight"].rearrange("(p t) -> p t", p=P)).then_inc(loaded, 16)
            sp.wait_ge(loaded, 64)

        @block.gpsimd
        def _(pool):
            pool.iota(diff_i[:, :], pattern=[[1, P]], base=0, channel_multiplier=-1).then_inc(iotas, 1)
            pool.iota(part_i[:, :], pattern=[[1, 1]], base=0, channel_multiplier=1).then_inc(iotas, 1)
            pool.iota(flat_i[:, :], pattern=[[1, T]], base=0, channel_multiplier=T).then_inc(iotas, 1)

        @block.vector
        def _(v):
            v.memset(zeros[:, :], 0.0).then_inc(consts, 1)
            v.memset(ones[:, :], 1.0).then_inc(consts, 1)
            v.wait_ge(iotas, 3)
            v.tensor_copy(diff[:, :], diff_i[:, :]).then_inc(made, 1)
            v.tensor_copy(part[:, :], part_i[:, :])
            v.tensor_copy(k["part"][:, :], part_i[:, :]).then_inc(made, 1)
            v.tensor_copy(flat[:, :], flat_i[:, :]).then_inc(made, 1)
            v.wait_ge(loaded, 64)
            for j, f in enumerate((SRC, TYPE, DST)):
                v.tensor_copy(k["meta"][:, f, :], raw[:, j, :]).then_inc(made, 1)
            for j, f in ((0, 2), (2, 0)):
                v.tensor_scalar(lohi_i[:, j, :], raw[:, f, :], P - 1, None, ALU.bitwise_and).then_inc(made, 1)
                v.tensor_scalar(lohi_i[:, j + 1, :], raw[:, f, :], 7, None,
                                ALU.arith_shift_right).then_inc(made, 1)
            v.wait_ge(made, 10)
            v.tensor_scalar(k["ident"][:, :], diff[:, :], 0.0, None, ALU.is_equal).then_inc(made, 1)
            v.tensor_scalar(k["identb"][:, :], diff[:, :], 0.0, None, ALU.is_equal).then_inc(made, 1)
            v.tensor_scalar(k["before"][:, :], diff[:, :], 0.0, None, ALU.is_lt).then_inc(made, 1)
            v.tensor_scalar(upper[:, :], diff[:, :], 0.0, None, ALU.is_gt).then_inc(made, 1)
            v.tensor_scalar(k["iota"][:, :], diff[:, :], part[:, 0:1], None, ALU.add).then_inc(made, 1)
            v.wait_ge(made, 15)
            v.tensor_copy(k["iotab"][:, :], k["iota"][:, :]).then_inc(made, 1)
            v.tensor_scalar(k["meta"][:, SELF, :], flat[:, :], float(EP), None, ALU.is_ge)
            for j, to in enumerate((k["dlo"], k["dhi"], k["slo"], k["shi"])):
                w = v.tensor_copy(to[:, :], lohi_i[:, j, :])
            w.then_inc(made, 1)
            rest = k["meta"][:, WEIGHT, :]
            for c in range(3):
                v.tensor_copy(wpart[:, :, c], rest).then_inc(split, 1)
                v.wait_ge(split, 2 * c + 1)
                if c < 2:
                    v.tensor_tensor(wrest[:, :, c], rest, wpart[:, :, c], ALU.subtract).then_inc(split, 1)
                    v.wait_ge(split, 2 * c + 2)
                    rest = wrest[:, :, c]
            v.wait_ge(made, MADE + 1)
            def batch(i):
                for h in range(2):
                    past(v, counted[h], i)
                    at = bass.ds(i * (2 * B) + h * B, B)
                    for j, (lo, hi) in enumerate(((k["dlo"], k["dhi"]), (k["slo"], k["shi"]))):
                        v.tensor_tensor(oh[:, h, j], bc(lo[:, at], [P, B, P], 2), bc(k["iota"][:, :], [P, B, P], 1),
                                        ALU.is_equal)
                        w = v.tensor_tensor(ohh[:, h, j], bc(hi[:, at], [P, B, NT], 2),
                                            bc(k["iota"][:, 0:NT], [P, B, NT], 1), ALU.is_equal)
                    w.then_inc(onehots[h], 1)
                    v.wait_ge(onehots[h], 2 * i + 1)
                    v.tensor_tensor(ohw[:, h], bc(ohh[:, h, 1], [P, B, 3, NT], 2), bc(wpart[:, at, :], [P, B, 3, NT], 3),
                                    ALU.mult).then_inc(onehots[h], 1)

            each(v, T // (2 * B), batch)
            v.wait_ge(total, 1)
            for j in range(2):
                v.tensor_copy(hist_sb[:, j, :], hist[j][:, 0:NT]).then_inc(hist_out, 1)
            v.wait_ge(prefix, 1)
            v.wait_ge(hist_out, 2)
            v.tensor_copy(tot_sb[:, :, :], tot[:, 0:2 * NT].rearrange("p (j t) -> p j t", j=2)).then_inc(based, 1)
            v.wait_ge(based, 1)
            for j in range(2):
                w = v.tensor_tensor_scan(run_sb[:, j, :], ones[:, 0:NT], tot_sb[:, j, :], 0.0, ALU.mult, ALU.add)
            w.then_inc(based, 1)
            v.wait_ge(based, 2)
            v.tensor_tensor(run_sb[:, :, :], run_sb[:, :, :], tot_sb[:, :, :], ALU.subtract).then_inc(based, 1)
            v.wait_ge(based, 3)
            v.tensor_tensor(k["base"][:, :, :], run_sb[:, :, :], pre[:, 0:2 * NT].rearrange("p (j t) -> p j t", j=2),
                            ALU.add).then_inc(based, 1)
            v.tensor_copy(parts_sb[:, :], hist[1][:, NT:4 * NT]).then_inc(based, 1)
            v.tensor_scalar(k["deg_dst"][:, :], hist_sb[:, 0, :], -1.0, None, ALU.add)
            v.tensor_scalar(k["deg_src"][:, :], hist_sb[:, 1, :], -1.0, None, ALU.add)
            v.wait_ge(based, 5)
            v.tensor_reduce(k["weight_src"][:, :], parts_sb[:, :].rearrange("p (c t) -> p t c", c=3), AX.X, ALU.add)

        @block.tensor
        def _(pe):
            pe.wait_ge(consts, 2)
            for j in range(2):
                pe.matmul(hist[j][:, 0:4 * NT], zeros[:, :], zeros[:, 0:4 * NT], start=True, stop=False)
            with pe.Fori(0, T // (2 * B)) as i:
                for h in range(2):
                    pe.wait_ge(onehots[h], 2 * i + 1)
                    for j in range(2):
                        for u in range(B):
                            pe.matmul(hist[j][:, 0:NT], oh[:, h, j, u, :], ohh[:, h, j, u, :],
                                      start=False, stop=False, skip_group_check=True)
                    pe.wait_ge(onehots[h], 2 * i + 2)
                    for u in range(B):
                        m = pe.matmul(hist[1][:, NT:4 * NT], oh[:, h, 1, u, :], ohw[:, h, u].rearrange("p c t -> p (c t)"),
                                      start=False, stop=False, skip_group_check=True)
                    m.then_inc(counted[h], 1)
            for j in range(2):
                m = pe.matmul(hist[j][:, 0:4 * NT], zeros[:, :], zeros[:, 0:4 * NT], start=False, stop=True)
            m.then_inc(total, 1)
            pe.wait_ge(hist_out, 2)
            pe.wait_ge(made, MADE)
            pe.matmul(pre[:, 0:2 * NT], upper[:, :], hist_sb[:, :, :], start=True, stop=True)
            pe.matmul(tot[:, 0:2 * NT], ones[:, :], hist_sb[:, :, :], start=True, stop=True).then_inc(prefix, 1)


def sort_phase(nc, d, k):
    with Space(nc, "sort") as s:
        width, field = (RW, RW2), (DST, SRC)
        lo, hi = (k["dlo"], k["slo"]), (k["dhi"], k["shi"])
        target = (d["records"], d["records2"])
        attr = s.sb("attr", [P, T, DE])
        asum = s.sb("asum", [P, DE])
        ones = s.sb("ones", [P, 1])
        oh = s.sb("oh", [P, 2, G, P], BF16)
        ohh = s.sb("ohh", [P, 2, G, NT])
        ohhb = s.sb("ohhb", [P, 2, G, NT], BF16)
        oht = s.sb("oht", [P, 2, G, P])
        dcol = s.sb("dcol", [P, 2, G])
        base = s.sb("base", [P, 2, 2, G, NT])
        junk = s.sb("junk", [P, 2, G, P])
        junk2 = s.sb("junk2", [P, 2, G, NT])
        inside, outside = s.sb("inside", [P, 2, G]), s.sb("outside", [P, 2, G])
        place = s.sb("place", [P, 2, 2, G], I32)
        rec = [s.sb(f"rec{j}", [P, 2, G, width[j]]) for j in range(2)]
        rowb = [s.ps(f"rowb{j}", [P, G, P]) for j in range(2)]
        tr = [s.ps(f"tr{j}", [P, G, P], BF16) for j in range(2)]
        step = [s.ps(f"step{j}", [P, G, P]) for j in range(2)]
        got = [s.ps(f"got{j}", [P, G, P]) for j in range(2)]
        mean = got[0][0:DE, 0, :]
        pair = lambda name: [s.sem(f"{name}{j}") for j in range(2)]
        loaded, summed, meaned, ready = s.sem("loaded"), s.sem("summed"), s.sem("meaned"), s.sem("ready")
        onehots = pair("onehots")
        rows = pair("rows")
        turned = pair("turned")
        tr_out = pair("tr_out")
        counted = pair("counted")
        based = pair("based")
        looked = pair("looked")
        chosen = pair("chosen")
        placed = [pair(f"placed{p}") for p in range(2)]
        recs = [pair(f"recs{p}") for p in range(2)]
        sent = [pair(f"sent{p}") for p in range(2)]
        block = s.block()
        n = T // (2 * G)

        @block.sync
        def _(sp):
            sp.dma_start(attr[:, :, :], d["attr"].rearrange("(p t) w -> p t w", p=P)).then_inc(loaded, 16)

        @block.vector
        def _(v):
            def onehot(i, p, j):
                at = bass.ds(i * (2 * G) + p * G, G)
                v.tensor_copy(dcol[:, j, :], k["meta"][:, field[j], at])
                v.tensor_tensor(oh[:, j], bc(lo[j][:, at], [P, G, P], 2), bc(k["iota"][:, :], [P, G, P], 1),
                                ALU.is_equal)
                v.tensor_tensor(ohhb[:, j], bc(hi[j][:, at], [P, G, NT], 2),
                                bc(k["iota"][:, 0:NT], [P, G, NT], 1), ALU.is_equal)
                v.tensor_tensor(ohh[:, j], bc(hi[j][:, at], [P, G, NT], 2),
                                bc(k["iota"][:, 0:NT], [P, G, NT], 1), ALU.is_equal).then_inc(onehots[j], 1)

            def count(i, p, j):
                g = i * 2 + p
                v.wait_ge(onehots[j], g + 1)
                v.wait_ge(rows[j], g + 1)
                past(v, placed[1 - p][j], i + p)
                for u in range(G):
                    v.scalar_tensor_tensor(junk[:, j, u, :], rowb[j][:, u, :], dcol[:, j, u:u + 1], k["before"][:, :],
                                           ALU.is_equal, ALU.mult, accum_out=inside[:, j, u:u + 1]
                                           ).then_inc(counted[j], 1)
                v.wait_ge(turned[j], g + 1)
                for u in range(G):
                    to = base[:, j, p, u + 1, :] if u < G - 1 else base[:, j, 1 - p, 0, :]
                    past(v, based[j], g * G + u)
                    v.tensor_tensor(to, base[:, j, p, u, :], step[j][:, u, 0:NT], ALU.add).then_inc(based[j], 1)

            def choose(i, p, j):
                g = i * 2 + p
                v.wait_ge(looked[j], g + 1)
                for u in range(G):
                    v.scalar_tensor_tensor(junk2[:, j, u, :], got[j][:, u, 0:NT], 1.0, ohh[:, j, u, :],
                                           ALU.mult, ALU.mult, accum_out=outside[:, j, u:u + 1]
                                           ).then_inc(chosen[j], 1)
                past(v, sent[p][j], i * (16 * G))
                v.wait_ge(chosen[j], (g + 1) * G)
                v.wait_ge(counted[j], (g + 1) * G)
                v.tensor_tensor(place[:, j, p, :], inside[:, j, :], outside[:, j, :], ALU.add).then_inc(placed[p][j], 1)

            def groups(i):
                for p in range(2):
                    for work in (onehot, count, choose):
                        for j in range(2):
                            work(i, p, j)

            v.memset(ones[:, :], 1.0).then_inc(ready, 1)
            v.tensor_copy(base[:, :, 0, 0, :], k["base"][:, :, :]).then_inc(ready, 1)
            v.wait_ge(ready, 2)
            each(v, n, groups)
            v.wait_ge(loaded, 16)
            v.tensor_reduce(asum[:, :], attr[:, :, :].rearrange("p t w -> p w t"), AX.X, ALU.add).then_inc(summed, 1)
            v.wait_ge(meaned, 1)
            v.tensor_scalar(k["mean"][:, :], mean[:, 0:1], 1.0 / E, None, ALU.mult).then_inc(summed, 1)

        @block.tensor
        def _(pe):
            def groups(i):
                for p in range(2):
                    g = i * 2 + p
                    for j in range(2):
                        pe.wait_ge(onehots[j], g + 1)
                        past(pe, counted[j], g * G)
                        for u in range(G):
                            m = pe.matmul(rowb[j][:, u, :], dcol[:, j, u:u + 1].to_broadcast([P, P]), k["ident"][:, :],
                                          start=True, stop=True)
                        m.then_inc(rows[j], 1)
                        past(pe, tr_out[j], g)
                        for u in range(G):
                            pe.transpose(tr[j][:, u, :], oh[:, j, u, :], k["identb"][:, :])
                        past(pe, based[j], g * G)
                        for u in range(G):
                            m = pe.matmul(step[j][:, u, 0:NT], oh[:, j, u, :], ohhb[:, j, u, :], start=True, stop=True)
                        m.then_inc(turned[j], 1)
                    for j in range(2):
                        pe.wait_ge(tr_out[j], g + 1)
                        pe.wait_ge(based[j], g * G + G - 1)
                        past(pe, chosen[j], g * G)
                        for u in range(G):
                            m = pe.matmul(got[j][:, u, 0:NT], oht[:, j, u, :], base[:, j, p, u, :], start=True, stop=True)
                        m.then_inc(looked[j], 1)

            pe.wait_ge(ready, 2)
            each(pe, n, groups)
            pe.wait_ge(summed, 1)
            pe.matmul(mean[:, 0:1], asum[:, :], ones[:, :], start=True, stop=True).then_inc(meaned, 1)

        @block.scalar
        def _(act):
            def groups(i):
                for p in range(2):
                    at = bass.ds(i * (2 * G) + p * G, G)
                    g = i * 2 + p
                    for j in range(2):
                        act.wait_ge(turned[j], g + 1)
                        past(act, looked[j], g)
                        act.copy(oht[:, j], tr[j][:, :, :]).then_inc(tr_out[j], 1)
                    for j in range(2):
                        past(act, sent[p][j], i * (16 * G))
                        if j == 0:
                            act.copy(rec[0][:, p, :, 0:DE], attr[:, at, :])
                            m = act.copy(rec[0][:, p, :, DE:RW], k["meta"][:, :, at].rearrange("p f t -> p t f"))
                        else:
                            for c, f in enumerate((DST, WEIGHT, SRC)):
                                m = act.copy(rec[1][:, p, :, c], k["meta"][:, f, at])
                        m.then_inc(recs[p][j], 1)

            act.wait_ge(loaded, 16)
            each(act, n, groups)

        @block.gpsimd
        def _(pool):
            def groups(i):
                for p in range(2):
                    for j in range(2):
                        pool.wait_ge(placed[p][j], i + 1)
                        pool.wait_ge(recs[p][j], i + 1)
                        hold(pool)
                        for u in range(G):
                            pool.indirect_dma_start(
                                out=target[j][:, :], out_offset=bass.IndirectOffsetOnAxis(ap=place[:, j, p, u:u + 1], axis=0),
                                in_=rec[j][:, p, u, :], in_offset=None).then_inc(sent[p][j], 16)

            each(pool, n, groups)
            for p in range(2):
                for j in range(2):
                    pool.wait_ge(sent[p][j], n * 16 * G)


def norm_tensors(s, name):
    return dict(stats=s.sb(f"{name}_stats", [P, NB, 6]), mv=s.sb(f"{name}_mv", [P, NB, 2]), sd=s.sb(f"{name}_sd", [P, NB]),
                rs=s.sb(f"{name}_rs", [P, NB]), have_stats=s.sem(f"{name}_have_stats"), have_mv=s.sem(f"{name}_have_mv"),
                have_sd=s.sem(f"{name}_have_sd"), have_rs=s.sem(f"{name}_have_rs"), normed=s.sem(f"{name}_normed"))


def norm_vector(v, q, i, x, out):
    for u in range(NB):
        w = v.bn_stats(q["stats"][:, u, :], x[:, u, :])
    w.then_inc(q["have_stats"], 1)
    v.wait_ge(q["have_stats"], i + 1)
    hold(v)
    for u in range(NB):
        w = v.bn_aggr(q["mv"][:, u, :], q["stats"][:, u, :])
    w.then_inc(q["have_mv"], 1)
    v.wait_ge(q["have_sd"], i + 1)
    v.reciprocal(q["rs"][:, :], q["sd"][:, :]).then_inc(q["have_rs"], 1)
    v.wait_ge(q["have_rs"], i + 1)
    for u in range(NB):
        w = v.tensor_scalar(out[:, u, :], x[:, u, :], q["mv"][:, u, 0:1], q["rs"][:, u:u + 1], ALU.subtract, ALU.mult)
    w.then_inc(q["normed"], 1)


def norm_scalar(act, q, i, k):
    act.wait_ge(q["have_mv"], i + 1)
    act.activation(q["sd"][:, :], q["mv"][:, :, 1], ACT.Sqrt, bias=k["eps"][:, 0:1]).then_inc(q["have_sd"], 1)


def rows_of(table, i):
    return table.rearrange("(a l) w -> l a w", l=P)[:, bass.ds(i * NB, NB), :]


def enter_phase(nc, d, k):
    with Space(nc, "enter") as s:
        wlr = s.sb("wlr", [P, 2 * D])
        we = s.sb("we", [DE, D])
        aug = s.sb("aug", [DE, DE + 1])
        xs, h0, hn, ht = (s.sb(n, [P, NB, D]) for n in ("xs", "h0", "hn", "ht"))
        lr = s.sb("lr", [P, 2, NB, D])
        tp = s.ps("tp", [P, 8, D])
        mm = s.ps("mm", [P, 6, 2 * D])
        wa = s.ps("wa", [P, 512])
        fb, fb2 = s.ps("fb", [P, 512]), s.ps("fb2", [P, 512])
        first, zero, one = s.sb("first", [1, T, 2]), s.sb("zero", [P, D]), s.sb("one", [1, P])
        firsts, zeroed, spread = s.sem("firsts"), s.sem("zeroed"), s.sem("spread")
        q1, q2 = norm_tensors(s, "n1"), norm_tensors(s, "n2")
        loaded, epsed, tabled = s.sem("loaded"), s.sem("epsed"), s.sem("tabled")
        augged, edged, kept = s.sem("augged"), s.sem("edged"), s.sem("kept")
        taken, relued, scaled = s.sem("taken"), s.sem("relued"), s.sem("scaled")
        affine, turned, turned_out = s.sem("affine"), s.sem("turned"), s.sem("turned_out")
        product, product_out, stored = s.sem("product"), s.sem("product_out"), s.sem("stored")
        block = s.block()
        n = NT // NB
        par = k["par"]

        @block.sync
        def _(sp):
            sp.dma_start(k["x"][:, :, :], d["x"].rearrange("(a l) w -> l a w", l=P)).then_inc(loaded, 16)
            sp.dma_start(wlr[:, :], d["wlr"]).then_inc(loaded, 16)
            sp.dma_start(we[:, :], d["we"]).then_inc(loaded, 16)
            sp.dma_start(k["rec2"][:, :, :], d["records2"].rearrange("(t p) w -> p t w", p=P)).then_inc(tabled, 16)
            sp.dma_start(k["par"][:, :, :], d["par"].rearrange("(o a) w -> o a w", o=1).to_broadcast([P, PARS, D])
                         ).then_inc(loaded, 16)
            sp.dma_start(first[:, :, :], d["records"].rearrange("(t p) w -> p t w", p=P)[0:1, :, DE + TYPE:DE + DST + 1]
                         ).then_inc(firsts, 16)
            sp.wait_ge(zeroed, 1)
            sp.dma_start(d["right"][NP:NP + P, :], zero[:, :]).then_inc(firsts, 16)

            def step(i):
                sp.wait_ge(product_out, i + 1)
                sp.dma_start(rows_of(d["left"][0:NP], i), lr[:, 0]).then_inc(stored, 16)
                sp.dma_start(rows_of(d["right"][0:NP], i), lr[:, 1]).then_inc(stored, 16)

            each(sp, n, step)
            sp.wait_ge(stored, 32 * n)
            sp.wait_ge(firsts, 32)
            sp.wait_ge(tabled, 16)

        @block.vector
        def _(v):
            v.memset(k["eps"][:, :], EPS).then_inc(epsed, 1)
            v.memset(one[:, :], 1.0)
            v.memset(zero[:, :], 0.0).then_inc(zeroed, 1)
            v.tensor_copy(aug[:, 0:DE], k["ident"][0:DE, 0:DE])
            v.tensor_copy(aug[:, DE:DE + 1], k["mean"][:, :]).then_inc(augged, 1)
            v.wait_ge(loaded, 64)

            def step(i):
                past(v, q1["normed"], i)
                v.tensor_copy(xs[:, :, :], k["x"][:, bass.ds(i * NB, NB), :]).then_inc(taken, 1)
                v.wait_ge(taken, i + 1)
                norm_vector(v, q1, i, xs, h0)
                v.wait_ge(relued, i + 1)
                norm_vector(v, q2, i, h0, hn)
                v.wait_ge(q2["normed"], i + 1)
                v.tensor_tensor(hn[:, :, :], hn[:, :, :], bc(par[:, LN1_G, :], [P, NB, D], 1), ALU.mult).then_inc(scaled, 1)
                v.wait_ge(scaled, i + 1)
                v.tensor_tensor(hn[:, :, :], hn[:, :, :], bc(par[:, LN1_B, :], [P, NB, D], 1), ALU.add).then_inc(affine, 1)
                v.wait_ge(product, i + 1)
                past(v, stored, i * 32)
                v.tensor_copy(lr[:, :, :, :].rearrange("p s a w -> p a s w"),
                              mm[:, 0:NB, :].rearrange("p a (s w) -> p a s w", s=2)).then_inc(product_out, 1)

            each(v, n, step)
            v.wait_ge(spread, 1)
            v.tensor_copy(k["start"][:, :], fb[:, 0:T])
            v.tensor_copy(k["start_i"][:, :], first[:, :, 1])
            v.tensor_copy(k["start2_i"][:, :], k["rec2"][0:1, :, 2])
            v.tensor_tensor(k["loc2"][:, :], k["rec2"][:, :, 2], fb2[:, 0:T], ALU.subtract)
            v.tensor_copy(k["idx2"][:, :], k["rec2"][:, :, 0])
            v.tensor_copy(k["w2"][:, :], k["rec2"][:, :, 1])

        @block.scalar
        def _(act):
            act.wait_ge(epsed, 1)
            with act.Fori(0, n) as i:
                norm_scalar(act, q1, i, k)
                act.wait_ge(q1["normed"], i + 1)
                act.activation(h0[:, :, :], h0[:, :, :], ACT.Relu).then_inc(relued, 1)
                act.wait_ge(relued, i + 1)
                act.copy(k["h"][:, bass.ds(i * NB, NB), :], h0[:, :, :]).then_inc(kept, 1)
                norm_scalar(act, q2, i, k)
                act.wait_ge(turned, i + 1)
                act.copy(ht[:, :, :], tp[:, 0:NB, :]).then_inc(turned_out, 1)
            act.wait_ge(edged, 1)
            act.copy(k["wedge"][:, :], wa[0:DE + 1, 0:D])

        @block.tensor
        def _(pe):
            with pe.Fori(0, n) as i:
                pe.wait_ge(affine, i + 1)
                for u in range(NB):
                    m = pe.transpose(tp[:, u, :], hn[:, u, :], k["ident"][:, :])
                m.then_inc(turned, 1)
                pe.wait_ge(turned_out, i + 1)
                pe.wait_ge(loaded, 64)
                for u in range(NB):
                    m = pe.matmul(mm[:, u, :], ht[:, u, :], wlr[:, :], start=True, stop=True)
                m.then_inc(product, 1)
            pe.wait_ge(firsts, 32)
            pe.wait_ge(tabled, 16)
            pe.matmul(fb2[:, 0:T], one[:, :], k["rec2"][0:1, :, 2], start=True, stop=True)
            pe.matmul(fb[:, 0:T], one[:, :], first[:, :, 1], start=True, stop=True).then_inc(spread, 1)
            pe.wait_ge(augged, 1)
            pe.wait_ge(loaded, 64)
            pe.matmul(wa[0:DE + 1, 0:D], aug[:, :], we[:, :], start=True, stop=True).then_inc(edged, 1)


def score_phase(nc, d, k):
    with Space(nc, "score") as s:
        rec = s.sb("rec", [P, SLOTS, U, RW])
        ends = s.sb("ends", [P, SLOTS, U], I32)
        loc = s.sb("loc", [P, SLOTS, U], BF16)
        rows = s.sb("rows", [P, SLOTS, U, D])
        win = s.sb("win", [P, SLOTS, U, D])
        hot = s.sb("hot", [P, 2, G, P])
        at_sb = s.sb("at_sb", [DE + 1, 2, G, P])
        lk = s.sb("lk", [P, 2, G, D])
        yf = s.sb("yf", [P, SLOTS, U])
        tp = [s.ps(f"tp{b}", [P, G, P]) for b in range(2)]
        rowb = [s.ps(f"rowb{b}", [P, G, P]) for b in range(2)]
        z = [s.ps(f"z{b}", [P, G, D]) for b in range(2)]
        slots = lambda name: [s.sem(f"{name}{h}") for h in range(SLOTS)]
        loaded, windows, cols, gathered, stored = (slots(x) for x in ("loaded", "windows", "cols", "gathered", "stored"))
        yready = s.sem("yready")
        turned, turned_out = s.sem("turned"), s.sem("turned_out")
        spread, hots = s.sem("spread"), s.sem("hots")
        summed, copied, leaky, weighed, scored = (s.sem(x) for x in ("summed", "copied", "leaky", "weighed", "scored"))
        block = s.block()
        n = T // (SLOTS * U)

        @block.sync
        def _(sp):
            def slots_of(i):
                for h in range(SLOTS):
                    q = i * SLOTS + h
                    at = bass.ds(q * U, U)
                    past(sp, scored, reused(i, h))
                    sp.dma_start(rec[:, h], d["records"].rearrange("(t p) w -> p t w", p=P)[:, at, :]
                                 ).then_inc(loaded[h], 16)
                    _, nodes = nc.values_load_multi_w_load_instructions(
                        k["start_i"][0:1, at], engines=[mybir.EngineType.SP], min_val=0, max_val=NP - 1)
                    for u in range(U):
                        sp.dma_start(win[:, h, u, :], d["right"][bass.ds(nodes[u], P), :]).then_inc(windows[h], 16)

            each(sp, n, slots_of)

        @block.vector
        def _(v):
            def extract(i, h):
                at = bass.ds((i * SLOTS + h) * U, U)
                v.wait_ge(loaded[h], (i + 1) * 16)
                v.tensor_copy(ends[:, h, :], rec[:, h, :, DE + SRC])
                v.tensor_tensor(loc[:, h, :], rec[:, h, :, DE + DST], k["start"][:, at], ALU.subtract).then_inc(cols[h], 1)
                v.tensor_tensor(k["loc"][:, at], rec[:, h, :, DE + DST], k["start"][:, at], ALU.subtract)
                v.scalar_tensor_tensor(yf[:, h, :], rec[:, h, :, DE + SRC], float(R), rec[:, h, :, DE + TYPE],
                                       ALU.mult, ALU.add).then_inc(yready, 1)
                v.tensor_copy(k["src"][:, at], rec[:, h, :, DE + SRC])
                v.tensor_copy(k["dst"][:, at], rec[:, h, :, DE + DST])
                v.tensor_scalar(k["real"][:, at], rec[:, h, :, DE + SELF], -1.0, 1.0, ALU.mult, ALU.add)
                v.wait_ge(yready, i * SLOTS + h + 1)
                v.tensor_copy(k["relsrc"][:, at], yf[:, h, :])

            def onehot(i, h, b):
                g = number(i, h, b)
                v.wait_ge(cols[h], i + 1)
                v.wait_ge(spread, g + 1)
                past(v, summed, g - 1)
                v.tensor_scalar(hot[:, b], rowb[b][:, :, :], k["part"][:, 0:1], None, ALU.is_equal).then_inc(hots, 1)

            def score(i, h, b):
                g = number(i, h, b)
                v.wait_ge(copied, g + 1)
                v.scalar_tensor_tensor(lk[:, b], lk[:, b], SLOPE, lk[:, b], ALU.mult, ALU.max).then_inc(leaky, 1)
                v.wait_ge(leaky, g + 1)
                v.tensor_tensor(lk[:, b], lk[:, b], bc(k["par"][:, ATT, :], [P, G, D], 1), ALU.mult).then_inc(weighed, 1)
                v.wait_ge(weighed, g + 1)
                v.tensor_reduce(k["alpha"][:, bass.ds(g * G, G), :], lk[:, b].rearrange("p g (h c) -> p g h c", h=H),
                                AX.X, ALU.add).then_inc(scored, 1)

            def body(i, last):
                for group, nxt, later in ring(i, last):
                    if nxt:
                        onehot(*nxt)
                    score(*group)
                    if later:
                        extract(*later)

            extract(0, 0)
            extract(0, 1)
            onehot(0, 0, 0)
            each_ahead(v, n, body)

        @block.gpsimd
        def _(pool):
            def slots_of(i):
                for h in range(SLOTS):
                    pool.wait_ge(cols[h], i + 1)
                    past(pool, scored, reused(i, h))
                    past(pool, stored[h], i * 16)
                    hold(pool)
                    for u in range(U):
                        pool.indirect_dma_start(
                            out=rows[:, h, u, :], out_offset=None, in_=d["left"][:, :],
                            in_offset=bass.IndirectOffsetOnAxis(ap=ends[:, h, u:u + 1], axis=0)
                        ).then_inc(gathered[h], 16)

            each(pool, n, slots_of)

        @block.tensor
        def _(pe):
            def prepare(i, h, b):
                g = number(i, h, b)
                pe.wait_ge(loaded[h], (i + 1) * 16)
                past(pe, turned_out, g - 1)
                hold(pe)
                for u in range(G):
                    m = pe.transpose(tp[b][0:DE + 1, u, :], rec[:, h, b * G + u, 0:DE + 1], k["ident"][:, :])
                m.then_inc(turned, 1)
                pe.wait_ge(cols[h], i + 1)
                past(pe, hots, g - 1)
                for u in range(G):
                    m = pe.matmul(rowb[b][:, u, :], loc[:, h, b * G + u:b * G + u + 1].to_broadcast([P, P]),
                                  k["identb"][:, :], start=True, stop=True)
                m.then_inc(spread, 1)

            def total(i, h, b):
                g = number(i, h, b)
                past(pe, copied, g - 1)
                pe.wait_ge(turned_out, g + 1)
                pe.wait_ge(hots, g + 1)
                if b == 0:
                    pe.wait_ge(windows[h], (i + 1) * (16 * U))
                    pe.wait_ge(gathered[h], (i + 1) * (16 * U))
                for u in range(G):
                    pe.matmul(z[b][:, u, :], at_sb[:, b, u, :], k["wedge"][:, :], start=True, stop=False)
                    pe.matmul(z[b][:, u, :], hot[:, b, u, :], win[:, h, b * G + u, :], start=False, stop=False)
                    m = pe.matmul(z[b][:, u, :], k["ident"][:, :], rows[:, h, b * G + u, :], start=False, stop=True)
                m.then_inc(summed, 1)

            def body(i, last):
                for group, nxt, later in ring(i, last):
                    if nxt:
                        prepare(*nxt)
                    total(*group)

            prepare(0, 0, 0)
            each_ahead(pe, n, body)

        @block.scalar
        def _(act):
            def copy_turned(i, h, b):
                g = number(i, h, b)
                act.wait_ge(turned, g + 1)
                past(act, summed, g - 1)
                act.copy(at_sb[:, b], tp[b][0:DE + 1]).then_inc(turned_out, 1)

            def body(i, last):
                for group, nxt, later in ring(i, last):
                    if nxt:
                        copy_turned(*nxt)
                    i, h, b = group
                    g = number(i, h, b)
                    act.wait_ge(summed, g + 1)
                    past(act, scored, g - 1)
                    act.copy(lk[:, b], z[b][:, :, :]).then_inc(copied, 1)
                    if b == 1:
                        act.wait_ge(gathered[h], (i + 1) * (16 * U))
                        act.dma_start(d["leftsrc"].rearrange("(t p) w -> p t w", p=P)[:, bass.ds((i * SLOTS + h) * U, U), :],
                                      rows[:, h]).then_inc(stored[h], 16)

            copy_turned(0, 0, 0)
            each_ahead(act, n, body)
            for h in range(SLOTS):
                act.wait_ge(stored[h], n * 16)


def softmax_phase(nc, d, k):
    with Space(nc, "softmax") as s:
        val, dst, run, back = (s.sb(x, [P, CT, P]) for x in ("val", "dst", "run", "back"))
        shut = s.sb("shut", [P, CL + 1])
        pack = s.sb("pack", [P, 2, CT, P])
        packed = s.sem("packed")
        one = s.sb("one", [1, 1])
        edge = s.sb("edge", [P, 4])
        lv, lk, lr, lf, lb = (s.sb(x, [1, 2 * P + 1]) for x in ("lv", "lk", "lr", "lf", "lb"))
        full = s.sb("full", [P, 2])
        tp = [s.ps(f"tp{b}", [P, 4, P]) for b in range(4)]
        line = s.ps("line", [1, 4, P])
        fullp = s.ps("fullp", [P, 512])
        turned, out = s.sem("turned"), s.sem("out")
        step = s.sem("step")
        lined, fulled = s.sem("lined"), s.sem("fulled")
        expd = s.sem("expd")
        turned2, out2 = s.sem("turned2"), s.sem("out2")
        block = s.block()
        n4 = -(-CT // 4)
        vf, df, rf, bf = (x[:, :, :].rearrange("p t e -> p (t e)") for x in (val, dst, run, back))

        @block.tensor
        def _(pe):
            pe.wait_ge(packed, 2)
            for q in range(2 * n4):
                if q >= 4:
                    pe.wait_ge(out, q - 3)
                for j in range(4 * (q // 2), min(CT, 4 * (q // 2) + 4)):
                    m = pe.transpose(tp[q % 4][:, j % 4, :], pack[:, q % 2, j, :], k["ident"][:, :])
                m.then_inc(turned, 1)
            pe.wait_ge(step, 5)
            for c in range(4):
                m = pe.transpose(line[:, c, :], edge[:, c:c + 1], k["ident"][:, :])
            m.then_inc(lined, 1)
            pe.wait_ge(step, 11)
            for c in range(2):
                m = pe.transpose(fullp[:, c:c + 1], lf[:, c * P:(c + 1) * P], one[:, :])
            m.then_inc(fulled, 1)
            for q in range(n4):
                pe.wait_ge(expd, q + 1)
                if q >= 4:
                    pe.wait_ge(out2, q - 3)
                for j in range(4 * q, min(CT, 4 * q + 4)):
                    m = pe.transpose(tp[q % 4][:, j % 4, :], val[:, j, :], k["ident"][:, :])
                m.then_inc(turned2, 1)

        @block.scalar
        def _(act):
            for q in range(2 * n4):
                a, b = 4 * (q // 2), min(CT, 4 * (q // 2) + 4)
                act.wait_ge(turned, q + 1)
                act.copy((val, dst)[q % 2][:, a:b, :], tp[q % 4][:, 0:b - a, :]).then_inc(out, 1)
            act.wait_ge(step, 17)
            for q in range(n4):
                a, b = 4 * q, min(CT, 4 * q + 4)
                act.activation(val[:, a:b, :], val[:, a:b, :], ACT.Exp).then_inc(expd, 1)

        @block.vector
        def _(v):
            v.tensor_copy(pack[:, 0].rearrange("p j (c h) -> p j c h", h=H),
                          k["alpha"][:, :, :].rearrange("p (c j) h -> p j c h", c=CH)).then_inc(packed, 1)
            v.tensor_copy(pack[:, 1].rearrange("p j (c h) -> p j c h", h=H),
                          k["dst"][:, :].rearrange("p (c j) -> p j c", c=CH).unsqueeze(3).to_broadcast([P, CT, CH, H])
                          ).then_inc(packed, 1)
            v.memset(one[:, :], 1.0)
            v.memset(shut[:, 0:1], 0.0)
            v.memset(shut[:, CL:CL + 1], 0.0)
            v.memset(lr[:, 0:1], 0.0)
            v.memset(lr[:, 2 * P:2 * P + 1], 0.0)
            v.wait_ge(out, 2 * n4)
            v.tensor_tensor(rf[:, 1:CL], df[:, 1:CL], df[:, 0:CL - 1], ALU.not_equal).then_inc(step, 1)
            v.wait_ge(step, 1)
            v.tensor_scalar(shut[:, 1:CL], rf[:, 1:CL], -FAR, None, ALU.mult).then_inc(step, 1)
            v.wait_ge(step, 2)
            v.tensor_tensor_scan(rf[:, :], shut[:, 0:CL], vf[:, :], -FAR, ALU.add, ALU.max).then_inc(step, 1)
            v.wait_ge(step, 3)
            v.tensor_tensor_scan(bf[:, ::-1], shut[:, 1:CL + 1][:, ::-1], rf[:, ::-1], -FAR, ALU.add, ALU.max).then_inc(step, 1)
            v.wait_ge(step, 4)
            for c, x in enumerate((bf[:, 0:1], bf[:, CL - 1:CL], df[:, 0:1], df[:, CL - 1:CL])):
                w = v.tensor_copy(edge[:, c:c + 1], x)
            w.then_inc(step, 1)
            v.wait_ge(lined, 1)
            for to, c in ((lv, 0), (lk, 2)):
                for e in range(2):
                    w = v.tensor_copy(to[:, e:2 * P:2].rearrange("o (h c) -> o h c", h=H),
                                      line[:, c + e, :].rearrange("o (c h) -> o h c", h=H))
            w.then_inc(step, 1)
            v.wait_ge(step, 6)
            v.tensor_tensor(lf[:, 1:2 * P], lk[:, 1:2 * P], lk[:, 0:2 * P - 1], ALU.not_equal).then_inc(step, 1)
            v.wait_ge(step, 7)
            v.tensor_scalar(lr[:, 1:2 * P], lf[:, 1:2 * P], -FAR, None, ALU.mult).then_inc(step, 1)
            v.wait_ge(step, 8)
            v.tensor_tensor_scan(lf[:, 0:2 * P], lr[:, 0:2 * P], lv[:, 0:2 * P], -FAR, ALU.add, ALU.max).then_inc(step, 1)
            v.wait_ge(step, 9)
            v.tensor_tensor_scan(lb[:, 0:2 * P][:, ::-1], lr[:, 1:2 * P + 1][:, ::-1], lf[:, 0:2 * P][:, ::-1], -FAR,
                                 ALU.add, ALU.max).then_inc(step, 1)
            v.wait_ge(step, 10)
            for e in range(2):
                w = v.tensor_copy(lf[:, e * P:(e + 1) * P].rearrange("o (c h) -> o h c", h=H),
                                  lb[:, e:2 * P:2].rearrange("o (h c) -> o h c", h=H))
            w.then_inc(step, 1)
            v.wait_ge(fulled, 1)
            v.tensor_copy(full[:, :], fullp[:, 0:2]).then_inc(step, 1)
            for e in range(2):
                v.wait_ge(step, 12 + 2 * e)
                v.tensor_scalar(rf[:, :], df[:, :], edge[:, 2 + e:3 + e], -FAR, ALU.not_equal, ALU.mult).then_inc(step, 1)
                v.wait_ge(step, 13 + 2 * e)
                v.scalar_tensor_tensor(bf[:, :], rf[:, :], full[:, e:e + 1], bf[:, :], ALU.add, ALU.max).then_inc(step, 1)
            v.wait_ge(step, 16)
            v.tensor_tensor(vf[:, :], vf[:, :], bf[:, :], ALU.subtract).then_inc(step, 1)
            for q in range(n4):
                v.wait_ge(turned2, q + 1)
                for j in range(4 * q, min(CT, 4 * q + 4)):
                    w = v.tensor_copy(k["alpha"][:, j::CT, :], tp[q % 4][:, j % 4, :].rearrange("p (c h) -> p c h", h=H))
                w.then_inc(out2, 1)


def run_sum_phase(nc, d, k, name, table, index, weight=None, loc="loc", start="start_i"):
    gat = weight is None
    with Space(nc, name) as s:
        idx = s.sb("idx", [P, SLOTS, U], I32)
        rows = s.sb("rows", [P, SLOTS, U, D])
        lcol, wcol = s.sb("lcol", [P, SLOTS, U]), s.sb("wcol", [P, SLOTS, U])
        msg, ex = (s.sb("msg", [P, 2, G, D]), s.sb("ex", [P, 2, G, H])) if gat else (None, None)
        hot = s.sb("hot", [P, 2, G, P])
        acc = [s.ps(f"acc{b}", [P, G, P]) for b in range(2)]
        accd = [s.ps(f"accd{b}", [H, G, P]) for b in range(2)] if gat else None
        den_sb = s.sb("den_sb", [H, 2, G, P]) if gat else None
        slots = lambda name: [s.sem(f"{name}{h}") for h in range(SLOTS)]
        cols, gathered = slots("cols"), slots("gathered")
        den_out, den_added = s.sem("den_out"), s.sem("den_added")
        masks, scaled, summed, added = (s.sem(x) for x in ("masks", "scaled", "summed", "added"))
        cleared = s.sem("cleared")
        block = s.block()
        n = T // (SLOTS * U)
        agg, den = k["agg"], k["den"]

        def nodes_of(engine, i, h, b):
            return nc.values_load_multi_w_load_instructions(
                k[start][0:1, bass.ds(number(i, h, b) * G, G)], engines=[engine], min_val=0, max_val=NP - 1)[1]

        @block.vector
        def _(v):
            def columns(i, h):
                at = bass.ds((i * SLOTS + h) * U, U)
                if not gat:
                    v.tensor_copy(idx[:, h, :], k[index][:, at])
                    v.tensor_copy(wcol[:, h, :], k[weight][:, at])
                v.tensor_copy(lcol[:, h, :], k[loc][:, at]).then_inc(cols[h], 1)

            def mask(u, i, h, b):
                if u == 0:
                    v.wait_ge(cols[h], i + 1)
                    past(v, summed, number(i, h, b) - 1)
                j = b * G + u
                if gat:
                    w = v.tensor_scalar(hot[:, b, u, :], k["iota"][:, :], lcol[:, h, j:j + 1], None, ALU.is_equal)
                else:
                    w = v.tensor_scalar(hot[:, b, u, :], k["iota"][:, :], lcol[:, h, j:j + 1], wcol[:, h, j:j + 1],
                                        ALU.is_equal, ALU.mult)
                w.then_inc(masks, 1)

            def scale(i, h, b):
                g = number(i, h, b)
                v.wait_ge(gathered[h], (i + 1) * 16)
                past(v, summed, g - 1)
                at = bass.ds(g * G, G)
                v.tensor_copy(ex[:, b], k["alpha"][:, at, :])
                v.tensor_tensor(msg[:, b].rearrange("p g (h c) -> p g h c", h=H),
                                rows[:, h, b * G:b * G + G, :].rearrange("p g (h c) -> p g h c", h=H),
                                k["alpha"][:, at, :].unsqueeze(3).to_broadcast([P, G, H, C]), ALU.mult
                                ).then_inc(scaled, 1)

            def add(u, node, i, h, b):
                g = number(i, h, b)
                if u == 0:
                    v.wait_ge(summed, g + 1)
                past(v, added, g * G + u)
                at = bass.ds(node, P)
                v.tensor_tensor(agg[:, at], agg[:, at], acc[b][:, u, :], ALU.add).then_inc(added, 1)

            def body(i, last):
                for group, nxt, later in ring(i, last):
                    nodes = nodes_of(mybir.EngineType.DVE, *group)
                    if gat and nxt:
                        scale(*nxt)
                    for u in range(G):
                        if nxt:
                            mask(u, *nxt)
                        add(u, nodes[u], *group)
                    if later:
                        columns(*later)

            if gat:
                v.memset(den[:, :], 0.0).then_inc(cleared, 1)
            v.memset(agg[:, :], 0.0).then_inc(cleared, 1)
            columns(0, 0)
            columns(0, 1)
            if gat:
                scale(0, 0, 0)
            for u in range(G):
                mask(u, 0, 0, 0)
            v.wait_ge(cleared, 2 if gat else 1)
            each_ahead(v, n, body)

        if gat:
            @block.scalar
            def _(act):
                def slots_of(i):
                    for h in range(SLOTS):
                        for b in range(2):
                            g = number(i, h, b)
                            act.wait_ge(summed, g + 1)
                            past(act, den_added, (g - 1) * G)
                            act.copy(den_sb[:, b], accd[b][:, :, :]).then_inc(den_out, 1)

                each(act, n, slots_of)

        @block.gpsimd
        def _(pool):
            def gather(i):
                for h in range(SLOTS):
                    pool.wait_ge(cols[h], i + 1)
                    past(pool, summed, reused(i, h))
                    hold(pool)
                    for u in range(U):
                        pool.indirect_dma_start(
                            out=rows[:, h, u, :], out_offset=None, in_=d[table][:, :],
                            in_offset=bass.IndirectOffsetOnAxis(ap=idx[:, h, u:u + 1], axis=0)
                        ).then_inc(gathered[h], 16)

            def add_exps(i):
                for h in range(SLOTS):
                    for b in range(2):
                        g = number(i, h, b)
                        nodes = nodes_of(mybir.EngineType.Pool, i, h, b)
                        pool.wait_ge(den_out, g + 1)
                        for u in range(G):
                            past(pool, den_added, g * G + u)
                            at = bass.ds(nodes[u], P)
                            pool.tensor_tensor(den[:, at], den[:, at], den_sb[:, b, u, :], ALU.add).then_inc(den_added, 1)

            if gat:
                pool.wait_ge(cleared, 1)
            each(pool, n, add_exps if gat else gather)

        @block.tensor
        def _(pe):
            def slots_of(i):
                for h in range(SLOTS):
                    for b in range(2):
                        g = number(i, h, b)
                        pe.wait_ge(masks, (g + 1) * G)
                        if gat:
                            pe.wait_ge(scaled, g + 1)
                            past(pe, den_out, g - 1)
                        elif b == 0:
                            pe.wait_ge(gathered[h], (i + 1) * (16 * U))
                        past(pe, added, (g - 1) * G)
                        for u in range(G):
                            if gat:
                                pe.matmul(accd[b][:, u, :], ex[:, b, u, :], hot[:, b, u, :], start=True, stop=True)
                            m = pe.matmul(acc[b][:, u, :], msg[:, b, u, :] if gat else rows[:, h, b * G + u, :],
                                          hot[:, b, u, :], start=True, stop=True)
                        m.then_inc(summed, 1)

            each(pe, n, slots_of)

        if gat:
            @block.sync
            def _(sp):
                def slots_of(i):
                    for h in range(SLOTS):
                        past(sp, scaled, reused(i, h))
                        sp.dma_start(rows[:, h], d[table].rearrange("(t p) w -> p t w", p=P)[:, bass.ds((i * SLOTS + h) * U, U), :]
                                     ).then_inc(gathered[h], 16)

                each(sp, n, slots_of)


def node_phase(nc, d, k, layer, table=None):
    with Space(nc, f"nodes{layer}") as s:
        NN = NT // NB
        raw = s.sb("raw", [P, NB, P])
        rawd = s.sb("rawd", [H, NB, P])
        a, at, y, xs = (s.sb(x, [P, NB, D]) for x in ("a", "at", "y", "xs"))
        hs, ht, tab = (s.sb(x, [P, NB, D]) for x in ("hs", "ht", "tab"))
        nrm = s.sb("nrm", [P, NB, H])
        tp = s.ps("tp", [P, 8, D])
        mm = s.ps("mm", [P, 8, D])
        mm2 = s.ps("mm2", [P, 8, D]) if layer == 2 else None
        dp = s.ps("dp", [P, 64, H]) if layer == 0 else None
        cols = s.sb("cols", [P, 4, NT])
        inv = s.sb("inv", [P, NT])
        w = s.sb("w", [P, 2 * D + 2 * D])
        b1 = s.sb("b1", [P, 2])
        ff = s.sb("ff", [P, 2, NB, D])
        fp = s.ps("fp", [P, 12, D]) if layer == 0 else None
        q1, q2 = norm_tensors(s, "n1"), norm_tensors(s, "n2")
        loaded = s.sem("loaded")
        names = ("rooted", "degree", "taken", "sliced", "den", "inv", "divided", "mixed", "ready", "turned", "turned_out",
                 "back", "product", "y1", "y2", "y3", "got_x", "scaled", "affine", "ff1", "gelu", "kept", "kept_h",
                 "relued", "tabled", "fresh")
        e = {x: s.sem(x) for x in names}
        stored = s.sem("stored")
        block = s.block()
        par = k["par"]
        normed_next = layer in (0, 1, 2)
        turns = layer in (0, 2)

        def row(j):
            return bc(par[:, j, :], [P, NB, D], 1)

        def col(c, i):
            return cols[:, c, bass.ds(i * NB, NB)].unsqueeze(2).to_broadcast([P, NB, D])

        DST_ROOT, SRC_ROOT = 0, 1

        @block.sync
        def _(sp):
            if layer == 0:
                sp.dma_start(w[:, 0:2 * D], d["w1"]).then_inc(loaded, 16)
                sp.dma_start(w[:, 2 * D:4 * D].rearrange("p (f w) -> p f w", f=2),
                             d["w2"].rearrange("(f p) w -> p f w", p=P)).then_inc(loaded, 16)
                sp.dma_start(b1[:, :], d["b1"]).then_inc(loaded, 16)
            else:
                sp.dma_start(w[:, 0:D], d["square"][SQUARE[layer]]).then_inc(loaded, 16)
                if layer == 2:
                    sp.dma_start(w[:, D:2 * D], d["square"][SQUARE[layer] + 1]).then_inc(loaded, 16)
            if table or layer == 4:
                def step(i):
                    sp.wait_ge(e["tabled"], i + 1)
                    sp.dma_start(rows_of(d[table] if table else d["out"], i), tab[:, :, :]).then_inc(stored, 16)

                each(sp, NN, step)
                sp.wait_ge(stored, 16 * NN)

        LOADS = 48 if layer == 0 else 32 if layer == 2 else 16

        @block.vector
        def _(v):
            for c, deg in enumerate(("deg_dst", "deg_src")):
                m = v.tensor_scalar(cols[:, 2 + c, :], k[deg][:, :], 1.0, None, ALU.max)
            m.then_inc(e["degree"], 1)
            v.reciprocal(inv[:, :], k["weight_src"][:, :])
            v.wait_ge(e["rooted"], 1)
            v.reciprocal(cols[:, 0:2, :], cols[:, 2:4, :]).then_inc(e["degree"], 1)
            v.wait_ge(e["degree"], 2)
            v.wait_ge(loaded, LOADS)

            def step(i):
                at_i = bass.ds(i * NB, NB)
                if layer == 4:
                    past(v, e["tabled"], i)
                v.tensor_copy(xs[:, :, :], k["x"][:, at_i, :])
                v.tensor_copy(hs[:, :, :], k["h"][:, at_i, :]).then_inc(e["taken"], 1)
                v.wait_ge(e["taken"], i + 1)
                if layer == 0:
                    v.wait_ge(e["back"], i + 1)
                    v.tensor_scalar(nrm[:, :, :], dp[:, 0:NB, :], 1e-16, None, ALU.add).then_inc(e["den"], 1)
                    v.wait_ge(e["den"], i + 1)
                    v.reciprocal(nrm[:, :, :], nrm[:, :, :]).then_inc(e["inv"], 1)
                    v.wait_ge(e["inv"], i + 1)
                    v.tensor_tensor(a[:, :, :].rearrange("p a (h c) -> p a h c", h=H),
                                    tp[:, 0:NB, :].rearrange("p a (h c) -> p a h c", h=H),
                                    nrm[:, :, :].unsqueeze(3).to_broadcast([P, NB, H, C]), ALU.mult).then_inc(e["divided"], 1)
                    v.wait_ge(e["divided"], i + 1)
                    v.tensor_tensor(a[:, :, :], a[:, :, :], row(BIAS), ALU.add).then_inc(e["mixed"], 1)
                    v.wait_ge(e["mixed"], i + 1)
                    v.tensor_tensor(hs[:, :, :], hs[:, :, :], a[:, :, :], ALU.add).then_inc(e["fresh"], 1)
                    v.wait_ge(e["fresh"], i + 1)
                    norm_vector(v, q1, i, hs, a)
                    v.wait_ge(q1["normed"], i + 1)
                    v.tensor_tensor(a[:, :, :], a[:, :, :], row(LN2_G), ALU.mult).then_inc(e["scaled"], 1)
                    v.wait_ge(e["scaled"], i + 1)
                    v.tensor_tensor(a[:, :, :], a[:, :, :], row(LN2_B), ALU.add).then_inc(e["ready"], 1)
                v.wait_ge(e["product"], i + 1)
                if layer == 0:
                    v.tensor_tensor(y[:, :, :], mm[:, 0:NB, :], hs[:, :, :], ALU.add).then_inc(e["y1"], 1)
                    v.wait_ge(e["y1"], i + 1)
                    v.tensor_tensor(y[:, :, :], y[:, :, :], row(L0_B2), ALU.add).then_inc(e["y2"], 1)
                    v.wait_ge(e["y2"], i + 1)
                    v.tensor_tensor(xs[:, :, :], xs[:, :, :], y[:, :, :], ALU.add).then_inc(e["got_x"], 1)
                elif layer == 1:
                    v.tensor_tensor(y[:, :, :], mm[:, 0:NB, :], col(DST_ROOT, i), ALU.mult).then_inc(e["y1"], 1)
                    v.wait_ge(e["y1"], i + 1)
                    v.scalar_tensor_tensor(xs[:, :, :], y[:, :, :], 0.0, xs[:, :, :], ALU.max, ALU.add).then_inc(e["got_x"], 1)
                elif layer == 2:
                    v.tensor_tensor(y[:, :, :], mm[:, 0:NB, :], row(L2_B2), ALU.add).then_inc(e["y1"], 1)
                    v.wait_ge(e["y1"], i + 1)
                    v.tensor_tensor(y[:, :, :], y[:, :, :], inv[:, at_i].unsqueeze(2).to_broadcast([P, NB, D]), ALU.mult)
                    v.tensor_tensor(a[:, :, :], mm2[:, 0:NB, :], row(L2_B1), ALU.add).then_inc(e["y2"], 1)
                    v.wait_ge(e["y2"], i + 1)
                    v.tensor_tensor(y[:, :, :], y[:, :, :], a[:, :, :], ALU.add).then_inc(e["y3"], 1)
                    v.wait_ge(e["y3"], i + 1)
                    v.tensor_tensor(xs[:, :, :], xs[:, :, :], y[:, :, :], ALU.add).then_inc(e["got_x"], 1)
                else:
                    v.tensor_tensor(y[:, :, :], mm[:, 0:NB, :], col(DST_ROOT, i), ALU.mult).then_inc(e["y1"], 1)
                    v.wait_ge(e["y1"], i + 1)
                    v.tensor_tensor(y[:, :, :], y[:, :, :], row(L3_B1 if layer == 3 else L3_B2), ALU.add).then_inc(e["y2"], 1)
                    v.wait_ge(e["y2"], i + 1)
                    past(v, stored, i * 16)
                    if layer == 3:
                        v.tensor_scalar(y[:, :, :], y[:, :, :], 0.0, None, ALU.max).then_inc(e["y3"], 1)
                        v.wait_ge(e["y3"], i + 1)
                        v.tensor_tensor(tab[:, :, :], y[:, :, :], col(SRC_ROOT, i), ALU.mult).then_inc(e["tabled"], 1)
                    else:
                        v.scalar_tensor_tensor(tab[:, :, :], y[:, :, :], 0.0, xs[:, :, :], ALU.max, ALU.add
                                               ).then_inc(e["tabled"], 1)
                if normed_next:
                    v.wait_ge(e["got_x"], i + 1)
                    norm_vector(v, q2, i, xs, y)
                    v.wait_ge(e["kept"], i + 1)
                    v.wait_ge(e["relued"], i + 1)
                    if table:
                        past(v, stored, i * 16)
                        if layer == 2:
                            v.tensor_tensor(tab[:, :, :], y[:, :, :], col(SRC_ROOT, i), ALU.mult).then_inc(e["tabled"], 1)
                        else:
                            v.tensor_copy(tab[:, :, :], y[:, :, :]).then_inc(e["tabled"], 1)
                    v.wait_ge(e["kept_h"], i + 1)

            each(v, NN, step)

        @block.scalar
        def _(act):
            act.wait_ge(e["degree"], 1)
            act.activation(cols[:, 2:4, :], cols[:, 2:4, :], ACT.Sqrt).then_inc(e["rooted"], 1)

            def step(i):
                at_i = bass.ds(i * NB, NB)
                past(act, e["product"], i)
                if layer == 0:
                    act.copy(rawd[:, :, :], k["den"][:, 0:NP].rearrange("p (t l) -> p t l", l=P)[:, at_i, :])
                act.copy(raw[:, :, :], k["agg"][:, 0:NP].rearrange("p (t l) -> p t l", l=P)[:, at_i, :]
                         ).then_inc(e["sliced"], 1)
                if layer == 0:
                    norm_scalar(act, q1, i, k)
                if turns:
                    act.wait_ge(e["turned"], i + 1)
                    act.copy(at[:, :, :], tp[:, 0:NB, :]).then_inc(e["turned_out"], 1)
                if layer == 0:
                    act.wait_ge(e["ff1"], i + 1)
                    for f in range(2):
                        m = act.activation(ff[:, f, :, :], fp[:, f * 6:f * 6 + NB, :], ACT.Gelu, bias=b1[:, f:f + 1])
                    m.then_inc(e["gelu"], 1)
                if normed_next:
                    act.wait_ge(e["got_x"], i + 1)
                    act.copy(k["x"][:, at_i, :], xs[:, :, :]).then_inc(e["kept"], 1)
                    norm_scalar(act, q2, i, k)
                    act.wait_ge(q2["normed"], i + 1)
                    act.activation(y[:, :, :], y[:, :, :], ACT.Relu).then_inc(e["relued"], 1)
                    act.wait_ge(e["relued"], i + 1)
                    act.copy(k["h"][:, at_i, :], y[:, :, :]).then_inc(e["kept_h"], 1)

            each(act, NN, step)

        @block.tensor
        def _(pe):
            pe.wait_ge(loaded, LOADS)

            def step(i):
                pe.wait_ge(e["sliced"], i + 1)
                past(pe, e["y1"], i)
                if layer == 2:
                    past(pe, e["y2"], i)
                if layer == 0:
                    hold(pe)
                    for u in range(NB):
                        pe.transpose(dp[:, u, :], rawd[:, u, :], k["ident"][0:H, 0:H])
                    for u in range(NB):
                        m = pe.transpose(tp[:, u, :], raw[:, u, :], k["ident"][:, :])
                    m.then_inc(e["back"], 1)
                    pe.wait_ge(e["ready"], i + 1)
                if layer == 2:
                    pe.wait_ge(e["taken"], i + 1)
                if turns:
                    for u in range(NB):
                        m = pe.transpose(tp[:, u, :], (a if layer == 0 else hs)[:, u, :], k["ident"][:, :])
                    m.then_inc(e["turned"], 1)
                    pe.wait_ge(e["turned_out"], i + 1)
                if layer == 0:
                    for f in range(2):
                        for u in range(NB):
                            m = pe.matmul(fp[:, f * 6 + u, :], w[:, f * D:(f + 1) * D], at[:, u, :], start=True, stop=True)
                    m.then_inc(e["ff1"], 1)
                    pe.wait_ge(e["gelu"], i + 1)
                    for u in range(NB):
                        for f in range(2):
                            m = pe.matmul(mm[:, u, :], ff[:, f, u, :], w[:, (2 + f) * D:(3 + f) * D],
                                          start=(f == 0), stop=(f == 1))
                else:
                    if layer == 2:
                        for u in range(NB):
                            pe.matmul(mm2[:, u, :], at[:, u, :], w[:, D:2 * D], start=True, stop=True)
                    for u in range(NB):
                        m = pe.matmul(mm[:, u, :], raw[:, u, :], w[:, 0:D], start=True, stop=layer != 1)
                        if layer == 1:
                            m = pe.matmul(mm[:, u, :], raw[:, u, :], k["ident"][:, :], start=False, stop=True)
                m.then_inc(e["product"], 1)

            each(pe, NN, step)


def relation_phase(nc, d, k):
    GR = 4
    HR = R // 2
    with Space(nc, "relation") as s:
        wr = s.sb("wr", [P, R, D])
        feat = s.sb("feat", [P, R, D])
        hs, ht = s.sb("hs", [P, D]), s.sb("ht", [P, D])
        out = s.sb("out", [P, 2, HR, D])
        tp = s.ps("tp", [P, 512])
        mm = [s.ps(f"mm{b}", [P, GR, D]) for b in range(HR // GR)]
        loaded = s.sem("loaded")
        taken, turned, turned_out = s.sem("taken"), s.sem("turned"), s.sem("turned_out")
        product = s.sem("product")
        made = [s.sem(f"made{b}") for b in range(HR // GR)]
        stored = [s.sem(f"stored{h}") for h in range(2)]
        block = s.block()
        K = R // GR
        HK = K // 2

        @block.sync
        def _(sp):
            sp.dma_start(wr[:, :, :], d["wr"].rearrange("r p w -> p r w")).then_inc(loaded, 16)
            sp.dma_start(feat[:, :, :], d["feat"].rearrange("(o a) w -> o a w", o=1).to_broadcast([P, R, D])
                         ).then_inc(loaded, 16)
            table = d["relation"].rearrange("(t l r) w -> l t (r w)", l=P, r=R)

            def step(i):
                for h in range(2):
                    for b in range(HK):
                        sp.wait_ge(made[b], i * 2 + h + 1)
                    sp.dma_start(table[:, bass.ds(i, 1), h * HR * D:(h + 1) * HR * D],
                                 out[:, h:h + 1].rearrange("p o r w -> p o (r w)")).then_inc(stored[h], 16)

            each(sp, NT, step)
            for h in range(2):
                sp.wait_ge(stored[h], NT * 16)

        @block.scalar
        def _(act):
            def step(i):
                act.copy(hs[:, :].rearrange("p (o w) -> p o w", o=1), k["h"][:, bass.ds(i, 1), :]).then_inc(taken, 1)
                act.wait_ge(turned, i + 1)
                past(act, product, i * K)
                act.copy(ht[:, :], tp[:, 0:D]).then_inc(turned_out, 1)

            each(act, NT, step)

        @block.tensor
        def _(pe):
            pe.wait_ge(loaded, 32)

            def step(i):
                pe.wait_ge(taken, i + 1)
                pe.transpose(tp[:, 0:D], hs[:, :], k["ident"][:, :]).then_inc(turned, 1)
                pe.wait_ge(turned_out, i + 1)
                for g in range(K):
                    past(pe, made[g % HK], i * 2 + g // HK)
                    pe.matmul(mm[g % HK][:, :, :], ht[:, :], wr[:, g * GR:(g + 1) * GR, :], start=True, stop=True
                              ).then_inc(product, 1)

            each(pe, NT, step)

        @block.vector
        def _(v):
            v.wait_ge(loaded, 32)

            def step(i):
                for g in range(K):
                    h = g // HK
                    if g % HK == 0:
                        past(v, stored[h], i * 16)
                    v.wait_ge(product, i * K + g + 1)
                    v.tensor_tensor(out[:, h, (g % HK) * GR:(g % HK + 1) * GR, :], mm[g % HK][:, :, :],
                                    feat[:, g * GR:(g + 1) * GR, :], ALU.add).then_inc(made[g % HK], 1)

            each(v, NT, step)


SQUARE = {1: 0, 2: 1, 3: 3, 4: 4}


def gnn_kernel(nc, d):
    with Space(nc, "kept") as s:
        k = {}
        k["meta"] = s.sb("meta", [P, 5, T])
        for name in ("ident", "before", "iota"):
            k[name] = s.sb(name, [P, P])
        for name in ("identb", "iotab"):
            k[name] = s.sb(name, [P, P], BF16)
        for name in ("dlo", "dhi", "slo", "shi", "dst", "loc", "loc2", "start", "w2", "real"):
            k[name] = s.sb(name, [P, T])
        for name in ("src", "relsrc", "idx2"):
            k[name] = s.sb(name, [P, T], I32)
        for name in ("start_i", "start2_i"):
            k[name] = s.sb(name, [1, T], I32)
        k["rec2"] = s.sb("rec2", [P, T, RW2])
        for name in ("deg_dst", "deg_src", "weight_src"):
            k[name] = s.sb(name, [P, NT])
        k["base"], k["part"], k["eps"] = s.sb("base", [P, 2, NT]), s.sb("part", [P, 1]), s.sb("eps", [P, 1])
        k["mean"] = s.sb("mean", [DE, 1])
        k["wedge"] = s.sb("wedge", [DE + 1, D])
        k["par"] = s.sb("par", [P, PARS, D])
        k["x"], k["h"] = s.sb("x", [P, NT, D]), s.sb("h", [P, NT, D])
        k["alpha"] = s.sb("alpha", [P, T, H])
        count_phase(nc, d, k)
        sort_phase(nc, d, k)
        enter_phase(nc, d, k)
        score_phase(nc, d, k)
        softmax_phase(nc, d, k)
        k["agg"], k["den"] = s.sb("agg", [P, NP + P]), s.sb("den", [H, NP + P])
        run_sum_phase(nc, d, k, "gat", "leftsrc", None)
        node_phase(nc, d, k, 0)
        relation_phase(nc, d, k)
        run_sum_phase(nc, d, k, "rel", "relation", "relsrc", "real")
        node_phase(nc, d, k, 1, table="table")
        run_sum_phase(nc, d, k, "avg", "table", "idx2", "w2", loc="loc2", start="start2_i")
        node_phase(nc, d, k, 2, table="table2")
        run_sum_phase(nc, d, k, "conv1", "table2", "src", "real")
        node_phase(nc, d, k, 3, table="table3")
        run_sum_phase(nc, d, k, "conv2", "table3", "src", "real")
        node_phase(nc, d, k, 4)


def kernel(**inputs):
    import numpy as np
    import concourse.bacc as bacc
    from concourse.bass_utils import run_bass_kernel_spmd

    z = {n: np.asarray(a) for n, a in inputs.items()}
    loops, pad = np.arange(NP, dtype=np.int32), EP - E
    rest = pad + NP
    l0 = lambda n: z["L0_gnn_" + n]
    arrays = {
        "x": np.concatenate([z["x"], np.zeros((NP - N, D), np.float32)]),
        "src": np.concatenate([z["src"], np.full(pad, N, np.int32), loops]),
        "dst": np.concatenate([z["dst"], np.full(pad, N, np.int32), loops]),
        "type": np.concatenate([z["edge_type_40"], np.zeros(rest, np.int32)]),
        "weight": np.concatenate([z["edge_weight"], np.ones(pad, np.float32), np.zeros(N, np.float32),
                                  np.ones(NP - N, np.float32)]),
        "attr": np.concatenate([z["edge_attr_32"], np.zeros((rest, DE), np.float32)]),
        "wlr": np.concatenate([l0("W_l"), l0("W_r")], axis=1),
        "we": l0("W_e"),
        "w1": l0("W1"),
        "w2": l0("W2"),
        "b1": np.ascontiguousarray(l0("b1").reshape(2, D).T),
        "par": np.stack([l0("ln1_g"), l0("ln1_b"), l0("ln2_g"), l0("ln2_b"), l0("att").reshape(D), l0("bias"), l0("b2"),
                         z["L2_gnn_b1"], z["L2_gnn_b2"], z["L3_gnn_b1"], z["L3_gnn_b2"]]),
        "wr": z["L1_gnn_relation_weights"],
        "feat": z["L1_gnn_rFeatures"],
        "square": np.stack([z["L1_gnn_loop_weight"], z["L2_gnn_W2"].T, z["L2_gnn_W1"].T, z["L3_gnn_W1"], z["L3_gnn_W2"]]),
    }
    arrays = {f"in_{n}": np.ascontiguousarray(a) for n, a in arrays.items()}
    nc = bacc.Bacc("TRN2", target_bir_lowering=False, num_devices=1)
    d = {n[3:]: nc.dram_tensor(n, a.shape, mybir.dt.from_np(a.dtype), kind="ExternalInput").ap() for n, a in arrays.items()}
    for name, rows, width in (("records", TE, RW), ("records2", TE, RW2), ("left", NP, D), ("right", NP + P, D), ("leftsrc", TE, D), ("relation", NP * R, D),
                              ("table", NP, D), ("table2", NP, D), ("table3", NP, D)):
        d[name] = nc.dram_tensor(name, (rows, width), F32, kind="Internal").ap()
    d["out"] = nc.dram_tensor("out_x", (NP, D), F32, kind="ExternalOutput").ap()
    gnn_kernel(nc, d)
    r = run_bass_kernel_spmd(nc, [arrays], core_ids=[0])
    return r.results[0]["out_x"][:N]
```

```python
from contextlib import ExitStack

import concourse.bass as bass
from concourse import mybir

F32 = mybir.dt.float32
BF16 = mybir.dt.bfloat16
F16 = mybir.dt.float16
I32 = mybir.dt.int32
ALU = mybir.AluOpType
ACT = mybir.ActivationFunctionType
AX = mybir.AxisListType

P = 128
D = 128
N = 3125
NT = -(-N // P)
NP = NT * P
E = 50000
ET = -(-E // P)
EP = ET * P
T = ET + NT
TE = T * P
LN1_G, LN1_B, LN2_G, LN2_B, ATT, BIAS, L0_B2, L2_B1, L2_B2, L3_B1, L3_B2 = range(11)
PARS = 11
H, C = 8, 16
DE = 32
R = 40
EPS = 1e-5
SLOPE = 0.2
RW = DE + 5
SELF, WEIGHT, TYPE, DST, SRC = range(5)
MIDDLE = NP // 2
assert MIDDLE <= 2048 and TE <= 65536
MW = D + 1
FAR = 1e30
G = 4
U = 2 * G
SLOTS = 4
NB = 5
CH = P // H
CT = T // CH
CL = CT * P
assert NT % 2 == 1 and T == CH * CT and T % (2 * G) == 0 and T % (SLOTS * U) == 0 and NT % NB == 0


class Space:

    def __init__(self, nc, name):
        self.nc, self.name, self.ctx, self.sems = nc, name, ExitStack(), []
        self.blocks = ExitStack()

    def __enter__(self):
        return self

    def __exit__(self, *a):
        self.blocks.close()
        if self.sems:
            self.nc.clear_and_free_semaphores(self.sems)
            self.nc.all_engine_barrier()
        self.ctx.close()

    def sb(self, name, shape, dt=F32):
        return self.ctx.enter_context(self.nc.sbuf_tensor(f"{self.name}_{name}", shape, dt))

    def ps(self, name, shape, dt=F32):
        return self.ctx.enter_context(self.nc.psum_tensor(f"{self.name}_{name}", shape, dt))

    def sem(self, name):
        self.sems.append(self.nc.alloc_semaphore(f"{self.name}_{name}"))
        return self.sems[-1]

    def block(self):
        return self.blocks.enter_context(self.nc.Block())


def bc(ap, shape, axis):
    return ap.unsqueeze(axis).to_broadcast(shape)


def hold(eng):
    eng.nop(nofuse=True)


def past(eng, sem, value):
    if not isinstance(value, int) or value > 0:
        eng.wait_ge(sem, value)


def each(eng, n, body):
    body(0)
    with eng.Fori(1, n) as i:
        body(i)


def each_ahead(eng, n, body):
    body(0, False)
    with eng.Fori(1, n - 1) as i:
        body(i, False)
    body(n - 1, True)


def node_registers(nc, engine, nodes):
    return nc.values_load_multi_w_load_instructions(
        nodes, engines=[engine], min_val=0, max_val=NP - 1,
        skip_runtime_bounds_check_because="a run's node is an edge's end or a self-loop's: below NP")[1]


def number(i, h, b=0):
    return (i * SLOTS + h) * 2 + b


def reused(i, h):
    return number(i - 1, h) + 2


def ring(i, last, lead=2):
    for h in range(SLOTS):
        for b in range(2):
            over = None if last else (i + 1, 0, 0)
            yield ((i, h, b), (i, h, 1) if b == 0 else (i, h + 1, 0) if h + 1 < SLOTS else over,
                   None if b == 1 else (i, h + lead) if h + lead < SLOTS else None if last else (i + 1, h + lead - SLOTS))


class Histogram:

    def __init__(self, s, k, table, B, parts=None):
        self.k, self.table, self.B, self.parts = k, table, B, parts
        self.oh, self.ohh = s.sb("hoh", [P, 2, B, P], BF16), s.sb("hohh", [P, 2, B, NT], BF16)
        self.ohw = s.sb("hohw", [P, 2, B, 3, NT], BF16) if parts is not None else None
        self.sum, self.sum3 = s.sb("hsum", [P, NT]), s.sb("hsum3", [P, 3 * NT])
        self.tot, self.run = s.sb("htot", [P, NT]), s.sb("hrun", [P, NT])
        self.bank, self.out = s.ps("hbank", [P, 512]), s.ps("hout", [P, 512])
        self.width = 4 * NT if parts is not None else NT
        self.rows, self.counted = s.sem("hrows"), s.sem("hcounted")
        self.total, self.taken, self.prefix, self.step = (s.sem(x) for x in ("htotal", "htaken", "hprefix", "hstep"))
        self.minus, self.far = s.sb("hminus", [P, 2, B]), s.sb("hfar", [P, 2, B, P])
        self.small, self.distant, self.scalar_rows = s.sem("hsmall"), s.sem("hdistant"), s.sem("hscalar_rows")
        self.steps = 2 if parts is not None else 1


    def onehot(self, v, q, p):
        at = bass.ds(q * self.B, self.B)
        past(v, self.counted, q - 1)
        if self.parts is None:
            v.tensor_tensor(self.oh[:, p], bc(self.table["lo"][:, at], [P, self.B, P], 2),
                            bc(self.k["iota"][:, :], [P, self.B, P], 1), ALU.is_equal)
        v.tensor_tensor(self.ohh[:, p], bc(self.table["hi"][:, at], [P, self.B, NT], 2),
                        bc(self.k["iota"][:, 0:NT], [P, self.B, NT], 1), ALU.is_equal).then_inc(self.rows, 1)
        if self.parts is not None:
            shape = [P, self.B, 3, NT]
            v.wait_ge(self.rows, 2 * q + 1)
            v.tensor_tensor(self.ohw[:, p], bc(self.ohh[:, p], shape, 2), bc(self.parts[:, at, :], shape, 3), ALU.mult
                            ).then_inc(self.rows, 1)

    def bases(self, v, base, degree, weight=None):
        v.wait_ge(self.total, 1)
        v.tensor_copy(self.sum[:, :], self.bank[:, 0:NT]).then_inc(self.taken, 1)
        if weight is not None:
            v.tensor_copy(self.sum3[:, :], self.bank[:, NT:4 * NT]).then_inc(self.step, 1)
        else:
            v.memset(self.sum3[:, :], 0.0).then_inc(self.step, 1)
        v.wait_ge(self.prefix, 1)
        v.tensor_copy(self.tot[:, :], self.out[:, NT:2 * NT]).then_inc(self.step, 1)
        v.wait_ge(self.step, 2)
        v.tensor_tensor_scan(self.run[:, :], self.k["ones"][:, 0:NT], self.tot[:, :], 0.0, ALU.mult, ALU.add
                             ).then_inc(self.step, 1)
        v.wait_ge(self.step, 3)
        v.tensor_tensor(self.run[:, :], self.run[:, :], self.tot[:, :], ALU.subtract).then_inc(self.step, 1)
        v.wait_ge(self.step, 4)
        v.tensor_tensor(base, self.run[:, :], self.out[:, 0:NT], ALU.add)
        v.wait_ge(self.taken, 1)
        v.tensor_scalar(degree, self.sum[:, :], -1.0, None, ALU.add)
        if weight is not None:
            v.tensor_reduce(weight, self.sum3[:, :].rearrange("p (c t) -> p t c", c=3), AX.X, ALU.add)


    def scalar_onehot(self, act, q, p):
        past(act, self.distant, q - 1)
        act.mul(self.minus[:, p], self.table["lo"][:, bass.ds(q * self.B, self.B)], -1.0).then_inc(self.small, 1)
        act.wait_ge(self.small, q + 1)
        past(act, self.scalar_rows, q - 1)
        for u in range(self.B):
            m = act.activation(self.far[:, p, u, :], self.k["iota"][:, :], ACT.Abs, bias=self.minus[:, p, u:u + 1])
        m.then_inc(self.distant, 1)
        act.wait_ge(self.distant, q + 1)
        past(act, self.counted, q - 1)
        act.activation(self.oh[:, p], self.far[:, p], ACT.Relu, scale=-1.0, bias=1.0).then_inc(self.scalar_rows, 1)


    def open(self, pe):
        pe.matmul(self.bank[:, 0:self.width], self.k["zerob"][:, :], self.k["zerob"][:, 0:self.width], start=True, stop=False)

    def add(self, pe, q, p):
        pe.wait_ge(self.rows, q * self.steps + 1)
        if self.parts is not None:
            pe.wait_ge(self.scalar_rows, q + 1)
        for u in range(self.B):
            m = pe.matmul(self.bank[:, 0:NT], self.oh[:, p, u, :], self.ohh[:, p, u, :],
                          start=False, stop=False, skip_group_check=True)
        if self.parts is not None:
            pe.wait_ge(self.rows, q * 2 + 2)
            for u in range(self.B):
                m = pe.matmul(self.bank[:, NT:4 * NT], self.oh[:, p, u, :], self.ohw[:, p, u].rearrange("p c t -> p (c t)"),
                              start=False, stop=False, skip_group_check=True)
        m.then_inc(self.counted, 1)

    def close(self, pe):
        pe.matmul(self.bank[:, 0:self.width], self.k["zerob"][:, :], self.k["zerob"][:, 0:self.width], start=False, stop=True
                  ).then_inc(self.total, 1)
        pe.wait_ge(self.taken, 1)
        pe.matmul(self.out[:, 0:NT], self.k["upper"][:, :], self.sum[:, :], start=True, stop=True)
        pe.matmul(self.out[:, NT:2 * NT], self.k["ones"][:, :], self.sum[:, :], start=True, stop=True).then_inc(self.prefix, 1)


def count_phase(nc, d, k):
    B = 16
    with Space(nc, "count") as s:
        diff_i, part_i, flat_i = s.sb("diff_i", [P, P], I32), s.sb("part_i", [P, 1], I32), s.sb("flat_i", [P, T], I32)
        diff = s.sb("diff", [P, P])
        part = s.sb("part", [P, 1])
        flat = s.sb("flat", [P, T])
        raw = s.sb("raw", [P, 3, T], I32)
        lohi_i = s.sb("lohi_i", [P, 4, T], I32)
        loaded, kept = s.sem("loaded"), s.sem("kept")
        iotas = s.sem("iotas")
        made = s.sem("made")
        consts, split = s.sem("consts"), s.sem("split")
        hist = Histogram(s, k, {x: k[x][:, 0, :] for x in ("lo", "hi")}, B)
        block = s.block()
        n = T // (2 * B)
        MADE = 16

        @block.sync
        def _(sp):
            for j, name in enumerate(("dst", "src", "type")):
                sp.dma_start(raw[:, j, :], d[name].rearrange("(p t) -> p t", p=P)).then_inc(loaded, 16)
            sp.dma_start(k["meta"][:, WEIGHT, :], d["weight"].rearrange("(p t) -> p t", p=P)).then_inc(loaded, 16)
            sp.dma_start(k["x"][:, :, :], d["x"].rearrange("(a l) w -> l a w", l=P)).then_inc(kept, 16)
            sp.dma_start(k["wlr"][:, :], d["wlr"]).then_inc(kept, 16)
            sp.dma_start(k["we"][:, :], d["we"]).then_inc(kept, 16)
            sp.dma_start(k["par"][:, :, :], d["par"].rearrange("(o a) w -> o a w", o=1).to_broadcast([P, PARS, D])
                         ).then_inc(kept, 16)
            sp.dma_start(k["w1"][:, :], d["w1"]).then_inc(kept, 16)
            sp.dma_start(k["w2"][:, :, :], d["w2"].rearrange("(f p) w -> p f w", p=P)).then_inc(kept, 16)
            sp.dma_start(k["b1"][:, :], d["b1"]).then_inc(kept, 16)
            sp.dma_start(k["square"][:, :, :], d["square"].rearrange("m p w -> p m w")).then_inc(kept, 16)
            sp.wait_ge(loaded, 64)
            sp.wait_ge(kept, 128)

        @block.gpsimd
        def _(pool):
            pool.iota(diff_i[:, :], pattern=[[1, P]], base=0, channel_multiplier=-1).then_inc(iotas, 1)
            pool.iota(part_i[:, :], pattern=[[1, 1]], base=0, channel_multiplier=1).then_inc(iotas, 1)
            pool.iota(flat_i[:, :], pattern=[[1, T]], base=0, channel_multiplier=T).then_inc(iotas, 1)

        @block.vector
        def _(v):
            v.memset(k["zerob"][:, :], 0.0).then_inc(consts, 1)
            v.memset(k["ones"][:, :], 1.0).then_inc(consts, 1)
            v.wait_ge(iotas, 3)
            v.tensor_copy(diff[:, :], diff_i[:, :]).then_inc(made, 1)
            v.tensor_copy(part[:, :], part_i[:, :])
            v.tensor_copy(k["part"][:, :], part_i[:, :]).then_inc(made, 1)
            v.tensor_copy(flat[:, :], flat_i[:, :]).then_inc(made, 1)
            v.wait_ge(loaded, 64)
            for j, f in enumerate((DST, SRC, TYPE)):
                v.tensor_copy(k["meta"][:, f, :], raw[:, j, :]).then_inc(made, 1)
            for j in range(2):
                v.tensor_scalar(lohi_i[:, 2 * j, :], raw[:, j, :], P - 1, None, ALU.bitwise_and).then_inc(made, 1)
                v.tensor_scalar(lohi_i[:, 2 * j + 1, :], raw[:, j, :], 7, None, ALU.arith_shift_right).then_inc(made, 1)
            v.wait_ge(made, 10)
            v.tensor_scalar(k["ident"][:, :], diff[:, :], 0.0, None, ALU.is_equal).then_inc(made, 1)
            v.tensor_scalar(k["identb"][:, :], diff[:, :], 0.0, None, ALU.is_equal).then_inc(made, 1)
            v.tensor_scalar(k["identh"][:, :], diff[:, :], 0.0, None, ALU.is_equal)
            v.tensor_scalar(k["before"][:, :], diff[:, :], 0.0, None, ALU.is_lt).then_inc(made, 1)
            v.tensor_scalar(k["upper"][:, :], diff[:, :], 0.0, None, ALU.is_gt).then_inc(made, 1)
            v.tensor_scalar(k["iota"][:, :], diff[:, :], part[:, 0:1], None, ALU.add).then_inc(made, 1)
            v.wait_ge(made, 15)
            v.tensor_copy(k["iotab"][:, :], k["iota"][:, :]).then_inc(made, 1)
            v.tensor_scalar(k["meta"][:, SELF, :], flat[:, :], float(EP), None, ALU.is_ge)
            v.tensor_copy(k["lo"][:, :, :], lohi_i[:, ::2, :])
            v.tensor_scalar(k["mid"][:, :], k["meta"][:, DST, :], -MIDDLE, None, ALU.add)
            v.tensor_scalar(k["midh"][:, :], k["meta"][:, DST, :], -MIDDLE, None, ALU.add)
            v.tensor_copy(k["hi"][:, :, :], lohi_i[:, 1::2, :]).then_inc(made, 1)
            v.wait_ge(made, MADE + 1)

            def batches(i):
                for p in range(2):
                    hist.onehot(v, 2 * i + p, p)

            each(v, n, batches)
            rest = k["meta"][:, WEIGHT, :]
            for c in range(3):
                v.tensor_copy(k["wpart"][:, :, c], rest).then_inc(split, 1)
                v.wait_ge(split, 2 * c + 1)
                if c < 2:
                    v.tensor_tensor(k["wrest"][:, :, c], rest, k["wpart"][:, :, c], ALU.subtract).then_inc(split, 1)
                    v.wait_ge(split, 2 * c + 2)
                    rest = k["wrest"][:, :, c]
            hist.bases(v, k["base"][:, 0, :], k["deg_dst"][:, :])

        @block.tensor
        def _(pe):
            pe.wait_ge(consts, 2)
            hist.open(pe)

            def batches(i):
                for p in range(2):
                    hist.add(pe, 2 * i + p, p)

            each(pe, n, batches)
            pe.wait_ge(made, MADE)
            hist.close(pe)


class Order:

    def __init__(self, s, k, table, base0):
        self.k, self.table, self.base0 = k, table, base0
        self.midh, self.mid, self.locol = s.sb("midh", [P, 2, G], F16), s.sb("mid", [P, 2, G]), s.sb("locol", [P, 2, G])
        self.oh, self.ohh = s.sb("oh", [P, 2, G, P], BF16), s.sb("ohh", [P, 2, G, NT], BF16)
        self.base = s.sb("base", [P, 2, G, NT])
        self.base_hi, self.base_lo = s.sb("base_hi", [P, 2, G, NT], BF16), s.sb("base_lo", [P, 2, G, NT], BF16)
        self.oht, self.junk, self.junk2 = s.sb("oht", [P, G, P], BF16), s.sb("junk", [P, G, P]), s.sb("junk2", [P, G, NT])
        self.inside, self.outside = s.sb("inside", [P, G]), s.sb("outside", [P, G])
        self.rowb = [s.ps(f"rowb{p}", [P, G, P]) for p in range(2)]
        self.tr = s.ps("tr", [P, G, P], BF16)
        taken, got = s.ps("taken", [P, 512]), s.ps("got", [P, 512])
        self.taken, self.got = (x[:, 0:G * NT].rearrange("p (u t) -> p u t", t=NT) for x in (taken, got))
        self.cols, self.turned, self.rounded = s.sem("ocols"), s.sem("oturned"), s.sem("orounded")
        self.onehots, self.based, self.split, self.counted = (s.sem(x) for x in ("oonehots", "obased", "osplit", "ocounted"))
        self.chosen, self.outer, self.placed = (s.sem(x) for x in ("ochosen", "oouter", "oplaced"))
        self.prepared, self.looked = s.sem("oprepared"), s.sem("olooked")


    def begin(self, v):
        v.tensor_copy(self.base[:, 1, G - 1, :], self.base0).then_inc(self.based, 1)
        v.wait_ge(self.rounded, 1)
        v.wait_ge(self.based, 1)
        v.tensor_tensor(self.base_lo[:, 1, G - 1], self.base[:, 1, G - 1], self.base_hi[:, 1, G - 1], ALU.subtract
                        ).then_inc(self.split, 1)

    def onehot(self, v, g, p):
        v.wait_ge(self.cols, g + 1)
        past(v, self.prepared, g - 1)
        v.tensor_tensor(self.ohh[:, p], bc(self.table["hi"][:, bass.ds(g * G, G)], [P, G, NT], 2),
                        bc(self.k["iotab"][:, 0:NT], [P, G, NT], 1), ALU.is_equal)
        for u in range(G):
            w = v.tensor_scalar(self.oh[:, p, u, :], self.k["iotab"][:, :], self.locol[:, p, u:u + 1], None, ALU.is_equal)
        w.then_inc(self.onehots, 1)

    def add_bases(self, v, g, p):
        v.wait_ge(self.prepared, g + 1)
        v.wait_ge(self.based, g + 1)
        past(v, self.split, g)
        v.tensor_tensor(self.base[:, p], self.taken, bc(self.base[:, 1 - p, G - 1, :], [P, G, NT], 1), ALU.add
                        ).then_inc(self.based, 1)

    def count(self, v, g, p, tiles):
        past(v, self.placed, g)
        for u in tiles:
            v.scalar_tensor_tensor(self.junk[:, u, :], self.rowb[p][:, u, :], self.mid[:, p, u:u + 1], self.k["before"][:, :],
                                   ALU.is_equal, ALU.mult, accum_out=self.inside[:, u:u + 1]).then_inc(self.counted, 1)

    def rest(self, v, g, p):
        v.wait_ge(self.rounded, g + 2)
        past(v, self.looked, g - 1)
        v.tensor_tensor(self.base_lo[:, p], self.base[:, p], self.base_hi[:, p], ALU.subtract).then_inc(self.split, 1)

    def choose(self, v, g, p, place):
        v.wait_ge(self.looked, g + 1)
        v.wait_ge(self.onehots, g + 1)
        v.tensor_tensor(self.junk2[:, :, :], self.got, self.ohh[:, p], ALU.mult).then_inc(self.chosen, 1)
        v.wait_ge(self.chosen, g + 1)
        v.tensor_reduce(self.outside[:, :], self.junk2[:, :, :], AX.X, ALU.add).then_inc(self.outer, 1)
        v.wait_ge(self.outer, g + 1)
        v.wait_ge(self.counted, (g + 1) * G)
        v.tensor_tensor(place, self.inside[:, :], self.outside[:, :], ALU.add).then_inc(self.placed, 1)


    def prepare(self, pe, g, p):
        pe.wait_ge(self.cols, g + 1)
        past(pe, self.counted, (g - 1) * G)
        for u in range(G):
            pe.matmul(self.rowb[p][:, u, :], self.midh[:, p, u:u + 1].to_broadcast([P, P]), self.k["identh"][:, :],
                      start=True, stop=True)
        pe.wait_ge(self.onehots, g + 1)
        past(pe, self.turned, g)
        for u in range(G):
            pe.transpose(self.tr[:, u, :], self.oh[:, p, u, :], self.k["identb"][:, :])
        pe.wait_ge(self.based, g + 1)
        for u in range(G):
            for a in range(u + 1):
                m = pe.matmul(self.taken[:, u, :], self.oh[:, p, a, :], self.ohh[:, p, a, :], start=(a == 0), stop=(a == u))
        m.then_inc(self.prepared, 1)

    def look(self, pe, g, p):
        pe.wait_ge(self.turned, g + 1)
        pe.wait_ge(self.split, g + 2)
        past(pe, self.chosen, g)
        for u in range(G):
            for part in (self.base_hi, self.base_lo):
                m = pe.matmul(self.got[:, u, :], self.oht[:, u, :], part[:, p, u - 1, :] if u else part[:, 1 - p, G - 1, :],
                              start=part is self.base_hi, stop=part is self.base_lo)
        m.then_inc(self.looked, 1)


    def columns(self, act, g, p):
        at = bass.ds(g * G, G)
        past(act, self.onehots, g - 1)
        past(act, self.counted, (g - 1) * G)
        past(act, self.prepared, g - 1)
        act.copy(self.midh[:, p], self.table["midh"][:, at])
        act.copy(self.mid[:, p], self.table["mid"][:, at])
        act.copy(self.locol[:, p], self.table["lo"][:, at]).then_inc(self.cols, 1)

    def round_first(self, act):
        act.wait_ge(self.based, 1)
        act.copy(self.base_hi[:, 1, G - 1], self.base[:, 1, G - 1]).then_inc(self.rounded, 1)

    def turn(self, act, g, p):
        act.wait_ge(self.based, g + 2)
        past(act, self.looked, g - 1)
        act.copy(self.base_hi[:, p], self.base[:, p]).then_inc(self.rounded, 1)
        act.wait_ge(self.prepared, g + 1)
        past(act, self.looked, g)
        act.copy(self.oht[:, :, :], self.tr[:, :, :]).then_inc(self.turned, 1)


def sort_phase(nc, d, k):
    with Space(nc, "sort") as s:
        attr = s.sb("attr", [P, T, DE])
        asum = s.sb("asum", [P, DE])
        ones = s.sb("ones", [P, 1])
        place = s.sb("place", [P, 2, G], I32)
        rec = s.sb("rec", [P, 2, G, RW])
        loaded, summed, meaned, ready = s.sem("loaded"), s.sem("summed"), s.sem("meaned"), s.sem("ready")
        recs = s.sem("recs")
        sent = [s.sem(f"sent{p}") for p in range(2)]
        order = Order(s, k, dict(lo=k["lo"][:, 0, :], hi=k["hi"][:, 0, :], mid=k["mid"], midh=k["midh"]), k["base"][:, 0, :])
        hist = Histogram(s, k, {x: k[x][:, 1, :] for x in ("lo", "hi")}, G, k["wpart"])
        mean = hist.out[0:DE, 2 * NT:2 * NT + 1]
        block = s.block()
        n = T // (2 * G)

        def groups(i, last):
            return (2 * i, 0, (2 * i + 1, 1)), (2 * i + 1, 1, None if last else (2 * i + 2, 0))

        @block.sync
        def _(sp):
            sp.dma_start(attr[:, :, :], d["attr"].rearrange("(p t) w -> p t w", p=P)).then_inc(loaded, 16)

        @block.vector
        def _(v):
            def body(i, last):
                for g, p, nxt in groups(i, last):
                    if nxt:
                        order.onehot(v, *nxt)
                    order.add_bases(v, g, p)
                    order.count(v, g, p, range(2))
                    order.rest(v, g, p)
                    order.count(v, g, p, range(2, G))
                    hist.onehot(v, g, p)
                    past(v, sent[p], i * (16 * G))
                    order.choose(v, g, p, place[:, p, :])

            v.memset(ones[:, :], 1.0).then_inc(ready, 1)
            order.begin(v)
            order.onehot(v, 0, 0)
            each_ahead(v, n, body)
            hist.bases(v, k["base"][:, 1, :], k["deg_src"][:, :], k["weight_src"][:, :])
            v.wait_ge(loaded, 16)
            v.tensor_reduce(asum[:, :], attr[:, :, :].rearrange("p t w -> p w t"), AX.X, ALU.add).then_inc(summed, 1)
            v.wait_ge(meaned, 1)
            v.tensor_scalar(k["mean"][:, :], mean, 1.0 / E, None, ALU.mult).then_inc(summed, 1)

        @block.tensor
        def _(pe):
            def body(i, last):
                for g, p, nxt in groups(i, last):
                    order.look(pe, g, p)
                    if nxt:
                        order.prepare(pe, *nxt)
                    if not isinstance(g, int) or g > 0:
                        hist.add(pe, g - 1, 1 - p)

            hist.open(pe)
            order.prepare(pe, 0, 0)
            each_ahead(pe, n, body)
            hist.add(pe, 2 * n - 1, 1)
            hist.close(pe)
            pe.wait_ge(ready, 1)
            pe.wait_ge(summed, 1)
            pe.matmul(mean, asum[:, :], ones[:, :], start=True, stop=True).then_inc(meaned, 1)

        @block.scalar
        def _(act):
            def body(i, last):
                for g, p, nxt in groups(i, last):
                    order.turn(act, g, p)
                    at = bass.ds(g * G, G)
                    past(act, sent[p], i * (16 * G))
                    act.copy(rec[:, p, :, 0:DE], attr[:, at, :])
                    act.copy(rec[:, p, :, DE:RW], k["meta"][:, :, at].rearrange("p f t -> p t f")).then_inc(recs, 1)
                    if not last:
                        order.columns(act, g + 2, p)
                    hist.scalar_onehot(act, g, p)

            order.columns(act, 0, 0)
            order.columns(act, 1, 1)
            order.round_first(act)
            act.wait_ge(loaded, 16)
            each_ahead(act, n, body)

        @block.gpsimd
        def _(pool):
            def step(i):
                for p in range(2):
                    pool.wait_ge(order.placed, 2 * i + p + 1)
                    pool.wait_ge(recs, 2 * i + p + 1)
                    hold(pool)
                    for u in range(G):
                        pool.indirect_dma_start(
                            out=d["records"][:, :], out_offset=bass.IndirectOffsetOnAxis(ap=place[:, p, u:u + 1], axis=0),
                            in_=rec[:, p, u, :], in_offset=None).then_inc(sent[p], 16)

            each(pool, n, step)
            for p in range(2):
                pool.wait_ge(sent[p], n * 16 * G)


def norm_tensors(s, name):
    return dict(stats=s.sb(f"{name}_stats", [P, NB, 6]), mv=s.sb(f"{name}_mv", [P, NB, 2]), sd=s.sb(f"{name}_sd", [P, NB]),
                rs=s.sb(f"{name}_rs", [P, NB]), have_stats=s.sem(f"{name}_have_stats"), have_mv=s.sem(f"{name}_have_mv"),
                have_sd=s.sem(f"{name}_have_sd"), have_rs=s.sem(f"{name}_have_rs"), normed=s.sem(f"{name}_normed"))


def norm_stats(v, q, i, x):
    for u in range(NB):
        w = v.bn_stats(q["stats"][:, u, :], x[:, u, :])
    w.then_inc(q["have_stats"], 1)
    v.wait_ge(q["have_stats"], i + 1)
    hold(v)
    for u in range(NB):
        w = v.bn_aggr(q["mv"][:, u, :], q["stats"][:, u, :])
    w.then_inc(q["have_mv"], 1)


def norm_apply(v, q, i, x, out):
    v.wait_ge(q["have_sd"], i + 1)
    v.reciprocal(q["rs"][:, :], q["sd"][:, :]).then_inc(q["have_rs"], 1)
    v.wait_ge(q["have_rs"], i + 1)
    for u in range(NB):
        w = v.tensor_scalar(out[:, u, :], x[:, u, :], q["mv"][:, u, 0:1], q["rs"][:, u:u + 1], ALU.subtract, ALU.mult)
    w.then_inc(q["normed"], 1)


def norm_vector(v, q, i, x, out):
    norm_stats(v, q, i, x)
    norm_apply(v, q, i, x, out)


def norm_scalar(act, q, i, k):
    act.wait_ge(q["have_mv"], i + 1)
    act.activation(q["sd"][:, :], q["mv"][:, :, 1], ACT.Sqrt, bias=k["eps"][:, 0:1]).then_inc(q["have_sd"], 1)


def rows_of(table, i):
    return table.rearrange("(a l) w -> l a w", l=P)[:, bass.ds(i * NB, NB), :]


def enter_phase(nc, d, k):
    with Space(nc, "enter") as s:
        aug = s.sb("aug", [DE, DE + 1])
        xs, h0, hn, ht = (s.sb(n, [P, NB, D]) for n in ("xs", "h0", "hn", "ht"))
        lr = s.sb("lr", [P, 2, NB, D])
        tp = s.ps("tp", [P, 8, D])
        mm = s.ps("mm", [P, 6, 2 * D])
        wa = s.ps("wa", [P, 512])
        fb = s.ps("fb", [P, 512])
        first, zero, one = s.sb("first", [1, T, 2]), s.sb("zero", [P, D]), s.sb("one", [1, P])
        firsts, zeroed, spread = s.sem("firsts"), s.sem("zeroed"), s.sem("spread")
        q1, q2 = norm_tensors(s, "n1"), norm_tensors(s, "n2")
        epsed = s.sem("epsed")
        augged, edged, kept = s.sem("augged"), s.sem("edged"), s.sem("kept")
        taken, relued, scaled = s.sem("taken"), s.sem("relued"), s.sem("scaled")
        affine, turned, turned_out = s.sem("affine"), s.sem("turned"), s.sem("turned_out")
        product, product_out, stored = s.sem("product"), s.sem("product_out"), s.sem("stored")
        block = s.block()
        n = NT // NB
        par = k["par"]

        @block.sync
        def _(sp):
            sp.dma_start(first[:, :, :], d["records"].rearrange("(t p) w -> p t w", p=P)[0:1, :, DE + TYPE:DE + DST + 1]
                         ).then_inc(firsts, 16)
            sp.wait_ge(zeroed, 1)
            for table in ("right", "table"):
                sp.dma_start(d[table][NP:NP + P, :], zero[:, :]).then_inc(firsts, 16)

            def step(i):
                sp.wait_ge(product_out, i + 1)
                sp.dma_start(rows_of(d["left"][0:NP], i), lr[:, 0]).then_inc(stored, 16)
                sp.dma_start(rows_of(d["right"][0:NP], i), lr[:, 1]).then_inc(stored, 16)

            each(sp, n, step)
            sp.wait_ge(stored, 32 * n)
            sp.wait_ge(firsts, 48)

        @block.vector
        def _(v):
            v.memset(k["eps"][:, :], EPS).then_inc(epsed, 1)
            v.memset(one[:, :], 1.0)
            v.memset(zero[:, :], 0.0).then_inc(zeroed, 1)
            v.tensor_copy(aug[:, 0:DE], k["ident"][0:DE, 0:DE])
            v.tensor_copy(aug[:, DE:DE + 1], k["mean"][:, :]).then_inc(augged, 1)

            def begin(i):
                past(v, q1["normed"], i)
                v.tensor_copy(xs[:, :, :], k["x"][:, bass.ds(i * NB, NB), :]).then_inc(taken, 1)
                v.wait_ge(taken, i + 1)
                norm_stats(v, q1, i, xs)

            def enter(i):
                past(v, q2["normed"], i)
                past(v, kept, i)
                norm_apply(v, q1, i, xs, h0)

            def take(i):
                v.wait_ge(product, i + 1)
                past(v, stored, i * 32)
                v.tensor_copy(lr[:, :, :, :].rearrange("p s a w -> p a s w"),
                              mm[:, 0:NB, :].rearrange("p a (s w) -> p a s w", s=2)).then_inc(product_out, 1)

            def step(i, last):
                v.wait_ge(relued, i + 1)
                norm_stats(v, q2, i, h0)
                if not last:
                    begin(i + 1)
                if not isinstance(i, int) or i > 0:
                    take(i - 1)
                past(v, turned, i)
                norm_apply(v, q2, i, h0, hn)
                v.wait_ge(q2["normed"], i + 1)
                v.tensor_tensor(hn[:, :, :], hn[:, :, :], bc(par[:, LN1_G, :], [P, NB, D], 1), ALU.mult).then_inc(scaled, 1)
                v.wait_ge(scaled, i + 1)
                v.tensor_tensor(hn[:, :, :], hn[:, :, :], bc(par[:, LN1_B, :], [P, NB, D], 1), ALU.add).then_inc(affine, 1)
                if not last:
                    enter(i + 1)

            begin(0)
            enter(0)
            each_ahead(v, n, step)
            take(n - 1)
            v.wait_ge(spread, 1)
            v.tensor_copy(k["start"][:, :], fb[:, 0:T])
            v.tensor_copy(k["start_i"][:, :], first[:, :, 1])

        @block.scalar
        def _(act):
            act.wait_ge(epsed, 1)
            def enter(i):
                act.wait_ge(q1["normed"], i + 1)
                act.activation(h0[:, :, :], h0[:, :, :], ACT.Relu).then_inc(relued, 1)
                act.wait_ge(relued, i + 1)
                act.copy(k["h"][:, bass.ds(i * NB, NB), :], h0[:, :, :]).then_inc(kept, 1)

            def step(i, last):
                norm_scalar(act, q2, i, k)
                if not last:
                    norm_scalar(act, q1, i + 1, k)
                act.wait_ge(turned, i + 1)
                past(act, product, i)
                act.copy(ht[:, :, :], tp[:, 0:NB, :]).then_inc(turned_out, 1)
                if not last:
                    enter(i + 1)

            norm_scalar(act, q1, 0, k)
            enter(0)
            each_ahead(act, n, step)
            act.wait_ge(edged, 1)
            act.copy(k["wedge"][:, :], wa[0:DE + 1, 0:D])

        @block.tensor
        def _(pe):
            def step(i):
                pe.wait_ge(affine, i + 1)
                for u in range(NB):
                    m = pe.transpose(tp[:, u, :], hn[:, u, :], k["ident"][:, :])
                m.then_inc(turned, 1)
                pe.wait_ge(turned_out, i + 1)
                past(pe, product_out, i)
                for u in range(NB):
                    m = pe.matmul(mm[:, u, :], ht[:, u, :], k["wlr"][:, :], start=True, stop=True)
                m.then_inc(product, 1)
            each(pe, n, step)
            pe.wait_ge(firsts, 48)
            pe.matmul(fb[:, 0:T], one[:, :], first[:, :, 1], start=True, stop=True).then_inc(spread, 1)
            pe.wait_ge(augged, 1)
            pe.matmul(wa[0:DE + 1, 0:D], aug[:, :], k["we"][:, :], start=True, stop=True).then_inc(edged, 1)


def score_phase(nc, d, k):
    with Space(nc, "score") as s:
        rec = s.sb("rec", [P, SLOTS, U, RW])
        ends = s.sb("ends", [P, SLOTS, U], I32)
        loc = s.sb("loc", [P, SLOTS, U], BF16)
        rows = s.sb("rows", [P, SLOTS, U, D])
        win = s.sb("win", [P, SLOTS, U, D])
        hot = s.sb("hot", [P, 2, G, P])
        at_sb = s.sb("at_sb", [DE + 1, 2, G, P])
        lk = s.sb("lk", [P, 2, G, D])
        yf, selfs = s.sb("yf", [P, SLOTS, U]), s.sb("selfs", [P, SLOTS, U])
        tp = [s.ps(f"tp{b}", [P, G, P]) for b in range(2)]
        rowb = [s.ps(f"rowb{b}", [P, G, P]) for b in range(2)]
        z = [s.ps(f"z{b}", [P, G, D]) for b in range(2)]
        slots = lambda name: [s.sem(f"{name}{h}") for h in range(SLOTS)]
        loaded, windows, cols, gathered, stored = (slots(x) for x in ("loaded", "windows", "cols", "gathered", "stored"))
        yready = s.sem("yready")
        turned, turned_out = s.sem("turned"), s.sem("turned_out")
        spread, hots = s.sem("spread"), s.sem("hots")
        summed, copied, leaky, weighed, scored = (s.sem(x) for x in ("summed", "copied", "leaky", "weighed", "scored"))
        block = s.block()
        n = T // (SLOTS * U)

        @block.sync
        def _(sp):
            def slots_of(i):
                for h in range(SLOTS):
                    q = i * SLOTS + h
                    at = bass.ds(q * U, U)
                    past(sp, scored, reused(i, h))
                    sp.dma_start(rec[:, h], d["records"].rearrange("(t p) w -> p t w", p=P)[:, at, :]
                                 ).then_inc(loaded[h], 16)
                    nodes = node_registers(nc, mybir.EngineType.SP, k["start_i"][0:1, at])
                    for u in range(U):
                        sp.dma_start(win[:, h, u, :], d["right"][bass.ds(nodes[u], P), :]).then_inc(windows[h], 16)

            each(sp, n, slots_of)

        @block.vector
        def _(v):
            def extract(i, h):
                at = bass.ds((i * SLOTS + h) * U, U)
                v.wait_ge(loaded[h], (i + 1) * 16)
                v.tensor_copy(ends[:, h, :], rec[:, h, :, DE + SRC])
                v.tensor_tensor(loc[:, h, :], rec[:, h, :, DE + DST], k["start"][:, at], ALU.subtract).then_inc(cols[h], 1)
                v.tensor_tensor(k["loc"][:, at], rec[:, h, :, DE + DST], k["start"][:, at], ALU.subtract)
                v.scalar_tensor_tensor(yf[:, h, :], rec[:, h, :, DE + SRC], float(R), rec[:, h, :, DE + TYPE],
                                       ALU.mult, ALU.add).then_inc(yready, 1)
                v.tensor_copy(k["src"][:, at], rec[:, h, :, DE + SRC])
                v.tensor_copy(k["w"][:, at], rec[:, h, :, DE + WEIGHT])
                v.tensor_copy(k["dst"][:, at], rec[:, h, :, DE + DST])
                v.scalar_tensor_tensor(selfs[:, h, :], rec[:, h, :, DE + SELF], -P, k["start"][:, at], ALU.mult, ALU.add
                                       ).then_inc(yready, 1)
                v.wait_ge(yready, (i * SLOTS + h + 1) * 2)
                v.tensor_copy(k["relsrc"][:, at], yf[:, h, :])
                v.tensor_tensor(k["away"][:, at], selfs[:, h, :], rec[:, h, :, DE + DST], ALU.subtract)

            def onehot(i, h, b):
                g = number(i, h, b)
                v.wait_ge(cols[h], i + 1)
                v.wait_ge(spread, g + 1)
                past(v, summed, g - 1)
                v.tensor_scalar(hot[:, b], rowb[b][:, :, :], k["part"][:, 0:1], None, ALU.is_equal).then_inc(hots, 1)

            def score(i, h, b):
                g = number(i, h, b)
                v.wait_ge(copied, g + 1)
                v.scalar_tensor_tensor(lk[:, b], lk[:, b], SLOPE, lk[:, b], ALU.mult, ALU.max).then_inc(leaky, 1)
                v.wait_ge(leaky, g + 1)
                v.tensor_tensor(lk[:, b], lk[:, b], bc(k["par"][:, ATT, :], [P, G, D], 1), ALU.mult).then_inc(weighed, 1)
                v.wait_ge(weighed, g + 1)
                v.tensor_reduce(k["alpha"][:, bass.ds(g * G, G), :], lk[:, b].rearrange("p g (h c) -> p g h c", h=H),
                                AX.X, ALU.add).then_inc(scored, 1)

            def body(i, last):
                for group, nxt, later in ring(i, last):
                    if nxt:
                        onehot(*nxt)
                    score(*group)
                    if later:
                        extract(*later)

            extract(0, 0)
            extract(0, 1)
            onehot(0, 0, 0)
            each_ahead(v, n, body)

        @block.gpsimd
        def _(pool):
            def slots_of(i):
                for h in range(SLOTS):
                    pool.wait_ge(cols[h], i + 1)
                    past(pool, scored, reused(i, h))
                    past(pool, stored[h], i * 16)
                    hold(pool)
                    for u in range(U):
                        pool.indirect_dma_start(
                            out=rows[:, h, u, :], out_offset=None, in_=d["left"][:, :],
                            in_offset=bass.IndirectOffsetOnAxis(ap=ends[:, h, u:u + 1], axis=0)
                        ).then_inc(gathered[h], 16)

            each(pool, n, slots_of)

        @block.tensor
        def _(pe):
            def prepare(i, h, b):
                g = number(i, h, b)
                pe.wait_ge(loaded[h], (i + 1) * 16)
                past(pe, turned_out, g - 1)
                hold(pe)
                for u in range(G):
                    m = pe.transpose(tp[b][0:DE + 1, u, :], rec[:, h, b * G + u, 0:DE + 1], k["ident"][:, :])
                m.then_inc(turned, 1)
                pe.wait_ge(cols[h], i + 1)
                past(pe, hots, g - 1)
                for u in range(G):
                    m = pe.matmul(rowb[b][:, u, :], loc[:, h, b * G + u:b * G + u + 1].to_broadcast([P, P]),
                                  k["identb"][:, :], start=True, stop=True)
                m.then_inc(spread, 1)

            def total(i, h, b):
                g = number(i, h, b)
                past(pe, copied, g - 1)
                pe.wait_ge(turned_out, g + 1)
                pe.wait_ge(hots, g + 1)
                if b == 0:
                    pe.wait_ge(windows[h], (i + 1) * (16 * U))
                    pe.wait_ge(gathered[h], (i + 1) * (16 * U))
                for u in range(G):
                    pe.matmul(z[b][:, u, :], at_sb[:, b, u, :], k["wedge"][:, :], start=True, stop=False)
                    pe.matmul(z[b][:, u, :], hot[:, b, u, :], win[:, h, b * G + u, :], start=False, stop=False)
                    m = pe.matmul(z[b][:, u, :], k["ident"][:, :], rows[:, h, b * G + u, :], start=False, stop=True)
                m.then_inc(summed, 1)

            def body(i, last):
                for group, nxt, later in ring(i, last):
                    if nxt:
                        prepare(*nxt)
                    total(*group)

            prepare(0, 0, 0)
            each_ahead(pe, n, body)

        @block.scalar
        def _(act):
            def copy_turned(i, h, b):
                g = number(i, h, b)
                act.wait_ge(turned, g + 1)
                past(act, summed, g - 1)
                act.copy(at_sb[:, b], tp[b][0:DE + 1]).then_inc(turned_out, 1)

            def body(i, last):
                for group, nxt, later in ring(i, last):
                    if nxt:
                        copy_turned(*nxt)
                    i, h, b = group
                    g = number(i, h, b)
                    act.wait_ge(summed, g + 1)
                    past(act, scored, g - 1)
                    act.copy(lk[:, b], z[b][:, :, :]).then_inc(copied, 1)
                    if b == 1:
                        act.wait_ge(gathered[h], (i + 1) * (16 * U))
                        act.dma_start(d["leftsrc"].rearrange("(t p) w -> p t w", p=P)[:, bass.ds((i * SLOTS + h) * U, U), :],
                                      rows[:, h]).then_inc(stored[h], 16)

            copy_turned(0, 0, 0)
            each_ahead(act, n, body)
            for h in range(SLOTS):
                act.wait_ge(stored[h], n * 16)


def softmax_phase(nc, d, k):
    with Space(nc, "softmax") as s:
        val, dst, run, back = (s.sb(x, [P, CT, P]) for x in ("val", "dst", "run", "back"))
        shut = s.sb("shut", [P, CL + 1])
        pack = s.sb("pack", [P, 2, CT, P])
        packed = s.sem("packed")
        one = s.sb("one", [1, 1])
        edge = s.sb("edge", [P, 4])
        lv, lk, lr, lf, lb = (s.sb(x, [1, 2 * P + 1]) for x in ("lv", "lk", "lr", "lf", "lb"))
        full = s.sb("full", [P, 2])
        tp = [s.ps(f"tp{b}", [P, 4, P]) for b in range(4)]
        line = s.ps("line", [1, 4, P])
        fullp = s.ps("fullp", [P, 512])
        turned, out = s.sem("turned"), s.sem("out")
        step = s.sem("step")
        lined, fulled = s.sem("lined"), s.sem("fulled")
        expd = s.sem("expd")
        turned2, out2 = s.sem("turned2"), s.sem("out2")
        block = s.block()
        n4 = -(-CT // 4)
        vf, df, rf, bf = (x[:, :, :].rearrange("p t e -> p (t e)") for x in (val, dst, run, back))

        @block.tensor
        def _(pe):
            pe.wait_ge(packed, 2)
            for q in range(2 * n4):
                if q >= 4:
                    pe.wait_ge(out, q - 3)
                for j in range(4 * (q // 2), min(CT, 4 * (q // 2) + 4)):
                    m = pe.transpose(tp[q % 4][:, j % 4, :], pack[:, q % 2, j, :], k["ident"][:, :])
                m.then_inc(turned, 1)
            pe.wait_ge(step, 5)
            for c in range(4):
                m = pe.transpose(line[:, c, :], edge[:, c:c + 1], k["ident"][:, :])
            m.then_inc(lined, 1)
            pe.wait_ge(step, 11)
            for c in range(2):
                m = pe.transpose(fullp[:, c:c + 1], lf[:, c * P:(c + 1) * P], one[:, :])
            m.then_inc(fulled, 1)
            for q in range(n4):
                pe.wait_ge(expd, q + 1)
                if q >= 4:
                    pe.wait_ge(out2, q - 3)
                for j in range(4 * q, min(CT, 4 * q + 4)):
                    m = pe.transpose(tp[q % 4][:, j % 4, :], val[:, j, :], k["ident"][:, :])
                m.then_inc(turned2, 1)

        @block.scalar
        def _(act):
            for q in range(2 * n4):
                a, b = 4 * (q // 2), min(CT, 4 * (q // 2) + 4)
                act.wait_ge(turned, q + 1)
                act.copy((val, dst)[q % 2][:, a:b, :], tp[q % 4][:, 0:b - a, :]).then_inc(out, 1)
            act.wait_ge(step, 17)
            for q in range(n4):
                a, b = 4 * q, min(CT, 4 * q + 4)
                act.activation(val[:, a:b, :], val[:, a:b, :], ACT.Exp).then_inc(expd, 1)

        @block.vector
        def _(v):
            v.tensor_copy(pack[:, 0].rearrange("p j (c h) -> p j c h", h=H),
                          k["alpha"][:, :, :].rearrange("p (c j) h -> p j c h", c=CH)).then_inc(packed, 1)
            v.tensor_copy(pack[:, 1].rearrange("p j (c h) -> p j c h", h=H),
                          k["dst"][:, :].rearrange("p (c j) -> p j c", c=CH).unsqueeze(3).to_broadcast([P, CT, CH, H])
                          ).then_inc(packed, 1)
            v.memset(one[:, :], 1.0)
            v.memset(shut[:, 0:1], 0.0)
            v.memset(shut[:, CL:CL + 1], 0.0)
            v.memset(lr[:, 0:1], 0.0)
            v.memset(lr[:, 2 * P:2 * P + 1], 0.0)
            v.wait_ge(out, 2 * n4)
            v.tensor_tensor(rf[:, 1:CL], df[:, 1:CL], df[:, 0:CL - 1], ALU.not_equal).then_inc(step, 1)
            v.wait_ge(step, 1)
            v.tensor_scalar(shut[:, 1:CL], rf[:, 1:CL], -FAR, None, ALU.mult).then_inc(step, 1)
            v.wait_ge(step, 2)
            v.tensor_tensor_scan(rf[:, :], shut[:, 0:CL], vf[:, :], -FAR, ALU.add, ALU.max).then_inc(step, 1)
            v.wait_ge(step, 3)
            v.tensor_tensor_scan(bf[:, ::-1], shut[:, 1:CL + 1][:, ::-1], rf[:, ::-1], -FAR, ALU.add, ALU.max).then_inc(step, 1)
            v.wait_ge(step, 4)
            for c, x in enumerate((bf[:, 0:1], bf[:, CL - 1:CL], df[:, 0:1], df[:, CL - 1:CL])):
                w = v.tensor_copy(edge[:, c:c + 1], x)
            w.then_inc(step, 1)
            v.wait_ge(lined, 1)
            for to, c in ((lv, 0), (lk, 2)):
                for e in range(2):
                    w = v.tensor_copy(to[:, e:2 * P:2].rearrange("o (h c) -> o h c", h=H),
                                      line[:, c + e, :].rearrange("o (c h) -> o h c", h=H))
            w.then_inc(step, 1)
            v.wait_ge(step, 6)
            v.tensor_tensor(lf[:, 1:2 * P], lk[:, 1:2 * P], lk[:, 0:2 * P - 1], ALU.not_equal).then_inc(step, 1)
            v.wait_ge(step, 7)
            v.tensor_scalar(lr[:, 1:2 * P], lf[:, 1:2 * P], -FAR, None, ALU.mult).then_inc(step, 1)
            v.wait_ge(step, 8)
            v.tensor_tensor_scan(lf[:, 0:2 * P], lr[:, 0:2 * P], lv[:, 0:2 * P], -FAR, ALU.add, ALU.max).then_inc(step, 1)
            v.wait_ge(step, 9)
            v.tensor_tensor_scan(lb[:, 0:2 * P][:, ::-1], lr[:, 1:2 * P + 1][:, ::-1], lf[:, 0:2 * P][:, ::-1], -FAR,
                                 ALU.add, ALU.max).then_inc(step, 1)
            v.wait_ge(step, 10)
            for e in range(2):
                w = v.tensor_copy(lf[:, e * P:(e + 1) * P].rearrange("o (c h) -> o h c", h=H),
                                  lb[:, e:2 * P:2].rearrange("o (h c) -> o h c", h=H))
            w.then_inc(step, 1)
            v.wait_ge(fulled, 1)
            v.tensor_copy(full[:, :], fullp[:, 0:2]).then_inc(step, 1)
            for e in range(2):
                v.wait_ge(step, 12 + 2 * e)
                v.tensor_scalar(rf[:, :], df[:, :], edge[:, 2 + e:3 + e], -FAR, ALU.not_equal, ALU.mult).then_inc(step, 1)
                v.wait_ge(step, 13 + 2 * e)
                v.scalar_tensor_tensor(bf[:, :], rf[:, :], full[:, e:e + 1], bf[:, :], ALU.add, ALU.max).then_inc(step, 1)
            v.wait_ge(step, 16)
            v.tensor_tensor(vf[:, :], vf[:, :], bf[:, :], ALU.subtract).then_inc(step, 1)
            for q in range(n4):
                v.wait_ge(turned2, q + 1)
                for j in range(4 * q, min(CT, 4 * q + 4)):
                    w = v.tensor_copy(k["alpha"][:, j::CT, :], tp[q % 4][:, j % 4, :].rearrange("p (c h) -> p c h", h=H))
                w.then_inc(out2, 1)


def run_sum_phase(nc, d, k, name, table, index=None, places=False):
    gat, mean = table == "leftsrc", table == "messages"
    linear = gat or mean
    SETS = 2 if linear or places else 1
    LEAD = 2 if linear else SLOTS - 1
    with Space(nc, name) as s:
        idx = s.sb("idx", [P, SLOTS, U], I32)
        rows = s.sb("rows", [P, SLOTS, U, MW if mean else D])
        first, one = s.sb("first", [1, T, 2]), s.sb("one", [1, P])
        start_i = s.sb("start_i", [1, T], I32) if mean else k["start_i"]
        start, fb = (s.sb("start", [P, T]), s.ps("fb", [P, 512])) if mean else (None, None)
        firsts, oned, broadcast, started = (s.sem(x) for x in ("firsts", "oned", "broadcast", "started"))
        away = s.sb("away", [P, SLOTS, U])
        far = s.sb("far", [P, 2, G, P])
        msg, ex = (s.sb("msg", [P, 2, G, D]), s.sb("ex", [P, 2, G, H])) if gat else (None, None)
        hot = s.sb("hot", [P, 2, G, P])
        acc = [s.ps(f"acc{b}", [P, G, P]) for b in range(2)]
        accd = [s.ps(f"accd{b}", [H, G, P]) for b in range(2)] if gat else None
        den_sb = s.sb("den_sb", [H, 2, G, P]) if gat else None
        agg = [k["agg"], s.sb("agg2", [P, NP + P])] if SETS == 2 else [k["agg"]]
        den = [k["den"], s.sb("den2", [H, NP + P])] if gat else []
        slots = lambda name: [s.sem(f"{name}{h}") for h in range(SLOTS)]
        cols = slots("cols")
        gathered = slots("gathered") if linear else [[s.sem(f"gathered{h}{b}") for b in range(2)] for h in range(SLOTS)]
        den_out, den_added = s.sem("den_out"), s.sem("den_added")
        fars, masks, scaled, summed, added = (s.sem(x) for x in ("fars", "masks", "scaled", "summed", "added"))
        cleared, tables = s.sem("cleared"), s.sem("tables")
        order = None
        if places:
            lohi_i, nodes_f = s.sb("lohi_i", [P, 2, T], I32), s.sb("nodes_f", [P, T])
            cut = {x: s.sb(f"all_{x}", [P, T], F16 if x == "midh" else F32) for x in ("lo", "hi", "mid", "midh")}
            order = Order(s, k, cut, k["base"][:, 1, :])
        block = s.block()
        n = T // (SLOTS * U)

        def nodes_of(engine, i, h, b):
            return node_registers(nc, engine, start_i[0:1, bass.ds(number(i, h, b) * G, G)])

        @block.vector
        def _(v):
            def columns(i, h):
                at = bass.ds((i * SLOTS + h) * U, U)
                if not linear:
                    v.tensor_copy(idx[:, h, :], k[index][:, at])
                    v.tensor_copy(away[:, h, :], k["away"][:, at]).then_inc(cols[h], 1)
                elif mean:
                    v.wait_ge(gathered[h], (i + 1) * 16)
                    v.tensor_tensor(away[:, h, :], start[:, at], rows[:, h, :, D], ALU.subtract).then_inc(cols[h], 1)
                else:
                    v.tensor_scalar(away[:, h, :], k["loc"][:, at], -1.0, None, ALU.mult).then_inc(cols[h], 1)

            def scale(i, h, b):
                g = number(i, h, b)
                v.wait_ge(gathered[h], (i + 1) * 16)
                past(v, summed, g - 1)
                at = bass.ds(g * G, G)
                v.tensor_copy(ex[:, b], k["alpha"][:, at, :])
                v.tensor_tensor(msg[:, b].rearrange("p g (h c) -> p g h c", h=H),
                                rows[:, h, b * G:b * G + G, :].rearrange("p g (h c) -> p g h c", h=H),
                                k["alpha"][:, at, :].unsqueeze(3).to_broadcast([P, G, H, C]), ALU.mult
                                ).then_inc(scaled, 1)

            def add(u, node, i, h, b):
                g = number(i, h, b)
                past(v, added, g * G + u + 1 - SETS)
                to = agg[u % SETS][:, bass.ds(node, P)]
                v.tensor_tensor(to, to, acc[b][:, u, :], ALU.add).then_inc(added, 1)

            def body(i, last):
                for group, nxt, later in ring(i, last, LEAD):
                    g, p = number(*group), group[2]
                    if places:
                        if nxt:
                            order.onehot(v, number(*nxt), nxt[2])
                        order.add_bases(v, g, p)
                        order.count(v, g, p, range(2))
                        order.rest(v, g, p)
                        order.count(v, g, p, range(2, G))
                    nodes = nodes_of(mybir.EngineType.DVE, *group)
                    if gat and nxt:
                        scale(*nxt)
                    v.wait_ge(summed, g + 1)
                    for u in range(G):
                        add(u, nodes[u], *group)
                    if places:
                        order.choose(v, g, p, k["place2"][:, bass.ds(g * G, G)])
                    if later:
                        columns(*later)

            if mean:
                v.memset(one[:, :], 1.0).then_inc(oned, 1)
                v.wait_ge(firsts, 16)
                v.tensor_copy(start_i[:, :], first[:, :, 1]).then_inc(started, 1)
                v.wait_ge(broadcast, 1)
                v.tensor_copy(start[:, :], fb[:, 0:T]).then_inc(started, 1)
                v.wait_ge(started, 2)
            for h in range(LEAD):
                columns(0, h)
            for x in den + agg:
                v.memset(x[:, :], 0.0).then_inc(cleared, 1)
            if places:
                v.tensor_scalar(lohi_i[:, 0, :], k["src"][:, :], P - 1, None, ALU.bitwise_and)
                v.tensor_scalar(lohi_i[:, 1, :], k["src"][:, :], 7, None, ALU.arith_shift_right)
                v.tensor_copy(nodes_f[:, :], k["src"][:, :]).then_inc(tables, 1)
                v.wait_ge(tables, 1)
                v.tensor_copy(cut["lo"][:, :], lohi_i[:, 0, :])
                v.tensor_copy(cut["hi"][:, :], lohi_i[:, 1, :])
                for x in ("mid", "midh"):
                    w = v.tensor_scalar(cut[x][:, :], nodes_f[:, :], -MIDDLE, None, ALU.add)
                w.then_inc(tables, 1)
                v.wait_ge(tables, 2)
                order.begin(v)
                order.onehot(v, 0, 0)
            if gat:
                scale(0, 0, 0)
            v.wait_ge(cleared, len(den + agg))
            each_ahead(v, n, body)
            if SETS == 2:
                v.wait_ge(added, T)
                v.tensor_tensor(agg[0][:, :], agg[0][:, :], agg[1][:, :], ALU.add)
            if gat:
                v.wait_ge(den_added, T)
                v.tensor_tensor(den[0][:, :], den[0][:, :], den[1][:, :], ALU.add)

        @block.scalar
        def _(act):
            def mask(i, h, b):
                g = number(i, h, b)
                act.wait_ge(cols[h], i + 1)
                past(act, masks, g - 1)
                for u in range(G):
                    m = act.activation(far[:, b, u, :], k["iota"][:, :], ACT.Abs, bias=away[:, h, b * G + u:b * G + u + 1])
                m.then_inc(fars, 1)
                act.wait_ge(fars, g + 1)
                past(act, summed, g - 1)
                act.activation(hot[:, b], far[:, b], ACT.Relu, scale=-1.0, bias=1.0).then_inc(masks, 1)

            def body(i, last):
                for group, nxt, later in ring(i, last):
                    g, p = number(*group), group[2]
                    if places:
                        order.turn(act, g, p)
                        if not (last and group[1:] >= (SLOTS - 1, 0)):
                            order.columns(act, g + 2, p)
                    if nxt:
                        mask(*nxt)
                    if gat:
                        act.wait_ge(summed, g + 1)
                        past(act, den_added, (g - 1) * G)
                        act.copy(den_sb[:, p], accd[p][:, :, :]).then_inc(den_out, 1)

            if places:
                act.wait_ge(tables, 2)
                order.columns(act, 0, 0)
                order.columns(act, 1, 1)
                order.round_first(act)
            mask(0, 0, 0)
            each_ahead(act, n, body)

        if not mean:
            @block.gpsimd
            def _(pool):
                def gather(i):
                    for h in range(SLOTS):
                        pool.wait_ge(cols[h], i + 1)
                        past(pool, summed, reused(i, h))
                        hold(pool)
                        for u in range(U):
                            pool.indirect_dma_start(
                                out=rows[:, h, u, :], out_offset=None, in_=d[table][:, :],
                                in_offset=bass.IndirectOffsetOnAxis(ap=idx[:, h, u:u + 1], axis=0)
                            ).then_inc(gathered[h][u // G], 16)

                def add_exps(i):
                    for h in range(SLOTS):
                        for b in range(2):
                            g = number(i, h, b)
                            nodes = nodes_of(mybir.EngineType.Pool, i, h, b)
                            pool.wait_ge(den_out, g + 1)
                            for u in range(G):
                                past(pool, den_added, g * G + u - 1)
                                to = den[u % 2][:, bass.ds(nodes[u], P)]
                                pool.tensor_tensor(to, to, den_sb[:, b, u, :], ALU.add).then_inc(den_added, 1)

                if gat:
                    pool.wait_ge(cleared, 2)
                each(pool, n, add_exps if gat else gather)

        @block.tensor
        def _(pe):
            def body(i, last):
                for group, nxt, later in ring(i, last):
                    i, h, b = group
                    g = number(*group)
                    pe.wait_ge(masks, g + 1)
                    if gat:
                        pe.wait_ge(scaled, g + 1)
                        past(pe, den_out, g - 1)
                    elif mean:
                        pe.wait_ge(gathered[h], (i + 1) * 16)
                    else:
                        pe.wait_ge(gathered[h][b], (i + 1) * (16 * G))
                    past(pe, added, (g - 1) * G)
                    for u in range(G):
                        if gat:
                            pe.matmul(accd[b][:, u, :], ex[:, b, u, :], hot[:, b, u, :], start=True, stop=True)
                        m = pe.matmul(acc[b][:, u, :], msg[:, b, u, :] if gat else rows[:, h, b * G + u, 0:D],
                                      hot[:, b, u, :], start=True, stop=True)
                    m.then_inc(summed, 1)
                    if places:
                        order.look(pe, g, b)
                        if nxt:
                            order.prepare(pe, number(*nxt), nxt[2])

            if mean:
                pe.wait_ge(oned, 1)
                pe.wait_ge(firsts, 16)
                pe.matmul(fb[:, 0:T], one[:, :], first[:, :, 1], start=True, stop=True).then_inc(broadcast, 1)
            if places:
                order.prepare(pe, 0, 0)
            each_ahead(pe, n, body)

        if linear:
            @block.sync
            def _(sp):
                if mean:
                    sp.dma_start(first[:, :, :], d[table].rearrange("(t p) w -> p t w", p=P)[0:1, :, D - 1:D + 1]
                                 ).then_inc(firsts, 16)

                def slots_of(i):
                    for h in range(SLOTS):
                        past(sp, scaled if gat else summed, reused(i, h))
                        sp.dma_start(rows[:, h], d[table].rearrange("(t p) w -> p t w", p=P)[:, bass.ds((i * SLOTS + h) * U, U), :]
                                     ).then_inc(gathered[h], 16)

                each(sp, n, slots_of)


def node_phase(nc, d, k, layer, table=None):
    with Space(nc, f"nodes{layer}") as s:
        NN = NT // NB
        raw = s.sb("raw", [P, NB, P])
        rawd = s.sb("rawd", [H, NB, P])
        a, at, y, xs = (s.sb(x, [P, NB, D]) for x in ("a", "at", "y", "xs"))
        hs, tab = (s.sb(x, [P, NB, D]) for x in ("hs", "tab"))
        nrm = s.sb("nrm", [P, NB, H])
        tp = s.ps("tp", [P, 8, D])
        mm = s.ps("mm", [P, 8, D])
        mm2 = s.ps("mm2", [P, 8, D]) if layer == 2 else None
        dp = s.ps("dp", [P, 64, H]) if layer == 0 else None
        cols = s.sb("cols", [P, 4, NT])
        inv = s.sb("inv", [P, NT])
        w = k["square"][:, SQUARE[layer], :] if layer else None
        ff = s.sb("ff", [P, 2, NB, D])
        fp = s.ps("fp", [P, 12, D]) if layer == 0 else None
        q1, q2 = norm_tensors(s, "n1"), norm_tensors(s, "n2")
        names = ("rooted", "degree", "taken", "sliced", "den", "inv", "divided", "ready", "turned", "turned_out",
                 "back", "product", "y1", "y2", "y3", "got_x", "scaled", "ff1", "gelu", "kept",
                 "relued", "tabled", "fresh")
        e = {x: s.sem(x) for x in names}
        stored = s.sem("stored")
        block = s.block()
        par = k["par"]
        normed_next = layer in (0, 1, 2)
        turns = layer in (0, 2)

        def row(j):
            return bc(par[:, j, :], [P, NB, D], 1)

        def col(c, i):
            return cols[:, c, bass.ds(i * NB, NB)].unsqueeze(2).to_broadcast([P, NB, D])

        DST_ROOT, SRC_ROOT = 0, 1

        @block.sync
        def _(sp):
            if table or layer == 4:
                def step(i):
                    sp.wait_ge(e["tabled"], i + 1)
                    sp.dma_start(rows_of(d[table][0:NP] if table else d["out"], i), tab[:, :, :]).then_inc(stored, 16)

                each(sp, NN, step)
                sp.wait_ge(stored, 16 * NN)

        @block.vector
        def _(v):
            for c, deg in enumerate(("deg_dst", "deg_src")):
                m = v.tensor_scalar(cols[:, 2 + c, :], k[deg][:, :], 1.0, None, ALU.max)
            m.then_inc(e["degree"], 1)
            v.reciprocal(inv[:, :], k["weight_src"][:, :])
            v.wait_ge(e["rooted"], 1)
            v.reciprocal(cols[:, 0:2, :], cols[:, 2:4, :]).then_inc(e["degree"], 1)
            v.wait_ge(e["degree"], 2)

            def step(i):
                at_i = bass.ds(i * NB, NB)
                x_i, h_i = k["x"][:, at_i, :], k["h"][:, at_i, :]
                if layer == 4:
                    past(v, e["tabled"], i)
                if layer == 0:
                    v.tensor_tensor(xs[:, :, :], x_i, row(L0_B2), ALU.add)
                    v.tensor_tensor(hs[:, :, :], h_i, row(BIAS), ALU.add).then_inc(e["taken"], 1)
                elif layer == 2:
                    v.tensor_copy(hs[:, :, :], h_i).then_inc(e["taken"], 1)
                    v.tensor_tensor(xs[:, :, :], x_i, row(L2_B1), ALU.add).then_inc(e["y1"], 1)
                    v.tensor_tensor(a[:, :, :], row(L2_B2), inv[:, at_i].unsqueeze(2).to_broadcast([P, NB, D]), ALU.mult
                                    ).then_inc(e["y1"], 1)
                    v.wait_ge(e["y1"], 2 * i + 2)
                    v.tensor_tensor(xs[:, :, :], xs[:, :, :], a[:, :, :], ALU.add).then_inc(e["y2"], 1)
                elif layer in (1, 4):
                    v.tensor_copy(xs[:, :, :], x_i).then_inc(e["taken"], 1)
                if layer == 0:
                    v.wait_ge(e["back"], i + 1)
                    v.tensor_scalar(nrm[:, :, :], dp[:, 0:NB, :], 1e-16, None, ALU.add).then_inc(e["den"], 1)
                    v.wait_ge(e["den"], i + 1)
                    v.reciprocal(nrm[:, :, :], nrm[:, :, :]).then_inc(e["inv"], 1)
                    v.wait_ge(e["inv"], i + 1)
                    v.tensor_tensor(a[:, :, :].rearrange("p a (h c) -> p a h c", h=H),
                                    tp[:, 0:NB, :].rearrange("p a (h c) -> p a h c", h=H),
                                    nrm[:, :, :].unsqueeze(3).to_broadcast([P, NB, H, C]), ALU.mult).then_inc(e["divided"], 1)
                    v.wait_ge(e["divided"], i + 1)
                    v.wait_ge(e["taken"], i + 1)
                    v.tensor_tensor(hs[:, :, :], hs[:, :, :], a[:, :, :], ALU.add).then_inc(e["fresh"], 1)
                    v.wait_ge(e["fresh"], i + 1)
                    norm_vector(v, q1, i, hs, a)
                    v.wait_ge(q1["normed"], i + 1)
                    v.tensor_tensor(a[:, :, :], a[:, :, :], row(LN2_G), ALU.mult).then_inc(e["scaled"], 1)
                    v.wait_ge(e["scaled"], i + 1)
                    v.tensor_tensor(a[:, :, :], a[:, :, :], row(LN2_B), ALU.add).then_inc(e["ready"], 1)
                    v.tensor_tensor(xs[:, :, :], xs[:, :, :], hs[:, :, :], ALU.add).then_inc(e["y2"], 1)
                if normed_next:
                    past(v, e["relued"], i)
                if table:
                    past(v, e["tabled"], i)
                v.wait_ge(e["product"], i + 1)
                if layer == 0:
                    v.wait_ge(e["y2"], i + 1)
                    v.tensor_tensor(xs[:, :, :], mm[:, 0:NB, :], xs[:, :, :], ALU.add).then_inc(e["got_x"], 1)
                elif layer == 1:
                    v.tensor_tensor(y[:, :, :], mm[:, 0:NB, :], col(DST_ROOT, i), ALU.mult).then_inc(e["y1"], 1)
                    v.wait_ge(e["y1"], i + 1)
                    v.wait_ge(e["taken"], i + 1)
                    v.scalar_tensor_tensor(xs[:, :, :], y[:, :, :], 0.0, xs[:, :, :], ALU.max, ALU.add).then_inc(e["got_x"], 1)
                elif layer == 2:
                    v.tensor_tensor(y[:, :, :], mm[:, 0:NB, :], inv[:, at_i].unsqueeze(2).to_broadcast([P, NB, D]), ALU.mult
                                    ).then_inc(e["scaled"], 1)
                    v.wait_ge(e["y2"], i + 1)
                    v.tensor_tensor(xs[:, :, :], mm2[:, 0:NB, :], xs[:, :, :], ALU.add).then_inc(e["y3"], 1)
                    v.wait_ge(e["scaled"], i + 1)
                    v.wait_ge(e["y3"], i + 1)
                    v.tensor_tensor(xs[:, :, :], xs[:, :, :], y[:, :, :], ALU.add).then_inc(e["got_x"], 1)
                else:
                    v.tensor_tensor(y[:, :, :], mm[:, 0:NB, :], col(DST_ROOT, i), ALU.mult).then_inc(e["y1"], 1)
                    v.wait_ge(e["y1"], i + 1)
                    v.tensor_tensor(y[:, :, :], y[:, :, :], row(L3_B1 if layer == 3 else L3_B2), ALU.add).then_inc(e["y2"], 1)
                    v.wait_ge(e["y2"], i + 1)
                    past(v, stored, i * 16)
                    if layer == 3:
                        v.scalar_tensor_tensor(tab[:, :, :], y[:, :, :], 0.0, col(SRC_ROOT, i), ALU.max, ALU.mult
                                               ).then_inc(e["tabled"], 1)
                    else:
                        v.wait_ge(e["taken"], i + 1)
                        v.scalar_tensor_tensor(tab[:, :, :], y[:, :, :], 0.0, xs[:, :, :], ALU.max, ALU.add
                                               ).then_inc(e["tabled"], 1)
                if normed_next:
                    v.wait_ge(e["got_x"], i + 1)
                    norm_vector(v, q2, i, xs, y)
                    v.wait_ge(q2["normed"], i + 1)
                    if table:
                        past(v, stored, i * 16)
                        if layer == 2:
                            v.scalar_tensor_tensor(tab[:, :, :], y[:, :, :], 0.0, col(SRC_ROOT, i), ALU.max, ALU.mult
                                                   ).then_inc(e["tabled"], 1)
                        else:
                            v.tensor_scalar(tab[:, :, :], y[:, :, :], 0.0, None, ALU.max).then_inc(e["tabled"], 1)
                    v.wait_ge(e["kept"], i + 1)

            each(v, NN, step)

        @block.scalar
        def _(act):
            act.wait_ge(e["degree"], 1)
            act.activation(cols[:, 2:4, :], cols[:, 2:4, :], ACT.Sqrt).then_inc(e["rooted"], 1)

            def step(i):
                at_i = bass.ds(i * NB, NB)
                past(act, e["product"], i)
                if layer == 0:
                    act.copy(rawd[:, :, :], k["den"][:, 0:NP].rearrange("p (t l) -> p t l", l=P)[:, at_i, :])
                act.copy(raw[:, :, :], k["agg"][:, 0:NP].rearrange("p (t l) -> p t l", l=P)[:, at_i, :]
                         ).then_inc(e["sliced"], 1)
                if layer == 0:
                    norm_scalar(act, q1, i, k)
                if turns:
                    act.wait_ge(e["turned"], i + 1)
                    act.copy(at[:, :, :], tp[:, 0:NB, :]).then_inc(e["turned_out"], 1)
                if layer == 0:
                    act.wait_ge(e["ff1"], i + 1)
                    for f in range(2):
                        m = act.activation(ff[:, f, :, :], fp[:, f * 6:f * 6 + NB, :], ACT.Gelu, bias=k["b1"][:, f:f + 1])
                    m.then_inc(e["gelu"], 1)
                if normed_next:
                    act.wait_ge(e["got_x"], i + 1)
                    act.copy(k["x"][:, at_i, :], xs[:, :, :]).then_inc(e["kept"], 1)
                    norm_scalar(act, q2, i, k)
                    act.wait_ge(q2["normed"], i + 1)
                    act.activation(k["h"][:, at_i, :], y[:, :, :], ACT.Relu).then_inc(e["relued"], 1)

            each(act, NN, step)

        @block.tensor
        def _(pe):
            def step(i):
                pe.wait_ge(e["sliced"], i + 1)
                past(pe, e["got_x"] if normed_next else e["y1"], i)
                if layer == 0:
                    hold(pe)
                    for u in range(NB):
                        pe.transpose(dp[:, u, :], rawd[:, u, :], k["ident"][0:H, 0:H])
                    for u in range(NB):
                        m = pe.transpose(tp[:, u, :], raw[:, u, :], k["ident"][:, :])
                    m.then_inc(e["back"], 1)
                    pe.wait_ge(e["ready"], i + 1)
                if layer == 2:
                    pe.wait_ge(e["taken"], i + 1)
                if turns:
                    for u in range(NB):
                        m = pe.transpose(tp[:, u, :], (a if layer == 0 else hs)[:, u, :], k["ident"][:, :])
                    m.then_inc(e["turned"], 1)
                    pe.wait_ge(e["turned_out"], i + 1)
                if layer == 0:
                    for f in range(2):
                        for u in range(NB):
                            m = pe.matmul(fp[:, f * 6 + u, :], k["w1"][:, f * D:(f + 1) * D], at[:, u, :], start=True, stop=True)
                    m.then_inc(e["ff1"], 1)
                    pe.wait_ge(e["gelu"], i + 1)
                    for u in range(NB):
                        for f in range(2):
                            m = pe.matmul(mm[:, u, :], ff[:, f, u, :], k["w2"][:, f, :],
                                          start=(f == 0), stop=(f == 1))
                else:
                    if layer == 2:
                        for u in range(NB):
                            pe.matmul(mm2[:, u, :], at[:, u, :], k["square"][:, SQUARE[2] + 1, :], start=True, stop=True)
                    for u in range(NB):
                        m = pe.matmul(mm[:, u, :], raw[:, u, :], w, start=True, stop=layer != 1)
                        if layer == 1:
                            m = pe.matmul(mm[:, u, :], raw[:, u, :], k["ident"][:, :], start=False, stop=True)
                m.then_inc(e["product"], 1)

            each(pe, NN, step)


def spread_phase(nc, d, k):
    with Space(nc, "spread") as s:
        win = s.sb("win", [P, SLOTS, U, D])
        loc = s.sb("loc", [P, SLOTS, U], BF16)
        wcol, to = s.sb("wcol", [P, SLOTS, U]), s.sb("to", [P, SLOTS, U], I32)
        hot = s.sb("hot", [P, 2, G, P])
        msg = s.sb("msg", [P, SLOTS, U, MW])
        rowb = [s.ps(f"rowb{b}", [P, G, P]) for b in range(2)]
        z = [s.ps(f"z{b}", [P, G, D]) for b in range(2)]
        slots = lambda name: [s.sem(f"{name}{h}") for h in range(SLOTS)]
        windows, cols, sent = slots("windows"), slots("cols"), slots("sent")
        spread, hots, summed, weighed = (s.sem(x) for x in ("spread", "hots", "summed", "weighed"))
        block = s.block()
        n = T // (SLOTS * U)

        @block.sync
        def _(sp):
            def slots_of(i):
                for h in range(SLOTS):
                    past(sp, summed, reused(i, h))
                    nodes = node_registers(nc, mybir.EngineType.SP, k["start_i"][0:1, bass.ds((i * SLOTS + h) * U, U)])
                    for u in range(U):
                        sp.dma_start(win[:, h, u, :], d["table"][bass.ds(nodes[u], P), :]).then_inc(windows[h], 16)

            each(sp, n, slots_of)

        @block.vector
        def _(v):
            def columns(i, h):
                at = bass.ds((i * SLOTS + h) * U, U)
                past(v, sent[h], i * (16 * U))
                v.tensor_copy(loc[:, h, :], k["loc"][:, at])
                v.tensor_copy(wcol[:, h, :], k["w"][:, at])
                v.tensor_copy(to[:, h, :], k["place2"][:, at])
                v.tensor_copy(msg[:, h, :, D], k["src"][:, at]).then_inc(cols[h], 1)

            def onehot(i, h, b):
                g = number(i, h, b)
                v.wait_ge(spread, g + 1)
                past(v, summed, g - 1)
                v.tensor_scalar(hot[:, b], rowb[b][:, :, :], k["part"][:, 0:1], None, ALU.is_equal).then_inc(hots, 1)

            def weigh(i, h, b):
                v.wait_ge(cols[h], i + 1)
                v.wait_ge(summed, number(i, h, b) + 1)
                v.tensor_tensor(msg[:, h, b * G:(b + 1) * G, 0:D], z[b][:, :, :],
                                wcol[:, h, b * G:(b + 1) * G].unsqueeze(2).to_broadcast([P, G, D]), ALU.mult
                                ).then_inc(weighed, 1)

            def body(i, last):
                for group, nxt, later in ring(i, last):
                    if nxt:
                        onehot(*nxt)
                    weigh(*group)
                    if later:
                        columns(*later)

            columns(0, 0)
            columns(0, 1)
            onehot(0, 0, 0)
            each_ahead(v, n, body)

        @block.tensor
        def _(pe):
            def prepare(i, h, b):
                g = number(i, h, b)
                pe.wait_ge(cols[h], i + 1)
                past(pe, hots, g - 1)
                for u in range(G):
                    m = pe.matmul(rowb[b][:, u, :], loc[:, h, b * G + u:b * G + u + 1].to_broadcast([P, P]),
                                  k["identb"][:, :], start=True, stop=True)
                m.then_inc(spread, 1)

            def expand(i, h, b):
                g = number(i, h, b)
                pe.wait_ge(hots, g + 1)
                past(pe, weighed, g - 1)
                if b == 0:
                    pe.wait_ge(windows[h], (i + 1) * (16 * U))
                for u in range(G):
                    m = pe.matmul(z[b][:, u, :], hot[:, b, u, :], win[:, h, b * G + u, :], start=True, stop=True)
                m.then_inc(summed, 1)

            def body(i, last):
                for group, nxt, later in ring(i, last):
                    if nxt:
                        prepare(*nxt)
                    expand(*group)

            prepare(0, 0, 0)
            each_ahead(pe, n, body)

        @block.gpsimd
        def _(pool):
            def slots_of(i):
                for h in range(SLOTS):
                    for b in range(2):
                        pool.wait_ge(weighed, number(i, h, b) + 1)
                        hold(pool)
                        for u in range(b * G, (b + 1) * G):
                            pool.indirect_dma_start(
                                out=d["messages"][:, :], out_offset=bass.IndirectOffsetOnAxis(ap=to[:, h, u:u + 1], axis=0),
                                in_=msg[:, h, u, :], in_offset=None).then_inc(sent[h], 16)

            each(pool, n, slots_of)
            for h in range(SLOTS):
                pool.wait_ge(sent[h], n * 16 * U)


def relation_phase(nc, d, k):
    GR = 4
    HR = R // 2
    with Space(nc, "relation") as s:
        wr = s.sb("wr", [P, R, D])
        feat = s.sb("feat", [P, R, D])
        hs, ht = s.sb("hs", [P, 2, D]), s.sb("ht", [P, 2, D])
        out = s.sb("out", [P, 2, HR, D])
        tp = [s.ps(f"tp{q}", [P, 512]) for q in range(2)]
        mm = [s.ps(f"mm{b}", [P, GR, D]) for b in range(HR // GR)]
        loaded = s.sem("loaded")
        taken, turned, turned_out = s.sem("taken"), s.sem("turned"), s.sem("turned_out")
        product = s.sem("product")
        made = [s.sem(f"made{b}") for b in range(HR // GR)]
        stored = [s.sem(f"stored{h}") for h in range(2)]
        block = s.block()
        K = R // GR
        HK = K // 2

        @block.sync
        def _(sp):
            sp.dma_start(wr[:, :, :], d["wr"].rearrange("r p w -> p r w")).then_inc(loaded, 16)
            sp.dma_start(feat[:, :, :], d["feat"].rearrange("(o a) w -> o a w", o=1).to_broadcast([P, R, D])
                         ).then_inc(loaded, 16)
            table = d["relation"].rearrange("(t l r) w -> l t (r w)", l=P, r=R)

            def step(i):
                for h in range(2):
                    for b in range(HK):
                        sp.wait_ge(made[b], i * 2 + h + 1)
                    sp.dma_start(table[:, bass.ds(i, 1), h * HR * D:(h + 1) * HR * D],
                                 out[:, h:h + 1].rearrange("p o r w -> p o (r w)")).then_inc(stored[h], 16)

            each(sp, NT, step)
            for h in range(2):
                sp.wait_ge(stored[h], NT * 16)

        @block.scalar
        def _(act):
            def turn(t, q):
                act.copy(hs[:, q:q + 1, :], k["h"][:, bass.ds(t, 1), :]).then_inc(taken, 1)
                act.wait_ge(turned, t + 1)
                past(act, product, (t - 1) * K)
                act.copy(ht[:, q, :], tp[q][:, 0:D]).then_inc(turned_out, 1)

            def pair(i):
                for q in range(2):
                    turn(2 * i + q, q)

            each(act, NT // 2, pair)
            turn(NT - 1, 0)

        @block.tensor
        def _(pe):
            def turn(t, q):
                pe.wait_ge(taken, t + 1)
                pe.transpose(tp[q][:, 0:D], hs[:, q, :], k["ident"][:, :]).then_inc(turned, 1)

            def multiply(t, q):
                pe.wait_ge(turned_out, t + 1)
                for g in range(K):
                    past(pe, made[g % HK], t * 2 + g // HK)
                    pe.matmul(mm[g % HK][:, :, :], ht[:, q, :], wr[:, g * GR:(g + 1) * GR, :], start=True, stop=True
                              ).then_inc(product, 1)

            def pair(i):
                for q in range(2):
                    turn(2 * i + q + 1, 1 - q)
                    multiply(2 * i + q, q)

            pe.wait_ge(loaded, 32)
            turn(0, 0)
            each(pe, NT // 2, pair)
            multiply(NT - 1, 0)

        @block.vector
        def _(v):
            v.wait_ge(loaded, 32)

            def step(i):
                for g in range(K):
                    h = g // HK
                    if g % HK == 0:
                        past(v, stored[h], i * 16)
                    v.wait_ge(product, i * K + g + 1)
                    v.tensor_tensor(out[:, h, (g % HK) * GR:(g % HK + 1) * GR, :], mm[g % HK][:, :, :],
                                    feat[:, g * GR:(g + 1) * GR, :], ALU.add).then_inc(made[g % HK], 1)

            each(v, NT, step)


SQUARE = {1: 0, 2: 1, 3: 3, 4: 4}


def gnn_kernel(nc, d):
    with Space(nc, "kept") as s:
        k = {}
        k["meta"] = s.sb("meta", [P, 5, T])
        for name in ("ident", "before", "iota", "upper", "ones"):
            k[name] = s.sb(name, [P, P])
        for name in ("identb", "iotab"):
            k[name] = s.sb(name, [P, P], BF16)
        k["lo"], k["hi"] = s.sb("lo", [P, 2, T]), s.sb("hi", [P, 2, T])
        k["mid"], k["midh"] = s.sb("mid", [P, T]), s.sb("midh", [P, T], F16)
        k["wpart"], k["wrest"] = s.sb("wpart", [P, T, 3], BF16), s.sb("wrest", [P, T, 2])
        k["zerob"] = s.sb("zerob", [P, P], BF16)
        k["w1"], k["w2"], k["b1"] = s.sb("w1", [P, 2 * D]), s.sb("w2", [P, 2, D]), s.sb("b1", [P, 2])
        k["wlr"], k["we"] = s.sb("wlr", [P, 2 * D]), s.sb("we", [DE, D])
        k["square"] = s.sb("square", [P, 5, D])
        k["identh"] = s.sb("identh", [P, P], F16)
        for name in ("dst", "loc", "start", "w", "away"):
            k[name] = s.sb(name, [P, T])
        for name in ("src", "relsrc", "place2"):
            k[name] = s.sb(name, [P, T], I32)
        k["start_i"] = s.sb("start_i", [1, T], I32)
        for name in ("deg_dst", "deg_src", "weight_src"):
            k[name] = s.sb(name, [P, NT])
        k["base"], k["part"], k["eps"] = s.sb("base", [P, 2, NT]), s.sb("part", [P, 1]), s.sb("eps", [P, 1])
        k["mean"] = s.sb("mean", [DE, 1])
        k["wedge"] = s.sb("wedge", [DE + 1, D])
        k["par"] = s.sb("par", [P, PARS, D])
        k["x"], k["h"] = s.sb("x", [P, NT, D]), s.sb("h", [P, NT, D])
        k["alpha"] = s.sb("alpha", [P, T, H])
        count_phase(nc, d, k)
        sort_phase(nc, d, k)
        enter_phase(nc, d, k)
        score_phase(nc, d, k)
        softmax_phase(nc, d, k)
        k["agg"], k["den"] = s.sb("agg", [P, NP + P]), s.sb("den", [H, NP + P])
        run_sum_phase(nc, d, k, "gat", "leftsrc")
        node_phase(nc, d, k, 0)
        relation_phase(nc, d, k)
        run_sum_phase(nc, d, k, "rel", "relation", "relsrc", places=True)
        node_phase(nc, d, k, 1, table="table")
        spread_phase(nc, d, k)
        run_sum_phase(nc, d, k, "avg", "messages")
        node_phase(nc, d, k, 2, table="table2")
        run_sum_phase(nc, d, k, "conv1", "table2", "src")
        node_phase(nc, d, k, 3, table="table3")
        run_sum_phase(nc, d, k, "conv2", "table3", "src")
        node_phase(nc, d, k, 4)


def kernel(**inputs):
    import numpy as np
    import concourse.bacc as bacc
    from concourse.bass_utils import run_bass_kernel_spmd

    z = {n: np.asarray(a) for n, a in inputs.items()}
    loops, pad = np.arange(NP, dtype=np.int32), EP - E
    rest = pad + NP
    l0 = lambda n: z["L0_gnn_" + n]
    arrays = {
        "x": np.concatenate([z["x"], np.zeros((NP - N, D), np.float32)]),
        "src": np.concatenate([z["src"], np.full(pad, N, np.int32), loops]),
        "dst": np.concatenate([z["dst"], np.full(pad, N, np.int32), loops]),
        "type": np.concatenate([z["edge_type_40"], np.zeros(rest, np.int32)]),
        "weight": np.concatenate([z["edge_weight"], np.ones(pad, np.float32), np.zeros(N, np.float32),
                                  np.ones(NP - N, np.float32)]),
        "attr": np.concatenate([z["edge_attr_32"], np.zeros((rest, DE), np.float32)]),
        "wlr": np.concatenate([l0("W_l"), l0("W_r")], axis=1),
        "we": l0("W_e"),
        "w1": l0("W1"),
        "w2": l0("W2"),
        "b1": np.ascontiguousarray(l0("b1").reshape(2, D).T),
        "par": np.stack([l0("ln1_g"), l0("ln1_b"), l0("ln2_g"), l0("ln2_b"), l0("att").reshape(D), l0("bias"), l0("b2"),
                         z["L2_gnn_b1"], z["L2_gnn_b2"], z["L3_gnn_b1"], z["L3_gnn_b2"]]),
        "wr": z["L1_gnn_relation_weights"],
        "feat": z["L1_gnn_rFeatures"],
        "square": np.stack([z["L1_gnn_loop_weight"], z["L2_gnn_W2"].T, z["L2_gnn_W1"].T, z["L3_gnn_W1"], z["L3_gnn_W2"]]),
    }
    arrays = {f"in_{n}": np.ascontiguousarray(a) for n, a in arrays.items()}
    nc = bacc.Bacc("TRN2", target_bir_lowering=False, num_devices=1)
    d = {n[3:]: nc.dram_tensor(n, a.shape, mybir.dt.from_np(a.dtype), kind="ExternalInput").ap() for n, a in arrays.items()}
    for name, rows, width in (("records", TE, RW), ("messages", TE, MW), ("left", NP, D), ("right", NP + P, D), ("leftsrc", TE, D), ("relation", NP * R, D),
                              ("table", NP + P, D), ("table2", NP, D), ("table3", NP, D)):
        d[name] = nc.dram_tensor(name, (rows, width), F32, kind="Internal").ap()
    d["out"] = nc.dram_tensor("out_x", (NP, D), F32, kind="ExternalOutput").ap()
    gnn_kernel(nc, d)
    r = run_bass_kernel_spmd(nc, [arrays], core_ids=[0])
    return r.results[0]["out_x"][:N]
```
